# Optimizing a Trainium2 kernel written in Bass

```python
import numpy as np
import jax
import jax.numpy as jnp

def _softmax(x, axis=-1):
    return jax.nn.softmax(x, axis=axis)

def _gelu(x):
    return jax.nn.gelu(x, approximate=True)

def _silu(x):
    return jax.nn.silu(x)

def _sigmoid(x):
    return jax.nn.sigmoid(x)

def _layernorm(x, axis=-1, eps=1e-05):
    m = jnp.mean(x, axis=axis, keepdims=True)
    v = jnp.var(x, axis=axis, keepdims=True)
    return (x - m) / jnp.sqrt(v + eps)

def _scatter_add(tgt, idx, src, axis=0):
    return tgt.at[idx].add(src)

def _segment_sum(src, seg, n):
    return jax.ops.segment_sum(src, seg, n)
kernel_name = 'mk_gnn_preln_d2_gnn_r8_076e07'

def setup_inputs(seed: int=0):
    np.random.seed(seed)
    _w = jnp.asarray

    def _rec_inputs():
        import jax
        import jax.numpy as jnp
        _gk = jax.random.key(seed)
        x = -0.0003713 + 1 * jax.random.normal(jax.random.fold_in(_gk, 1), (6250, 256), jnp.float32)
        src = jax.random.randint(jax.random.fold_in(_gk, 2), (100000,), 0, 6250, jnp.int32)
        dst = jnp.minimum((6250 * jax.random.uniform(jax.random.fold_in(_gk, 3), (100000,)) ** 2.0).astype(jnp.int32), 49999)
        _o = jnp.argsort(dst, stable=True)
        src = src[_o]
        dst = dst[_o]
        edge_type_6 = jax.random.randint(jax.random.fold_in(_gk, 13), (100000,), 0, 6, jnp.int32)
        node_type_3 = jax.random.randint(jax.random.fold_in(_gk, 14), (6250,), 0, 3, jnp.int32)
        return (x, src, dst, edge_type_6, node_type_3)
    x, src, dst, edge_type_6, node_type_3 = _rec_inputs()

    def _L0_gnn_setup():
        import jax, jax.numpy as jnp
        import numpy as np
        N, E, D, T, R, H = (6250, 50000, 256, 3, 6, 4)
        DK = D // H
        OUT = H * DK
        LN_EPS = 1e-05
        key = jax.random.key(seed)
        ks = jax.random.split(key, 16)
        std = 0.02
        f32 = jnp.float32
        inp = {'x': jax.random.normal(ks[0], (N, D), f32), 'Wk': jax.random.normal(ks[1], (T, D, OUT), f32) * std, 'bk': jnp.zeros((T, OUT), f32), 'Wq': jax.random.normal(ks[2], (T, D, OUT), f32) * std, 'bq': jnp.zeros((T, OUT), f32), 'Wv': jax.random.normal(ks[3], (T, D, OUT), f32) * std, 'bv': jnp.zeros((T, OUT), f32), 'Wa': jax.random.normal(ks[4], (T, OUT, OUT), f32) * std, 'ba': jnp.zeros((T, OUT), f32), 'rel_pri': jnp.ones((R, H), f32), 'rel_att': jax.random.normal(ks[5], (R, H, DK, DK), f32) * (1.0 / np.sqrt(DK)), 'rel_msg': jax.random.normal(ks[6], (R, H, DK, DK), f32) * (1.0 / np.sqrt(DK)), 'skip': jnp.ones((T,), f32), 'ln_g': jnp.ones((T, OUT), f32), 'ln_b': jnp.zeros((T, OUT), f32), 'node_type': jax.random.randint(ks[7], (N,), 0, T), 'edge_src': jax.random.randint(ks[8], (E,), 0, N), 'edge_dst': jax.random.randint(ks[9], (E,), 0, N), 'edge_type': jax.random.randint(ks[10], (E,), 0, R), 'n_heads': H}
        return inp
    _L0_gnn_all = _L0_gnn_setup()
    _L0_gnn_in = {k: v for k, v in _L0_gnn_all.items() if k in ('Wk', 'bk', 'Wq', 'bq', 'Wv', 'bv', 'Wa', 'ba', 'rel_pri', 'rel_att', 'rel_msg', 'skip', 'ln_g', 'ln_b')}
    del _L0_gnn_all

    def _L1_gnn_setup():
        import jax, jax.numpy as jnp
        import numpy as np
        N = 6250
        E = 100000
        IN = 256
        H = 4
        C = 64
        NEG_SLOPE = 0.2
        BN_EPS = 1e-05
        key = jax.random.key(seed)
        ks = jax.random.split(key, 6)
        feature = jax.random.normal(ks[0], (N, IN), jnp.float32)
        edge_index = jax.random.randint(ks[1], (2, E), 0, N, dtype=jnp.int64)
        W = jax.random.normal(ks[2], (IN, H * C), jnp.float32) * 0.05
        att_src = jax.random.normal(ks[3], (H, C), jnp.float32) * 0.1
        att_dst = jax.random.normal(ks[4], (H, C), jnp.float32) * 0.1
        bias = jnp.zeros((H * C,), jnp.float32)
        gamma = jnp.ones((H * C,), jnp.float32)
        beta = jnp.zeros((H * C,), jnp.float32)
        return {'feature': feature, 'edge_index': edge_index, 'W': W, 'att_src': att_src, 'att_dst': att_dst, 'bias': bias, 'gamma': gamma, 'beta': beta}
    _L1_gnn_all = _L1_gnn_setup()
    _L1_gnn_in = {k: v for k, v in _L1_gnn_all.items() if k in ('W', 'att_src', 'att_dst', 'bias', 'gamma', 'beta')}
    del _L1_gnn_all
    return {'x': x, 'src': src, 'dst': dst, 'edge_type_6': edge_type_6, 'node_type_3': node_type_3, 'L0_gnn_Wk': _L0_gnn_in['Wk'], 'L0_gnn_bk': _L0_gnn_in['bk'], 'L0_gnn_Wq': _L0_gnn_in['Wq'], 'L0_gnn_bq': _L0_gnn_in['bq'], 'L0_gnn_Wv': _L0_gnn_in['Wv'], 'L0_gnn_bv': _L0_gnn_in['bv'], 'L0_gnn_Wa': _L0_gnn_in['Wa'], 'L0_gnn_ba': _L0_gnn_in['ba'], 'L0_gnn_rel_pri': _L0_gnn_in['rel_pri'], 'L0_gnn_rel_att': _L0_gnn_in['rel_att'], 'L0_gnn_rel_msg': _L0_gnn_in['rel_msg'], 'L0_gnn_skip': _L0_gnn_in['skip'], 'L0_gnn_ln_g': _L0_gnn_in['ln_g'], 'L0_gnn_ln_b': _L0_gnn_in['ln_b'], 'L1_gnn_W': _L1_gnn_in['W'], 'L1_gnn_att_src': _L1_gnn_in['att_src'], 'L1_gnn_att_dst': _L1_gnn_in['att_dst'], 'L1_gnn_bias': _L1_gnn_in['bias'], 'L1_gnn_gamma': _L1_gnn_in['gamma'], 'L1_gnn_beta': _L1_gnn_in['beta']}

def reference(x, src, dst, edge_type_6, node_type_3, L0_gnn_Wk, L0_gnn_bk, L0_gnn_Wq, L0_gnn_bq, L0_gnn_Wv, L0_gnn_bv, L0_gnn_Wa, L0_gnn_ba, L0_gnn_rel_pri, L0_gnn_rel_att, L0_gnn_rel_msg, L0_gnn_skip, L0_gnn_ln_g, L0_gnn_ln_b, L1_gnn_W, L1_gnn_att_src, L1_gnn_att_dst, L1_gnn_bias, L1_gnn_gamma, L1_gnn_beta):
    import jax
    import jax.numpy as jnp

    def _L0_gnn_ref(x, Wk, bk, Wq, bq, Wv, bv, Wa, ba, rel_pri, rel_att, rel_msg, skip, ln_g, ln_b, node_type, edge_src, edge_dst, edge_type, n_heads):
        import jax, jax.numpy as jnp
        import numpy as np
        N, E, D, T, R, H = (6250, 50000, 256, 3, 6, 4)
        DK = D // H
        OUT = H * DK
        LN_EPS = 1e-05
        n, d = x.shape
        r, h = rel_pri.shape
        dk = rel_att.shape[-1]
        out_dim = h * dk
        ar = jnp.arange(n)

        def typed_linear(inp_, W, b):
            y = jnp.einsum('ni,tio->tno', inp_, W) + b[:, None, :]
            return y[node_type, ar]
        k = typed_linear(x, Wk, bk).reshape(n, h, dk)
        q = typed_linear(x, Wq, bq).reshape(n, h, dk)
        v = typed_linear(x, Wv, bv).reshape(n, h, dk)
        k_rel = jnp.einsum('nhd,rhde->rnhe', k, rel_att)
        v_rel = jnp.einsum('nhd,rhde->rnhe', v, rel_msg)
        key_e = k_rel[edge_type, edge_src]
        val_e = v_rel[edge_type, edge_src]
        att = (q[edge_dst] * key_e).sum(-1) * rel_pri[edge_type] / jnp.sqrt(jnp.float32(dk))
        seg = edge_dst * r + edge_type
        S = n * r
        amax = jax.ops.segment_max(att, seg, num_segments=S)
        amax = jax.lax.stop_gradient(jnp.where(jnp.isfinite(amax), amax, 0.0))
        ex = jnp.exp(att - amax[seg])
        denom = jax.ops.segment_sum(ex, seg, num_segments=S)
        w = ex / denom[seg]
        hsum = jax.ops.segment_sum(w[:, :, None] * val_e, seg, num_segments=S)
        cnt = jax.ops.segment_sum(jnp.ones((seg.shape[0],), x.dtype), seg, num_segments=S)
        t_rel = hsum.reshape(n, r, out_dim)
        present = cnt.reshape(n, r) > 0
        nrel = jnp.maximum(present.sum(-1), 1).astype(x.dtype)
        t = (t_rel * present[..., None].astype(x.dtype)).sum(1) / nrel[:, None]
        trans = typed_linear(t, Wa, ba)
        alpha = jax.nn.sigmoid(skip)[node_type][:, None]
        out = trans * alpha + x * (1.0 - alpha)
        mu = out.mean(-1, keepdims=True)
        var = out.var(-1, keepdims=True)
        normed = (out - mu) * jax.lax.rsqrt(var + LN_EPS) * ln_g[node_type] + ln_b[node_type]
        has_msg = present.any(-1)[:, None]
        return jnp.where(has_msg, normed, x)

    def _L1_gnn_ref(feature, edge_index, W, att_src, att_dst, bias, gamma, beta):
        import jax, jax.numpy as jnp
        import numpy as np
        N = 6250
        E = 100000
        IN = 256
        H = 4
        C = 64
        NEG_SLOPE = 0.2
        BN_EPS = 1e-05
        n = feature.shape[0]
        x = (feature @ W).reshape(n, H, C)
        a_src = jnp.einsum('nhc,hc->nh', x, att_src)
        a_dst = jnp.einsum('nhc,hc->nh', x, att_dst)
        loop = jnp.arange(n, dtype=edge_index.dtype)
        src = jnp.concatenate([edge_index[0], loop])
        dst = jnp.concatenate([edge_index[1], loop])
        e = jax.nn.leaky_relu(a_src[src] + a_dst[dst], NEG_SLOPE)
        m = jax.ops.segment_max(e, dst, num_segments=n)
        ex = jnp.exp(e - m[dst])
        denom = jax.ops.segment_sum(ex, dst, num_segments=n)
        alpha = ex / denom[dst]
        msg = x[src] * alpha[:, :, None]
        out = jax.ops.segment_sum(msg, dst, num_segments=n)
        h = out.reshape(n, H * C) + bias
        mu = jnp.mean(h, axis=0)
        var = jnp.var(h, axis=0)
        h = (h - mu) * jax.lax.rsqrt(var + BN_EPS) * gamma + beta
        h = jax.nn.elu(h)
        return feature + h
    edge_index = jnp.stack([src, dst])
    h = jnp.maximum(_layernorm(x, axis=-1), 0.0)
    x = x + _L0_gnn_ref(h, L0_gnn_Wk, L0_gnn_bk, L0_gnn_Wq, L0_gnn_bq, L0_gnn_Wv, L0_gnn_bv, L0_gnn_Wa, L0_gnn_ba, L0_gnn_rel_pri, L0_gnn_rel_att, L0_gnn_rel_msg, L0_gnn_skip, L0_gnn_ln_g, L0_gnn_ln_b, node_type_3, src, dst, edge_type_6, 4)
    h = jnp.maximum(_layernorm(x, axis=-1), 0.0)
    x = x + _L1_gnn_ref(h, edge_index, L1_gnn_W, L1_gnn_att_src, L1_gnn_att_dst, L1_gnn_bias, L1_gnn_gamma, L1_gnn_beta)
    return x

_drawn_inputs = setup_inputs


def setup_inputs(seed=0):
    import zlib

    import numpy as np

    out = dict(_drawn_inputs(seed))
    spreads = {'L0_gnn_bk': (0.0, 0.8),
     'L0_gnn_bq': (0.0, 0.8),
     'L0_gnn_bv': (0.0, 0.295),
     'L0_gnn_ba': (0.0, 0.1),
     'L0_gnn_rel_pri': (1.0, 0.6),
     'L0_gnn_skip': (1.0, 0.2),
     'L0_gnn_ln_g': (1.0, 0.2),
     'L0_gnn_ln_b': (0.0, 0.1),
     'L1_gnn_bias': (0.0, 0.8),
     'L1_gnn_gamma': (1.0, 0.2),
     'L1_gnn_beta': (0.0, 0.1)}
    factors = {'L0_gnn_Wk': 8.0, 'L0_gnn_Wq': 8.0, 'L0_gnn_rel_att': 8.0}
    for name, (base, spread) in spreads.items():
        noise = np.random.default_rng([zlib.crc32(name.encode()), seed]).standard_normal(out[name].shape)
        drawn = base * np.exp(spread * noise) if base else spread * noise
        out[name] = jnp.asarray(drawn.astype(out[name].dtype))
    for name, factor in factors.items():
        out[name] = (out[name] * factor).astype(out[name].dtype)
    return out
```

```python
from contextlib import ExitStack

import concourse.bass as bass
from concourse import mybir
from concourse.alu_op_type import AluOpType as ALU

P = 128
N, D, H, DK, R, T = 6250, 256, 4, 64, 6, 3
E = 100000
NB = -(-N // P)
NP = NB * P
NLAST = N - (NB - 1) * P
SUP = 2 * P
NS = 392
EP = NS * SUP
PADDST = NP - 1
NV = NS + NB - 1
VT = 4
NT = NV // VT
NC = 2 * NV
LV = NV * SUP
GR = P // H
SL = LV // GR
CT = 8
CW = NC // CT
ROW1 = D + H
MSG = D + 2 * H
BIG = 1e30
EPS = 1e-5
SLOPE = 0.2
assert NV % VT == 0 and LV % GR == 0 and NC % CT == 0 and EP >= E + 1 and NS % 4 == 0

F32, BF16, I32, I16 = mybir.dt.float32, mybir.dt.bfloat16, mybir.dt.int32, mybir.dt.int16
ACT = mybir.ActivationFunctionType
AX = mybir.AxisListType
ds, ts = bass.ds, bass.ts

F_DST, F_KV, F_SRC, F_REL, F_FIRST, F_LAST, NF = 0, 1, 2, 3, 4, 5, 6


class Chain:

    def __init__(self, engine, sem):
        self.engine, self.sem, self.n = engine, sem, 0

    def __call__(self, ins):
        ins.then_inc(self.sem, 1)
        self.n += 1
        self.engine.wait_ge(self.sem, self.n)


class Stage(ExitStack):

    def __init__(self, nc):
        super().__init__()
        self.nc, self.sems = nc, []

    def sem(self, name):
        self.sems.append(self.nc.alloc_semaphore(name))
        return self.sems[-1]

    def __exit__(self, *e):
        if e[0] is None:
            self.nc.clear_and_free_semaphores(self.sems)
            with self.nc.Block():
                pass
        return super().__exit__(*e)


def scratch(nc):
    def d(name, shape, dt=F32):
        return nc.dram_tensor(name, shape, dt, kind="Internal").ap()
    return dict(
        rec=d("rec", (NS, NF * SUP)),
        typerow=d("typerow", (T, NP)),
        kv=d("kv", (NP * R, 2 * D)),
        rel=d("rel_v", (LV,), BF16), first=d("first_v", (LV,), BF16), last=d("last_v", (LV,), BF16),
        att=d("att_v", (H, LV)), self_=d("self_v", (H, LV)),
        w0=d("w0_v", (H, LV)), w1=d("w1_v", (2 * H, LV)),
        val=d("val_v", (NC * P, D)),
        msg=d("msg_v", (NV * P, MSG)),
        x1t=d("x1t", (NP, ROW1)),
    )


def consts(nc, ctx):
    def sb(name, shape, dt=F32):
        return ctx.enter_context(nc.sbuf_tensor(name, shape, dt))
    c = dict(ident=sb("ident", [P, P]), identb=sb("identb", [P, P], BF16), ones=sb("ones", [P, P]),
             iota=sb("iota", [P, P]), piota=sb("piota", [P, 1]), npiota=sb("npiota", [P, 1]),
             one=sb("one", [P, 1]), pint=sb("pint", [P, 1], I32), eps=sb("eps", [P, 1]),
             nbeg=sb("nbeg", [P, NB]))
    sem = nc.alloc_semaphore("const_done")
    with nc.Block() as block:
        @block.gpsimd
        def _(pool):
            done = Chain(pool, sem)
            done(nc.gpsimd.memset(c["ones"][:], 1.0))
            done(nc.gpsimd.memset(c["one"][:], 1.0))
            done(nc.gpsimd.memset(c["eps"][:], EPS))
            done(nc.gpsimd.iota(c["iota"][:], [[1, P]], base=0, channel_multiplier=0,
                                allow_small_or_imprecise_dtypes=True))
            done(nc.gpsimd.iota(c["piota"][:], [[0, 1]], base=0, channel_multiplier=1,
                                allow_small_or_imprecise_dtypes=True))
            done(nc.gpsimd.iota(c["npiota"][:], [[0, 1]], base=0, channel_multiplier=-1,
                                allow_small_or_imprecise_dtypes=True))
            done(nc.gpsimd.iota(c["pint"][:], [[0, 1]], base=0, channel_multiplier=1))
            done(nc.gpsimd.iota(c["nbeg"][:], [[P, NB]], base=0, channel_multiplier=0,
                                allow_small_or_imprecise_dtypes=True))
            done(nc.gpsimd.affine_select(out=c["ident"][:], in_=c["ones"][:], compare_op=ALU.is_equal, fill=0.0,
                                         base=0, pattern=[[-1, P]], channel_multiplier=1))
            done(nc.gpsimd.tensor_copy(c["identb"][:], c["ident"][:]))
    return c


def prepare_edges(nc, ctx, c, dr, src, dst, etype, ntype):
    def keep(name, shape, dt=F32):
        return ctx.enter_context(nc.sbuf_tensor(name, shape, dt))
    v = dict(dr=keep("dr", [P, NC]), kvi=keep("kvi", [P, NC], I32), srci=keep("srci", [P, NC], I32),
             same=keep("same", [P, NV]), blk=keep("blk", [1, NV], I32), drrow=keep("drrow", [P, VT, SUP], BF16),
             vend=keep("vend", [P, NB], I32), types=keep("types", [P, NB, T]))
    Q = NS // 4
    full, rest = divmod(E, SUP)
    tail = full - 3 * Q
    with Stage(nc) as tmp:
        def sb(name, shape, dt=F32):
            return tmp.enter_context(nc.sbuf_tensor(name, shape, dt))

        def sem(name):
            return tmp.sem(name)
        ei = sb("ei", [Q, 3, 4, SUP], I32)
        e_prev = sb("e_prev", [Q, 4, SUP], I32)
        e_next = sb("e_next", [Q, 4, SUP], I32)
        ef = sb("ef", [Q, 4, NF, SUP])
        fprev = sb("fprev", [Q, 4, SUP])
        fnext = sb("fnext", [Q, 4, SUP])
        below = sb("below", [Q, NB])
        junk = sb("junk", [Q, 4, SUP])
        ones49 = sb("es", [P, 1])
        esi = sb("esi", [P, 1], I32)
        turn = sb("turn", [P, 1])
        pplus = sb("pplus", [P, 1])
        viota = sb("viota", [P, NV])
        cmp = sb("cmp", [P, NV])
        tdiag = sb("tdiag", [P, NB])
        bfull = sb("bfull", [P, NV])
        bvt = sb("bvt", [P, VT])
        cvf = sb("cvf", [P, VT])
        cvi = sb("cvi", [P, VT], I32)
        viota4 = sb("viota4", [P, VT])
        b128 = sb("b128", [P, VT])
        rv = sb("rv", [P, VT, NF, SUP])
        dq = sb("dq", [P, VT, SUP])
        va = sb("va", [P, VT, SUP])
        vb = sb("vb", [P, VT, SUP])
        vrow = sb("vrow", [P, 3, VT, SUP], BF16)
        vendf = sb("vendf", [P, NB])
        ti = sb("ti", [NB, P], I32)
        tf = sb("tf", [NB, P])
        tm = sb("tm", [NB, T, P])
        psum = tmp.enter_context(nc.psum_tensor("ps_prep", [P, 4, 512], F32))
        s_init, s_dma, s_vec, s_rec, s_cnt, s_ps, s_idx = map(sem, ("prep_init", "prep_load", "prep_vec", "prep_rec",
                                                                   "prep_cnt", "prep_ps", "prep_idx"))
        s_got, s_wr, s_tr, s_cp, s_ty = map(sem, ("prep_got", "prep_wr", "prep_tr", "prep_cp", "prep_ty"))
        s_pe2 = sem("prep_pe2")
        s_cmp = sem("prep_cmp")
        flat = [dst, src, etype]
        NTR = 3 * 2 * VT
        with nc.Block() as block:
            @block.gpsimd
            def _(pool):
                init = Chain(pool, s_init)
                init(nc.gpsimd.memset(ei[:, 0], PADDST))
                init(nc.gpsimd.memset(ei[:, 1], 0))
                init(nc.gpsimd.memset(ei[:, 2], 0))
                init(nc.gpsimd.memset(e_prev[:], PADDST))
                init(nc.gpsimd.memset(e_prev[0:1, 0, 0:1], -1))
                init(nc.gpsimd.memset(e_next[:], PADDST))
                init(nc.gpsimd.memset(ti[:], T))
                init(nc.gpsimd.iota(viota[:], [[1, NV]], base=0, channel_multiplier=0,
                                    allow_small_or_imprecise_dtypes=True))
                init(nc.gpsimd.iota(viota4[:], [[1, VT]], base=0, channel_multiplier=VT,
                                    allow_small_or_imprecise_dtypes=True))
                init(nc.gpsimd.iota(pplus[:], [[0, 1]], base=1, channel_multiplier=1,
                                    allow_small_or_imprecise_dtypes=True))
                pool.wait_ge(s_rec, 4 * NF * 16)
                pool.wait_ge(s_idx, 1)
                for t in range(VT):
                    nc.gpsimd.indirect_dma_start(
                        out=rv[0:NT, t].rearrange("p f s -> p (f s)"), out_offset=None, in_=dr["rec"],
                        in_offset=bass.IndirectOffsetOnAxis(ap=cvi[0:NT, t:t + 1], axis=0)).then_inc(s_got, 16)
                pool.wait_ge(s_got, 64)

            @block.sync
            def _(sp):
                sp.wait_ge(s_init, 10)
                for n, a in enumerate(flat):
                    sp.dma_start(ei[:, n, 0:3], a[0:3 * Q * SUP].rearrange("(t q s) -> q t s", t=3, s=SUP)).then_inc(s_dma, 16)
                    sp.dma_start(ei[0:tail, n, 3], a[3 * Q * SUP:full * SUP].rearrange("(q s) -> q s", s=SUP)).then_inc(s_dma, 16)
                    sp.dma_start(ei[tail:tail + 1, n, 3, 0:rest], a[full * SUP:E].rearrange("(q s) -> q s", q=1)).then_inc(s_dma, 16)
                sp.dma_start(e_prev[0:1, 0, 1:SUP], dst[0:SUP - 1].rearrange("(q s) -> q s", q=1)).then_inc(s_dma, 16)
                sp.dma_start(e_prev[1:Q, 0], dst[SUP - 1:Q * SUP - 1].rearrange("(q s) -> q s", s=SUP)).then_inc(s_dma, 16)
                sp.dma_start(e_prev[:, 1:3], dst[Q * SUP - 1:3 * Q * SUP - 1].rearrange("(t q s) -> q t s", t=2, s=SUP)).then_inc(s_dma, 16)
                sp.dma_start(e_prev[0:tail, 3], dst[3 * Q * SUP - 1:full * SUP - 1].rearrange("(q s) -> q s", s=SUP)).then_inc(s_dma, 16)
                sp.dma_start(e_prev[tail:tail + 1, 3, 0:rest + 1], dst[full * SUP - 1:E].rearrange("(q s) -> q s", q=1)).then_inc(s_dma, 16)
                sp.dma_start(e_next[:, 0:3], dst[1:3 * Q * SUP + 1].rearrange("(t q s) -> q t s", t=3, s=SUP)).then_inc(s_dma, 16)
                sp.dma_start(e_next[0:tail, 3], dst[3 * Q * SUP + 1:full * SUP + 1].rearrange("(q s) -> q s", s=SUP)).then_inc(s_dma, 16)
                sp.dma_start(e_next[tail:tail + 1, 3, 0:rest - 1], dst[full * SUP + 1:E].rearrange("(q s) -> q s", q=1)).then_inc(s_dma, 16)
                sp.dma_start(ti[0:NB - 1, :], ntype[0:(NB - 1) * P].rearrange("(b p) -> b p", p=P)).then_inc(s_dma, 16)
                sp.dma_start(ti[NB - 1:NB, 0:NLAST], ntype[(NB - 1) * P:N].rearrange("(b p) -> b p", b=1)).then_inc(s_dma, 16)
                sp.wait_ge(s_vec, 1)
                for t in range(4):
                    for f in range(NF):
                        sp.dma_start(dr["rec"][t * Q:(t + 1) * Q, f * SUP:(f + 1) * SUP], ef[:, t, f]).then_inc(s_rec, 16)
                sp.dma_start(dr["typerow"].rearrange("t (b p) -> b t p", p=P), tm[:]).then_inc(s_ty, 16)
                sp.wait_ge(s_vec, 2)
                for n, name in enumerate(("rel", "first", "last")):
                    sp.dma_start(dr[name].rearrange("(i t s) -> i t s", t=VT, s=SUP), vrow[0:NT, n]).then_inc(s_wr, 16)
                sp.wait_ge(s_wr, 48)
                sp.wait_ge(s_ty, 16)

            @block.vector
            def _(dve):
                step = Chain(dve, sem("prep_steps"))
                tt, tsc = nc.vector.tensor_tensor, nc.vector.tensor_scalar
                dve.wait_ge(s_init, 10)
                dve.wait_ge(s_dma, 19 * 16)
                step(nc.vector.tensor_copy(ef[:, :, F_DST], ei[:, 0]))
                step(tsc(ef[:, :, F_KV], ei[:, 1], float(R), None, ALU.mult))
                step(nc.vector.tensor_copy(ef[:, :, F_REL], ei[:, 2]))
                step(tt(ef[:, :, F_KV], ef[:, :, F_KV], ef[:, :, F_REL], ALU.add))
                step(nc.vector.tensor_copy(ef[:, :, F_SRC], ei[:, 1]))
                step(nc.vector.tensor_copy(fprev[:], e_prev[:]))
                step(nc.vector.tensor_copy(fnext[:], e_next[:]))
                step(tt(ef[:, :, F_FIRST], ef[:, :, F_DST], fprev[:], ALU.not_equal))
                step(tt(ef[:, :, F_LAST], ef[:, :, F_DST], fnext[:], ALU.not_equal))
                step(nc.vector.tensor_copy(tf[:], ti[:]))
                for t in range(T):
                    step(tsc(tm[:, t], tf[:], float(t), None, ALU.is_equal))
                nc.vector.memset(below[:, NB - 1:NB], 0.0).then_inc(s_vec, 1)
                for b in range(NB - 1):
                    step(nc.vector.tensor_scalar(junk[:], ef[:, :, F_DST], float((b + 1) * P), None, ALU.is_lt,
                                                 ALU.add, accum_out=below[:, b:b + 1]))
                nc.vector.memset(cmp[:], 0.0).then_inc(s_cnt, 1)
                dve.wait_ge(s_ps, 1)
                step(nc.vector.tensor_copy(esi[0:NB - 1], psum[0:NB - 1, 0, 0:1]))
                step(tsc(esi[0:NB - 1], esi[0:NB - 1], SUP.bit_length() - 1, None, ALU.arith_shift_right))
                step(nc.vector.tensor_copy(turn[0:NB - 1], esi[0:NB - 1]))
                step(tsc(turn[0:NB - 1], turn[0:NB - 1], float(NS - 1), pplus[0:NB - 1, 0:1], ALU.min, ALU.add))
                step(tsc(cmp[0:NB - 1], viota[0:NB - 1], turn[0:NB - 1, 0:1], None, ALU.is_ge))
                tsc(tdiag[0:NB - 1, 0:NB - 1], c["ident"][0:NB - 1, 0:NB - 1], turn[0:NB - 1, 0:1], None,
                    ALU.mult).then_inc(s_cmp, 1)
                dve.wait_ge(s_ps, 2)
                step(nc.vector.tensor_copy(bfull[:], psum[:, 1, 0:NV]))
                step(nc.vector.tensor_copy(bvt[0:NT], psum[0:NT, 2, 0:VT]))
                step(tt(cvf[0:NT], viota4[0:NT], bvt[0:NT], ALU.subtract))
                nc.vector.tensor_copy(cvi[0:NT], cvf[0:NT]).then_inc(s_idx, 1)
                step(nc.vector.memset(v["same"][:, 0:1], 0.0))
                step(tt(v["same"][:, 1:NV], bfull[:, 1:NV], bfull[:, 0:NV - 1], ALU.is_equal))
                step(nc.vector.tensor_copy(v["blk"][:], bfull[0:1, :]))
                step(nc.vector.memset(vendf[:], float(NV - 1)))
                step(tsc(vendf[:, 0:NB - 1], psum[:, 3, 0:NB - 1], 1.0, None, ALU.subtract))
                step(tsc(vendf[:], vendf[:], float(P), c["piota"][:, 0:1], ALU.mult, ALU.add))
                step(nc.vector.tensor_copy(v["vend"][:], vendf[:]))
                step(tsc(b128[0:NT], bvt[0:NT], float(P), None, ALU.mult))
                dve.wait_ge(s_got, 64)
                r = rv[0:NT]
                for t in range(VT):
                    step(tsc(dq[0:NT, t], r[:, t, F_DST], b128[0:NT, t:t + 1], None, ALU.subtract))
                step(tsc(va[0:NT], dq[0:NT], 0.0, None, ALU.is_ge))
                step(tsc(vb[0:NT], dq[0:NT], float(P), None, ALU.is_lt))
                step(tt(va[0:NT], va[0:NT], vb[0:NT], ALU.mult))
                step(tsc(dq[0:NT], dq[0:NT], 1.0, None, ALU.add))
                step(tt(dq[0:NT], dq[0:NT], va[0:NT], ALU.mult))
                step(tsc(dq[0:NT], dq[0:NT], 1.0, None, ALU.subtract))
                step(nc.vector.tensor_copy(v["drrow"][0:NT], dq[0:NT]))
                step(tsc(vb[0:NT], r[:, :, F_REL], 1.0, None, ALU.add))
                step(tt(vb[0:NT], vb[0:NT], va[0:NT], ALU.mult))
                step(tsc(vrow[0:NT, 0], vb[0:NT], 1.0, None, ALU.subtract))
                step(tt(vrow[0:NT, 1], r[:, :, F_FIRST], va[0:NT], ALU.mult))
                tt(vrow[0:NT, 2], r[:, :, F_LAST], va[0:NT], ALU.mult).then_inc(s_vec, 1)
                for n in range(6):
                    dve.wait_ge(s_tr, n + 1)
                    o = (v["dr"], v["kvi"], v["srci"])[n // 2].rearrange("p (i t j) -> p t j i", t=VT, j=2)
                    half = psum[:, n % 2 * 2:n % 2 * 2 + 1, :]
                    k = n % 2
                    for q in range(2):
                        src_ = psum[:, 2 * (n % 2) + q, 0:2 * NT].rearrange("p (j i) -> p j i", j=2)
                        step(nc.vector.tensor_copy(o[:, 2 * k + q], src_))
                    nc.vector.memset(junk[0:1, 0, 0:1], 0.0).then_inc(s_cp, 1)
                    step(nc.vector.memset(junk[0:1, 1, 0:1], 0.0))
                dve.wait_ge(s_tr, 7)
                step(nc.vector.tensor_copy(v["types"][:].rearrange("p b t -> p t b"),
                                           psum[:, 0, 0:T * NB].rearrange("p (t b) -> p t b", t=T)))

            @block.tensor
            def _(pe):
                mm = nc.tensor.matmul
                pe.wait_ge(s_cnt, 1)
                mm(psum[0:NB - 1, 0, 0:1], below[:, 0:NB - 1], c["ones"][0:Q, 0:1], start=True, stop=True).then_inc(s_ps, 1)
                pe.wait_ge(s_cmp, 1)
                mm(psum[:, 1, 0:NV], c["ones"][0:NB - 1, :], cmp[0:NB - 1, :], start=True, stop=True)
                for t in range(VT):
                    mm(psum[0:NT, 2, t:t + 1], cmp[0:NB - 1, t::VT], c["ones"][0:NB - 1, 0:1], start=True, stop=True)
                mm(psum[:, 3, 0:NB - 1], c["ones"][0:NB - 1, :], tdiag[0:NB - 1, 0:NB - 1], start=True, stop=True).then_inc(s_ps, 1)
                pe.wait_ge(s_vec, 2)
                for n in range(6):
                    if n >= 2:
                        pe.wait_ge(s_cp, n - 1)
                    for q in range(2):
                        t = 2 * (n % 2) + q
                        for j in range(2):
                            a = (dq[0:NT, t], rv[0:NT, t, F_KV], rv[0:NT, t, F_SRC])[n // 2][:, j * P:(j + 1) * P]
                            ins = nc.tensor.transpose(psum[:, 2 * (n % 2) + q, j * NT:(j + 1) * NT], a, c["ident"][0:NT, 0:NT])
                    ins.then_inc(s_tr, 1)
                pe.wait_ge(s_cp, 6)
                for t in range(T):
                    ins = nc.tensor.transpose(psum[:, 0, t * NB:(t + 1) * NB], tm[:, t], c["ident"][0:NB, 0:NB])
                ins.then_inc(s_tr, 1)
    return v


def node_stats(nc, c, tag, xs, mv, scale, shift, load=None):
    with Stage(nc) as tmp:
        stats = tmp.enter_context(nc.sbuf_tensor(f"stats_{tag}", [P, NB, 6], F32))
        std = tmp.enter_context(nc.sbuf_tensor(f"std_{tag}", [P, NB], F32))
        s_in, s_st, s_ag, s_sq, s_step = (tmp.sem(f"{n}_{tag}")
                                          for n in ("st_in", "st_bn", "st_ag", "st_sq", "st_step"))
        with nc.Block() as block:
            if load is not None:
                @block.sync
                def _(sp):
                    sp.dma_start(xs[:, 0:NB - 1], load[0:(NB - 1) * P].rearrange("(b p) d -> p b d", p=P)).then_inc(s_in, 16)
                    sp.dma_start(xs[0:NLAST, NB - 1], load[(NB - 1) * P:N]).then_inc(s_in, 16)

            @block.vector
            def _(dve):
                if load is not None:
                    dve.wait_ge(s_in, 32)
                for b in range(NB):
                    nc.vector.bn_stats(stats[:, b], xs[:, b, 0:D]).then_inc(s_st, 1)
                for b in range(NB):
                    dve.wait_ge(s_st, b + 1)
                    nc.vector.bn_aggr(mv[:, b], stats[:, b]).then_inc(s_ag, 1)
                step = Chain(dve, s_step)
                dve.wait_ge(s_sq, 1)
                step(nc.vector.reciprocal(scale[:], std[:]))
                step(nc.vector.scalar_tensor_tensor(out=shift[:], in0=mv[:, :, 0], scalar=-1.0, in1=scale[:],
                                                    op0=ALU.mult, op1=ALU.mult))

            @block.scalar
            def _(act):
                act.wait_ge(s_ag, NB)
                nc.scalar.activation(std[:], mv[:, :, 1], ACT.Sqrt, bias=c["eps"][:, 0:1]).then_inc(s_sq, 1)


def project(nc, c, dr, v, xs, qs, scale, shift, a):
    with Stage(nc) as tmp:
        def sb(name, shape, dt=F32):
            return tmp.enter_context(nc.sbuf_tensor(name, shape, dt))

        def sem(name):
            return tmp.sem(name)
        wkv = sb("wkv", [P, 2, T, 2, D])
        wq = sb("wq", [P, 2, T, D])
        bkv = sb("bkv", [T, 2, D])
        bq = sb("bq", [T, D])
        rel = sb("relw", [P, 2, 2, R, P])
        pri = sb("pri", [P, R, H])
        tsc_ = sb("tscale", [P, T, NB])
        tsh_ = sb("tshift", [P, T, NB])
        tmb = sb("tmb", [T, P])
        hm = sb("hm", [P, T, D])
        hT = sb("hT", [P, T * 2, P])
        kvT = sb("kvT", [P, 4, P])
        stage = sb("stage", [P, 2, R, D])
        psT = tmp.enter_context(nc.psum_tensor("psT", [P, 2, 512], F32))
        psKV = tmp.enter_context(nc.psum_tensor("psKV", [P, 512], F32))
        psQ = tmp.enter_context(nc.psum_tensor("psQ", [P, 512], F32))
        psR = tmp.enter_context(nc.psum_tensor("psR", [P, 4, 512], F32))
        w_in, z_done, pri_done, mk_done = map(sem, ("w_in", "z_done", "pri_done", "mk_done"))
        hm_done, tr_done, hT_done, kv_done, kvT_done, q_done, q_out = map(sem, (
            "hm_done", "tr_done", "hT_done", "kv_done", "kvT_done", "q_done", "q_out"))
        rel_done, rel_dve, rel_act, tm_in, k_wr, v_wr = map(sem, ("rel_done", "rel_dve", "rel_act", "tm_in", "k_wr", "v_wr"))
        with nc.Block() as block:
            @block.gpsimd
            def _(pool):
                nc.gpsimd.memset(rel[:], 0.0).then_inc(z_done, 1)

            @block.sync
            def _(sp):
                sp.sem_inc(k_wr, 16)
                sp.sem_inc(v_wr, 16)
                for t in range(T):
                    for o, w in ((wkv[:, :, t, 0], a['L0_gnn_Wk']), (wkv[:, :, t, 1], a['L0_gnn_Wv']), (wq[:, :, t], a['L0_gnn_Wq'])):
                        sp.dma_start(o, w[t].rearrange("(g p) d -> p g d", p=P)).then_inc(w_in, 16)
                sp.dma_start(bkv[:, 0], a['L0_gnn_bk']).then_inc(w_in, 16)
                sp.dma_start(bkv[:, 1], a['L0_gnn_bv']).then_inc(w_in, 16)
                sp.dma_start(bq[:], a['L0_gnn_bq']).then_inc(w_in, 16)
                sp.dma_start(pri[:].rearrange("p r h -> p (r h)"), a['L0_gnn_rel_pri'].rearrange("(o r) h -> o (r h)", o=1).to_broadcast([P, R * H])).then_inc(w_in, 16)
                sp.wait_ge(z_done, 1)
                for n, w in enumerate((a['L0_gnn_rel_att'], a['L0_gnn_rel_msg'])):
                    for g in range(2):
                        for u in range(2):
                            sp.dma_start(rel[u * DK:(u + 1) * DK, n, g, :, u * DK:(u + 1) * DK],
                                         w[:, 2 * g + u].rearrange("r d e -> d r e")).then_inc(w_in, 16)

                def block_io(b, first=False):
                    if not first:
                        sp.wait_ge(q_done, b)
                    sp.dma_start(tmb[:], dr["typerow"][:, ts(b, P)]).then_inc(tm_in, 16)
                    for n, s in ((0, k_wr), (1, v_wr)):
                        sp.wait_ge(rel_dve, 4 * b + 2 * n + 4)
                        sp.wait_ge(rel_act, 4 * b + 2 * n + 4)
                        sp.dma_start(dr["kv"].rearrange("(b p r) d -> b p r d", p=P, r=R)[ds(b, 1), :, :, n * D:(n + 1) * D]
                                     .rearrange("o p r d -> (o p) r d"), stage[:, n]).then_inc(s, 16)
                block_io(0, True)
                with sp.Fori(1, NB) as b:
                    block_io(b)
                sp.wait_ge(k_wr, 16 * (NB + 1))
                sp.wait_ge(v_wr, 16 * (NB + 1))

            @block.scalar
            def _(act):
                act.sem_inc(rel_act, 2)
                act.sem_inc(kvT_done, 1)

                def masked(b):
                    for t in range(T):
                        nc.scalar.activation(hm[:, t], xs[:, ds(b, 1)].rearrange("p o d -> p (o d)"), ACT.Relu,
                                             bias=tsh_[:, t, ds(b, 1)], scale=tsc_[:, t, ds(b, 1)]).then_inc(hm_done, 1)
                act.wait_ge(mk_done, 1)
                masked(0)

                def rest(b, more):
                    act.wait_ge(kv_done, b + 1)
                    act.wait_ge(rel_done, 8 * b + 1)
                    nc.scalar.copy(kvT[:].rearrange("p n q -> p (n q)"), psKV[:]).then_inc(kvT_done, 1)
                    if more:
                        act.wait_ge(tr_done, b + 1)
                        masked(b + 1)
                    for m in range(1, 8, 2):
                        n, g, u = m // 4, m // 2 % 2, m % 2
                        act.wait_ge(rel_done, 8 * b + m + 2)
                        if m < 2 or m == 5:
                            act.wait_ge((k_wr, v_wr)[n], 16 * (b + 1))
                        nc.scalar.copy(stage[:, n, 3 * u:3 * u + 3, g * P:(g + 1) * P],
                                       psR[:, m % 4, 0:3 * P].rearrange("p (r e) -> p r e", r=3)).then_inc(rel_act, 1)
                with act.Fori(0, NB - 1) as b:
                    rest(b, True)
                rest(NB - 1, False)

            @block.vector
            def _(dve):
                step = Chain(dve, sem("proj_steps"))
                dve.sem_inc(rel_dve, 2)
                for t in range(T):
                    step(nc.vector.tensor_tensor(tsc_[:, t], scale[:], v["types"][:, :, t], ALU.mult))
                    step(nc.vector.tensor_tensor(tsh_[:, t], shift[:], v["types"][:, :, t], ALU.mult))
                nc.vector.memset(hT[0:1, 0, 0:1], 0.0).then_inc(mk_done, 1)
                dve.wait_ge(w_in, (9 + 4 + 8) * 16)
                step(nc.vector.tensor_scalar(pri[:], pri[:], float(DK) ** -0.5, None, ALU.mult))
                for g in range(2):
                    for u in range(2):
                        w = rel[u * DK:(u + 1) * DK, 0, g, :, u * DK:(u + 1) * DK]
                        nc.vector.tensor_tensor(w, w, pri[u * DK:(u + 1) * DK, :, 2 * g + u].unsqueeze(2).to_broadcast([DK, R, DK]),
                                                ALU.mult).then_inc(pri_done, 1)

                def turn_(b):
                    dve.wait_ge(tr_done, b + 1)
                    dve.wait_ge(q_done, b + 1)
                    nc.vector.tensor_copy(hT[:, 0:4].rearrange("p n q -> p (n q)"), psT[:, 0, :]).then_inc(hT_done, 1)
                    nc.vector.tensor_copy(hT[:, 4:6].rearrange("p n q -> p (n q)"), psT[:, 1, 0:2 * P]).then_inc(hT_done, 1)

                def rest(b):
                    for m in range(0, 8, 2):
                        n, g, u = m // 4, m // 2 % 2, m % 2
                        dve.wait_ge(rel_done, 8 * b + m + 2)
                        if m in (0, 4):
                            dve.wait_ge((k_wr, v_wr)[n], 16 * (b + 1))
                        nc.vector.tensor_copy(stage[:, n, 3 * u:3 * u + 3, g * P:(g + 1) * P],
                                              psR[:, m % 4, 0:3 * P].rearrange("p (r e) -> p r e", r=3)).then_inc(rel_dve, 1)
                        if m == 2:
                            dve.wait_ge(q_done, b + 2)
                            nc.vector.tensor_copy(qs[:, ds(b, 1)].rearrange("p o d -> p (o d)"), psQ[:, 0:D]).then_inc(q_out, 1)
                turn_(0)
                with dve.Fori(0, NB - 1) as b:
                    turn_(b + 1)
                    rest(b)
                rest(NB - 1)

            @block.tensor
            def _(pe):
                pe.sem_inc(rel_done, 1)
                pe.sem_inc(q_done, 1)

                def transposes(b, first=False):
                    pe.wait_ge(hm_done, 3 * (b + 1))
                    if not first:
                        pe.wait_ge(hT_done, 2 * b)
                    for n in range(6):
                        t, g = n // 2, n % 2
                        ins = nc.tensor.transpose(psT[:, n // 4, n % 4 * P:(n % 4 + 1) * P], hm[:, t, g * P:(g + 1) * P], c["ident"][:])
                    ins.then_inc(tr_done, 1)

                def block_(b, more, first=False):
                    pe.wait_ge(hT_done, 2 * (b + 1))
                    pe.wait_ge(tm_in, 16 * (b + 1))
                    pe.wait_ge(kvT_done, b + 1)
                    for n in range(4):
                        for t in range(T):
                            for g in range(2):
                                nc.tensor.matmul(psKV[:, n * P:(n + 1) * P], wkv[:, g, t, n // 2, n % 2 * P:(n % 2 + 1) * P],
                                                 hT[:, 2 * t + g], start=(t == 0 and g == 0), stop=False)
                        ins = nc.tensor.matmul(psKV[:, n * P:(n + 1) * P], bkv[:, n // 2, n % 2 * P:(n % 2 + 1) * P], tmb[:],
                                               start=False, stop=True)
                    ins.then_inc(kv_done, 1)
                    if not first:
                        pe.wait_ge(q_out, b)
                    for t in range(T):
                        for g in range(2):
                            nc.tensor.matmul(psQ[:, 0:D], hT[:, 2 * t + g], wq[:, g, t], start=(t == 0 and g == 0), stop=False)
                    nc.tensor.matmul(psQ[:, 0:D], tmb[:], bq[:], start=False, stop=True).then_inc(q_done, 1)
                    if more:
                        transposes(b + 1)
                    pe.wait_ge(kvT_done, b + 2)
                    for m in range(8):
                        n, g, u = m // 4, m // 2 % 2, m % 2
                        pe.wait_ge((rel_dve, rel_act)[m % 2], 4 * b + m // 2 + 1)
                        nc.tensor.matmul(psR[:, m % 4, 0:3 * P], kvT[:, 2 * n + g],
                                         rel[:, n, g, 3 * u:3 * u + 3].rearrange("p r e -> p (r e)"),
                                         start=True, stop=True).then_inc(rel_done, 1)
                pe.wait_ge(w_in, (9 + 4 + 8) * 16)
                pe.wait_ge(pri_done, 4)
                transposes(0, True)
                block_(0, True, True)
                with pe.Fori(1, NB - 1) as b:
                    block_(b, True)
                block_(NB - 1, False)


GS = 4
SLOTS = 4 * GS
NI = NC // SLOTS


def edge_scores(nc, c, dr, v, layer, table, index, node, width):
    L = layer
    vcol = D if L == 0 else 0
    cols = D if L == 0 else 2 * H
    with Stage(nc) as tmp:
        def sb(name, shape, dt=F32):
            return tmp.enter_context(nc.sbuf_tensor(f"{name}{L}", shape, dt))

        def sem(name):
            return tmp.sem(f"{name}{L}")
        rows = sb("rows", [P, SLOTS, width])
        ids = sb("ids", [P, SLOTS], I32)
        off = sb("off", [P, 2, SUP])
        hot = sb("hot", [P, 2, SUP])
        prod = sb("prod", [P, 4, D])
        sc = sb("sc", [P, SLOTS, H])
        att = sb("att", [P, H, NC])
        own = sb("own", [P, H, NC]) if L == 1 else None
        stage = sb("stage_att", [CW, 2, H, P])
        psB = tmp.enter_context(nc.psum_tensor(f"psB{L}", [P, 2, 512], F32))
        psD = tmp.enter_context(nc.psum_tensor(f"psD{L}", [P, 4, 512], F32))
        psX = tmp.enter_context(nc.psum_tensor(f"psX{L}", [P, 2, 512], F32))
        got = [sem(f"got{k}_") for k in range(SLOTS)]
        kept = [sem(f"kept{g}_") for g in range(SLOTS // GS)]
        ids_done, go, used, bc_done, off_done, hot_done, dst_done, prod_done, sc_done, sc_kept = map(sem, (
            "ids_done", "go", "used", "bc_done", "off_done", "hot_done", "dst_done", "prod_done", "sc_done", "sc_kept"))
        tr_done, tr_out = map(sem, ("atr_done", "atr_out"))
        wr = [sem("awr0_"), sem("awr1_")]
        NX = CT * (1 + (L == 1))
        with nc.Block() as block:
            @block.gpsimd
            def _(pool):
                with pool.Fori(0, NI) as i:
                    for g in range(SLOTS // GS):
                        pool.wait_ge(used, i * SLOTS + (g + 1) * GS)
                        pool.sem_inc(go, 1)
                        pool.wait_ge(kept[g], 16 * (i + 1))
                        pool.sem_inc(go, 1)
                        nc.gpsimd.tensor_copy(ids[:, g * GS:(g + 1) * GS],
                                              index[:, ts(i * (SLOTS // GS) + g, GS)]).then_inc(ids_done, 1)
                        pool.wait_ge(ids_done, i * (SLOTS // GS) + g + 1)
                        pool.sem_inc(go, 1)
                        for k in range(g * GS, (g + 1) * GS):
                            nc.gpsimd.indirect_dma_start(
                                out=rows[:, k], out_offset=None, in_=table,
                                in_offset=bass.IndirectOffsetOnAxis(ap=ids[:, k:k + 1], axis=0)).then_inc(got[k], 16)

            @block.sync
            def _(sp):
                for s in kept:
                    sp.sem_inc(s, 16)
                with sp.Fori(0, NI) as i:
                    for g in range(SLOTS // GS):
                        for k in range(g * GS, (g + 1) * GS):
                            sp.wait_ge(got[k], 16 * (i + 1))
                        o = dr["val"].rearrange("(i k p) d -> i p k d", k=GS, p=P)[ds(i * (SLOTS // GS) + g, 1)]
                        sp.dma_start(o.rearrange("o p k d -> (o p) k d"), rows[:, g * GS:(g + 1) * GS, vcol:vcol + D]).then_inc(kept[g], 16)
                for n in range(NX):
                    a = dr["att"] if n < CT else dr["self_"]
                    sp.wait_ge(tr_out, n + 1)
                    sp.dma_start(a.rearrange("h (t c p) -> t c h p", t=CT, p=P)[n % CT], stage[:, n % 2]).then_inc(wr[n % 2], 16)
                for s in kept:
                    sp.wait_ge(s, 16 * (NI + 1))
                for s in wr:
                    sp.wait_ge(s, 16 * (NX // 2))

            @block.tensor
            def _(pe):
                pe.sem_inc(dst_done, 4)
                with pe.Fori(0, NI) as i:
                    blk = [pe.value_load(v["blk"][0:1, ds(i * (SLOTS // 2) + t, 1)], min_val=0, max_val=NB - 1)
                           for t in range(SLOTS // 2)]

                    def spread_places(t):
                        pe.wait_ge(off_done, i * (SLOTS // 2) + t + 1)
                        row = c["identb"][0:NT, ds(i * (SLOTS // 2 // VT) + t // VT, 1)].to_broadcast([NT, P])
                        nc.tensor.matmul(psB[:, t % 2, 0:SUP], row, v["drrow"][0:NT, t % VT], start=True, stop=True).then_inc(bc_done, 1)
                    spread_places(0)
                    for t in range(SLOTS // 2):
                        if t + 1 < SLOTS // 2:
                            spread_places(t + 1)
                        pe.wait_ge(hot_done, i * (SLOTS // 2) + t + 1)
                        for j in range(2):
                            k = 2 * t + j
                            pe.wait_ge(prod_done, i * SLOTS + k + 1)
                            nc.tensor.matmul(psD[:, k % 4, 0:cols], hot[:, t % 2, j * P:(j + 1) * P],
                                             node[:, ds(blk[t], 1)].rearrange("p o d -> p (o d)"), start=True, stop=True).then_inc(dst_done, 1)
                for n in range(NX):
                    a = att if n < CT else own
                    if n == 0:
                        pe.wait_ge(sc_kept, 2 * NI if L == 1 else NI)
                    if n >= 2:
                        pe.wait_ge(tr_out, n - 1)
                    for h in range(H):
                        ins = nc.tensor.transpose(psX[0:CW, n % 2, h * P:(h + 1) * P], a[:, h, n % CT * CW:(n % CT + 1) * CW], c["ident"][:])
                    ins.then_inc(tr_done, 1)

            @block.scalar
            def _(act):
                act.sem_inc(off_done, 2)
                with act.Fori(0, NI) as i:
                    for t in range(SLOTS // 2):
                        V = i * (SLOTS // 2) + t
                        act.wait_ge(bc_done, V + 1)
                        nc.scalar.activation(off[:, t % 2], psB[:, t % 2, 0:SUP], ACT.Abs, bias=c["npiota"][:, 0:1]).then_inc(off_done, 1)
                        act.wait_ge(off_done, V + 3)
                        act.wait_ge(dst_done, 2 * V)
                        nc.scalar.activation(hot[:, t % 2], off[:, t % 2], ACT.Relu, bias=1.0, scale=-1.0).then_inc(hot_done, 1)

            @block.vector
            def _(dve):
                dve.sem_inc(used, SLOTS)
                dve.sem_inc(prod_done, 4)
                dve.sem_inc(sc_done, 4)
                with dve.Fori(0, NI) as i:
                    K = i * SLOTS

                    def reduce_(k):
                        dve.wait_ge(prod_done, K + k + 5)
                        nc.vector.tensor_reduce(sc[:, k], prod[:, k % 4].rearrange("p (h d) -> p h d", h=H), AX.X, ALU.add).then_inc(sc_done, 1)
                    for k in range(SLOTS):
                        dve.wait_ge(got[k], 16 * (i + 1))
                        dve.wait_ge(dst_done, K + k + 5)
                        if L == 0:
                            dve.wait_ge(sc_done, K + k + 1)
                            ins = nc.vector.tensor_tensor(prod[:, k % 4], rows[:, k, 0:D], psD[:, k % 4, 0:D], ALU.mult)
                            ins.then_inc(prod_done, 1)
                            if k:
                                reduce_(k - 1)
                        else:
                            nc.vector.tensor_tensor(sc[:, k], rows[:, k, D:D + H], psD[:, k % 4, 0:H], ALU.add).then_inc(sc_done, 1)
                            nc.vector.tensor_copy(own[:, :, ds(K + k, 1)].rearrange("p h o -> p (h o)"), psD[:, k % 4, H:2 * H]).then_inc(prod_done, 1)
                        if k % GS == GS - 1:
                            if L == 0:
                                dve.wait_ge(prod_done, K + k + 5)
                            else:
                                dve.wait_ge(sc_done, K + k + 5)
                            dve.sem_inc(used, GS)
                    if L == 0:
                        reduce_(SLOTS - 1)
                    dve.wait_ge(sc_done, K + SLOTS + 4)
                    nc.vector.tensor_copy(att[:, :, ts(i, SLOTS)], sc[:].rearrange("p k h -> p h k")).then_inc(sc_kept, 1)
                    dve.wait_ge(sc_kept, i + 1)
                if L == 1:
                    dve.wait_ge(prod_done, NC + 4)
                    dve.sem_inc(sc_kept, NI)
                for n in range(NX):
                    dve.wait_ge(tr_done, n + 1)
                    if n >= 2:
                        dve.wait_ge(wr[n % 2], 16 * (n // 2))
                    nc.vector.tensor_copy(stage[:, n % 2].rearrange("c h p -> c (h p)"), psX[0:CW, n % 2]).then_inc(tr_out, 1)


def run_flags(nc, dr, sp, sem, tiles):
    for tile, name in tiles:
        for h in range(H):
            sp.dma_start(tile[h * GR:(h + 1) * GR], dr[name].rearrange("(g s) -> g s", s=SL)).then_inc(sem, 16)


class Carry:

    def __init__(self, nc, c, tmp, tag):
        def sb(name, shape, dt=F32):
            return tmp.enter_context(nc.sbuf_tensor(f"{name}_{tag}", shape, dt))
        self.nc, self.c = nc, c
        self.edge = sb("edge", [P, 2])
        self.row = sb("crow", [1, 2, P])
        self.flag = sb("cflag", [1, 2, P])
        self.got = sb("cgot", [1, 2, P + 1])
        self.back = sb("cback", [P, 2])
        self.ps = tmp.enter_context(nc.psum_tensor(f"ps_carry_{tag}", [P, 512], F32))
        self.psb = tmp.enter_context(nc.psum_tensor(f"ps_cback_{tag}", [P, 512], F32))
        self.out, self.inn, self.ret, self.done = (tmp.sem(f"{n}_{tag}")
                                                   for n in ("c_edge", "c_row", "c_got", "c_back"))
        self.n = self.m = 0

    def to_row(self, step, dve, a, b, o):
        nc = self.nc
        step(nc.vector.tensor_copy(self.edge[:, 0:1], a))
        nc.vector.tensor_copy(self.edge[:, 1:2], b).then_inc(self.out, 1)
        self.n += 1
        dve.wait_ge(self.inn, self.n)
        step(nc.vector.tensor_copy(o[:].rearrange("a b p -> a (b p)"), self.ps[0:1, 0:2 * P]))

    def carry(self, step, dve, a, b, neutral, op0, op1):
        nc = self.nc
        self.to_row(step, dve, a, b, self.row)
        step(nc.vector.memset(self.got[:], neutral))
        step(nc.vector.tensor_tensor_scan(self.got[0:1, 0, 1:P + 1], self.flag[0:1, 0], self.row[0:1, 0], neutral, op0, op1))
        nc.vector.tensor_tensor_scan(self.got[0:1, 1, 0:P][:, ::-1], self.flag[0:1, 1][:, ::-1], self.row[0:1, 1][:, ::-1],
                                     neutral, op0, op1).then_inc(self.ret, 1)
        self.m += 1
        dve.wait_ge(self.done, self.m)
        step(nc.vector.tensor_copy(self.back[:], self.psb[:, 0:2]))

    def tensor(self, pe, plan):
        nc, n, m = self.nc, 0, 0
        for back in plan:
            n += 1
            pe.wait_ge(self.out, n)
            nc.tensor.transpose(self.ps[0:1, 0:P], self.edge[:, 0:1], self.c["ident"][:])
            nc.tensor.transpose(self.ps[0:1, P:2 * P], self.edge[:, 1:2], self.c["ident"][:]).then_inc(self.inn, 1)
            if back:
                m += 1
                pe.wait_ge(self.ret, m)
                nc.tensor.matmul(self.psb[:, 0:1], self.got[0:1, 0, 0:P], self.c["one"][0:1], start=True, stop=True)
                nc.tensor.matmul(self.psb[:, 1:2], self.got[0:1, 1, 1:P + 1], self.c["one"][0:1], start=True, stop=True).then_inc(self.done, 1)


def softmax_by_relation(nc, c, dr):
    with Stage(nc) as tmp:
        def sb(name, shape, dt=F32):
            return tmp.enter_context(nc.sbuf_tensor(name, shape, dt))
        att, am, fw, bw, sel = (sb(n, [P, SL]) for n in ("s_att", "s_am", "s_fw", "s_bw", "s_sel"))
        rel, fi, la, pf, sf, mk = (sb(n, [P, SL], BF16) for n in ("s_rel", "s_fi", "s_la", "s_pf", "s_sf", "s_mk"))
        s_in, s_e, s_x, s_w, s_out, s_fl = (tmp.sem(n) for n in ("sm_in", "sm_e", "sm_x", "sm_w", "sm_out", "sm_st"))
        cy = Carry(nc, c, tmp, "r")
        view = "h (g s) -> (h g) s"
        with nc.Block() as block:
            @block.sync
            def _(sp):
                sp.dma_start(att[:], dr["att"].rearrange(view, g=GR)).then_inc(s_in, 16)
                run_flags(nc, dr, sp, s_in, ((rel, "rel"), (fi, "first"), (la, "last")))
                sp.wait_ge(s_w, 1)
                sp.dma_start(dr["w0"].rearrange(view, g=GR), att[:]).then_inc(s_out, 16)
                sp.wait_ge(s_out, 16)

            @block.scalar
            def _(act):
                act.wait_ge(s_e, 1)
                nc.scalar.activation(att[:], att[:], ACT.Exp).then_inc(s_x, 1)

            @block.tensor
            def _(pe):
                cy.tensor(pe, ([False] + [True] * R) * 2)

            @block.vector
            def _(dve):
                step = Chain(dve, s_fl)
                tt, tsc, stt, scan = (nc.vector.tensor_tensor, nc.vector.tensor_scalar, nc.vector.scalar_tensor_tensor,
                                      nc.vector.tensor_tensor_scan)
                dve.wait_ge(s_in, 16 * (1 + 3 * H))
                step(tsc(fi[:], fi[:], -BIG, None, ALU.mult))
                step(tsc(la[:], la[:], -BIG, None, ALU.mult))
                step(scan(pf[:], fi[:], fi[:], 0.0, ALU.add, ALU.min))
                step(scan(sf[:][:, ::-1], la[:][:, ::-1], la[:][:, ::-1], 0.0, ALU.add, ALU.min))
                cy.to_row(step, dve, pf[:, SL - 1:SL], sf[:, 0:1], cy.flag)
                step(nc.vector.memset(sel[:], 0.0))
                for r in range(R):
                    step(tsc(mk[:], rel[:], float(r), -BIG, ALU.not_equal, ALU.mult))
                    step(tt(am[:], att[:], mk[:], ALU.add))
                    step(scan(fw[:], fi[:], am[:], -BIG, ALU.add, ALU.max))
                    step(scan(bw[:][:, ::-1], la[:][:, ::-1], am[:][:, ::-1], -BIG, ALU.add, ALU.max))
                    cy.carry(step, dve, fw[:, SL - 1:SL], bw[:, 0:1], -BIG, ALU.add, ALU.max)
                    step(tt(fw[:], fw[:], bw[:], ALU.max))
                    step(stt(out=fw[:], in0=pf[:], scalar=cy.back[:, 0:1], in1=fw[:], op0=ALU.add, op1=ALU.max))
                    step(stt(out=fw[:], in0=sf[:], scalar=cy.back[:, 1:2], in1=fw[:], op0=ALU.add, op1=ALU.max))
                    step(tsc(mk[:], rel[:], float(r), None, ALU.is_equal))
                    step(nc.vector.copy_predicated(sel[:], mk[:].bitcast(I16), fw[:]))
                tt(att[:], att[:], sel[:], ALU.subtract).then_inc(s_e, 1)
                step(tsc(fi[:], fi[:], 0.0, None, ALU.is_equal))
                step(tsc(la[:], la[:], 0.0, None, ALU.is_equal))
                step(tsc(pf[:], pf[:], 0.0, None, ALU.is_equal))
                step(tsc(sf[:], sf[:], 0.0, None, ALU.is_equal))
                cy.to_row(step, dve, pf[:, SL - 1:SL], sf[:, 0:1], cy.flag)
                step(nc.vector.memset(sel[:], 1.0))
                dve.wait_ge(s_x, 1)
                for r in range(R):
                    step(tsc(mk[:], rel[:], float(r), None, ALU.is_equal))
                    step(tt(am[:], att[:], mk[:], ALU.mult))
                    step(scan(fw[:], fi[:], am[:], 0.0, ALU.mult, ALU.add))
                    step(scan(bw[:][:, ::-1], la[:][:, ::-1], am[:][:, ::-1], 0.0, ALU.mult, ALU.add))
                    cy.carry(step, dve, fw[:, SL - 1:SL], bw[:, 0:1], 0.0, ALU.mult, ALU.add)
                    step(tt(bw[:], bw[:], am[:], ALU.subtract))
                    step(tt(fw[:], fw[:], bw[:], ALU.add))
                    step(stt(out=fw[:], in0=pf[:], scalar=cy.back[:, 0:1], in1=fw[:], op0=ALU.mult, op1=ALU.add))
                    step(stt(out=fw[:], in0=sf[:], scalar=cy.back[:, 1:2], in1=fw[:], op0=ALU.mult, op1=ALU.add))
                    step(nc.vector.copy_predicated(sel[:], mk[:].bitcast(I16), fw[:]))
                step(nc.vector.reciprocal(sel[:], sel[:]))
                tt(att[:], att[:], sel[:], ALU.mult).then_inc(s_w, 1)


def softmax_weights(nc, c, dr):
    with Stage(nc) as tmp:
        def sb(name, shape, dt=F32):
            return tmp.enter_context(nc.sbuf_tensor(name, shape, dt))
        att, own, fw, bw = (sb(n, [P, SL]) for n in ("t_att", "t_own", "t_fw", "t_bw"))
        rel, fi, la, pf, sf = (sb(n, [P, SL], BF16) for n in ("t_rel", "t_fi", "t_la", "t_pf", "t_sf"))
        s_in, s_e, s_x, s_w, s_out, s_fl = (tmp.sem(n) for n in ("tm_in_", "tm_e", "tm_x", "tm_w", "tm_out", "tm_st"))
        cy = Carry(nc, c, tmp, "w")
        view = "h (g s) -> (h g) s"
        with nc.Block() as block:
            @block.sync
            def _(sp):
                sp.dma_start(att[:], dr["att"].rearrange(view, g=GR)).then_inc(s_in, 16)
                sp.dma_start(own[:], dr["self_"].rearrange(view, g=GR)).then_inc(s_in, 16)
                run_flags(nc, dr, sp, s_in, ((rel, "rel"), (fi, "first"), (la, "last")))
                sp.wait_ge(s_x, 1)
                sp.dma_start(dr["w1"][0:H].rearrange(view, g=GR), att[:]).then_inc(s_out, 16)
                sp.wait_ge(s_w, 1)
                sp.dma_start(dr["w1"][H:2 * H].rearrange(view, g=GR), own[:]).then_inc(s_out, 16)
                sp.wait_ge(s_out, 32)

            @block.scalar
            def _(act):
                act.wait_ge(s_e, 1)
                nc.scalar.activation(att[:], att[:], ACT.Exp).then_inc(s_x, 1)
                act.wait_ge(s_e, 2)
                nc.scalar.activation(own[:], own[:], ACT.Exp).then_inc(s_x, 1)

            @block.tensor
            def _(pe):
                cy.tensor(pe, [False, True])

            @block.vector
            def _(dve):
                step = Chain(dve, s_fl)
                tt, tsc, stt, scan = (nc.vector.tensor_tensor, nc.vector.tensor_scalar, nc.vector.scalar_tensor_tensor,
                                      nc.vector.tensor_tensor_scan)
                dve.wait_ge(s_in, 16 * (2 + 3 * H))
                step(stt(out=att[:], in0=att[:], scalar=SLOPE, in1=att[:], op0=ALU.mult, op1=ALU.max))
                step(tsc(rel[:], rel[:], 0.0, -BIG, ALU.is_lt, ALU.mult))
                step(tt(bw[:], att[:], own[:], ALU.max))
                step(tt(bw[:], bw[:], rel[:], ALU.add))
                step(tsc(la[:], la[:], -BIG, None, ALU.mult))
                step(tsc(rel[:], fi[:], 1.0, None, ALU.mult))
                step(tsc(fi[:], fi[:], -BIG, None, ALU.mult))
                step(scan(pf[:], fi[:], fi[:], 0.0, ALU.add, ALU.min))
                step(scan(sf[:][:, ::-1], la[:][:, ::-1], la[:][:, ::-1], 0.0, ALU.add, ALU.min))
                cy.to_row(step, dve, pf[:, SL - 1:SL], sf[:, 0:1], cy.flag)
                step(scan(fw[:], fi[:], bw[:], -BIG, ALU.add, ALU.max))
                step(scan(bw[:][:, ::-1], la[:][:, ::-1], bw[:][:, ::-1], -BIG, ALU.add, ALU.max))
                cy.carry(step, dve, fw[:, SL - 1:SL], bw[:, 0:1], -BIG, ALU.add, ALU.max)
                step(tt(fw[:], fw[:], bw[:], ALU.max))
                step(stt(out=fw[:], in0=pf[:], scalar=cy.back[:, 0:1], in1=fw[:], op0=ALU.add, op1=ALU.max))
                step(stt(out=fw[:], in0=sf[:], scalar=cy.back[:, 1:2], in1=fw[:], op0=ALU.add, op1=ALU.max))
                step(tt(att[:], att[:], fw[:], ALU.subtract))
                tsc(att[:], att[:], 0.0, None, ALU.min).then_inc(s_e, 1)
                step(tt(own[:], own[:], fw[:], ALU.subtract))
                tsc(own[:], own[:], 0.0, None, ALU.min).then_inc(s_e, 1)
                dve.wait_ge(s_x, 2)
                tt(own[:], own[:], rel[:], ALU.mult).then_inc(s_w, 1)


def sum_messages(nc, c, dr, v, layer, weights, nh):
    L = layer
    width = D + nh
    V8 = SLOTS // 2
    with Stage(nc) as tmp:
        def sb(name, shape, dt=F32):
            return tmp.enter_context(nc.sbuf_tensor(f"{name}{L}", shape, dt))

        def sem(name):
            return tmp.sem(f"{name}{L}")
        win = sb("win", [CW, 2, nh, P])
        w = sb("wgt", [P, NC, nh])
        rows = sb("vrows", [P, SLOTS, D])
        wv = sb("wv", [P, SLOTS, width])
        hot = sb("vhot", [P, SLOTS, P])
        run = sb("run", [P, V8, MSG])
        psW = tmp.enter_context(nc.psum_tensor(f"psW{L}", [P, 2, 1024], F32))
        psM = tmp.enter_context(nc.psum_tensor(f"psM{L}", [P, 4, 512], F32))
        w_in = [sem("w_in0_"), sem("w_in1_")]
        loaded = [sem(f"loaded{g}_") for g in range(4)]
        saved = [sem(f"saved{g}_") for g in range(2)]
        wv_done = [sem("wv_even_"), sem("wv_odd_")]
        w_tr, w_out, ww_done, hot_done, m_done, run_done, done = map(sem, (
            "w_tr", "w_out", "ww_done", "vhot_done", "m_done", "run_done", "sum_steps"))
        NG = SLOTS // GS

        def weigh(engine, ops, i, g):
            engine.wait_ge(loaded[g], 16 * (i + 1))
            engine.wait_ge(m_done, i * V8 + 2 * g + 2)
            ops.tensor_tensor(
                wv[:, g * GS:(g + 1) * GS, 0:D].rearrange("p k (h d) -> p k h d", h=H),
                rows[:, g * GS:(g + 1) * GS].rearrange("p k (h d) -> p k h d", h=H),
                w[:, ts(i * NG + g, GS), 0:H].unsqueeze(3).to_broadcast([P, GS, H, DK]), ALU.mult).then_inc(wv_done[g % 2], 1)

        with nc.Block() as block:
            @block.sync
            def _(sp):
                for t in range(CT):
                    if t >= 2:
                        sp.wait_ge(w_tr, t - 1)
                    sp.dma_start(win[:, t % 2], weights.rearrange("h (t c p) -> t c h p", t=CT, p=P)[t]).then_inc(w_in[t % 2], 16)
                with sp.Fori(0, NI) as i:
                    for g in range(NG):
                        sp.wait_ge(wv_done[g % 2], i * (NG // 2) + g // 2 + 1)
                        o = dr["val"].rearrange("(i k p) d -> i p k d", k=GS, p=P)[ds(i * NG + g, 1)]
                        sp.dma_start(rows[:, g * GS:(g + 1) * GS], o.rearrange("o p k d -> (o p) k d")).then_inc(loaded[g], 16)

            @block.scalar
            def _(act):
                for s in saved:
                    act.sem_inc(s, 16)
                act.wait_ge(w_out, CT)
                with act.Fori(0, NI) as i:
                    for g in range(NG):
                        act.wait_ge(m_done, i * V8 + 2 * g + 2)
                        nc.scalar.copy(wv[:, g * GS:(g + 1) * GS, D:width], w[:, ts(i * NG + g, GS)]).then_inc(ww_done, 1)
                    for g in range(2):
                        act.wait_ge(run_done, i * V8 + 4 * g + 8)
                        o = dr["msg"].rearrange("(i k p) d -> i p k d", k=4, p=P)[ds(i * 2 + g, 1)]
                        act.dma_start(o.rearrange("o p k d -> (o p) k d"), run[:, 4 * g:4 * g + 4]).then_inc(saved[g], 16)
                for s in saved:
                    act.wait_ge(s, 16 * (NI + 1))

            @block.gpsimd
            def _(pool):
                pool.sem_inc(wv_done[1], NG // 2)
                pool.wait_ge(w_out, CT)
                with pool.Fori(0, NI) as i:
                    for g in range(1, NG, 2):
                        weigh(pool, nc.gpsimd, i, g)

            @block.tensor
            def _(pe):
                pe.sem_inc(m_done, V8)
                for t in range(CT):
                    pe.wait_ge(w_in[t % 2], 16 * (t // 2 + 1))
                    if t >= 2:
                        pe.wait_ge(w_out, t - 1)
                    for h in range(nh):
                        ins = nc.tensor.transpose(psW[:, t % 2, h * P:h * P + CW], win[:, t % 2, h], c["ident"][0:CW, 0:CW])
                    ins.then_inc(w_tr, 1)
                with pe.Fori(0, NI) as i:
                    for t in range(V8):
                        if t % 2 == 0:
                            pe.wait_ge(hot_done, i * NG + t // 2 + 1)
                            pe.wait_ge(wv_done[t // 2 % 2], (i + 1) * (NG // 2) + t // 4 + 1)
                            pe.wait_ge(ww_done, i * NG + t // 2 + 1)
                        pe.wait_ge(run_done, i * V8 + t + 1)
                        for j in range(2):
                            ins = nc.tensor.matmul(psM[:, t % 4, 0:width], hot[:, 2 * t + j], wv[:, 2 * t + j], start=(j == 0), stop=(j == 1))
                        ins.then_inc(m_done, 1)

            @block.vector
            def _(dve):
                step = Chain(dve, done)
                dve.sem_inc(wv_done[0], NG // 2)
                for t in range(CT):
                    dve.wait_ge(w_tr, t + 1)
                    nc.vector.tensor_copy(w[:, t * CW:(t + 1) * CW].rearrange("p c h -> p h c"),
                                          psW[:, t % 2].rearrange("p (h c) -> p h c", c=P)[:, 0:nh, 0:CW]).then_inc(w_out, 1)
                dve.sem_inc(run_done, 3)
                nc.vector.memset(run[:], 0.0).then_inc(run_done, 1)
                dve.wait_ge(w_out, CT)

                def add(i, t):
                    V = i * V8 + t
                    dve.wait_ge(m_done, V + 1 + V8)
                    dve.wait_ge(run_done, V + 4)
                    if t % 4 == 0:
                        dve.wait_ge(saved[t // 4], 16 * (i + 1))
                    nc.vector.scalar_tensor_tensor(out=run[:, t, 0:width], in0=run[:, (t - 1) % V8, 0:width], scalar=v["same"][:, ds(V, 1)],
                                                   in1=psM[:, t % 4, 0:width], op0=ALU.mult, op1=ALU.add).then_inc(run_done, 1)
                with dve.Fori(0, NI) as i:
                    for g in range(NG):
                        if g % 2 == 0:
                            weigh(dve, nc.vector, i, g)
                        dve.wait_ge(m_done, i * V8 + 2 * g + 2)
                        nc.vector.tensor_tensor(hot[:, g * GS:(g + 1) * GS], c["iota"][:].unsqueeze(1).to_broadcast([P, GS, P]),
                                                v["dr"][:, ts(i * NG + g, GS)].unsqueeze(2).to_broadcast([P, GS, P]),
                                                ALU.is_equal).then_inc(hot_done, 1)
                        if g:
                            add(i, 2 * g - 2)
                            add(i, 2 * g - 1)
                    add(i, V8 - 2)
                    add(i, V8 - 1)


def fetch_sums(nc, pool, dr, v, acc, sem, width):
    for b in range(NB):
        nc.gpsimd.indirect_dma_start(out=acc[:, b, 0:width], out_offset=None, in_=dr["msg"],
                                     in_offset=bass.IndirectOffsetOnAxis(ap=v["vend"][:, b:b + 1], axis=0)).then_inc(sem, 16)
    pool.wait_ge(sem, 16 * NB)


def flat(ap):
    return ap.rearrange("p o d -> p (o d)")


def update_nodes(nc, c, dr, v, xs, acc, mv, scale, shift, a):
    with Stage(nc) as tmp:
        def sb(name, shape, dt=F32):
            return tmp.enter_context(nc.sbuf_tensor(name, shape, dt))

        def sem(name):
            return tmp.sem(name)
        wa = sb("wa", [P, 2, T, D])
        ba = sb("ba", [T, D])
        gate = sb("gate", [P, T])
        tmb = sb("utmb", [T, P])
        tsc_ = sb("utscale", [P, T, NB])
        inv = sb("uinv", [P, NB])
        al = sb("ual", [P, NB])
        om = sb("uom", [P, NB])
        tmpb = sb("utmp", [P, NB])
        hm = sb("uhm", [P, T, D])
        h = sb("uh", [P, D])
        hk = sb("uhk", [P, D])
        hT = sb("uhT", [P, T * 2, P])
        psT = tmp.enter_context(nc.psum_tensor("upsT", [P, 2, 512], F32))
        psO = tmp.enter_context(nc.psum_tensor("upsO", [P, 2, 512], F32))
        w_in, fetched, pre, hm_done, tr_done, hT_done, o_done, o_out, tm_in, h_done, hk_done, gt, pe_done = map(sem, (
            "u_w_in", "u_fetched", "u_pre", "u_hm", "u_tr", "u_hT", "u_o", "u_oo", "u_tm", "u_h", "u_hk", "u_gate", "u_pe"))
        with nc.Block() as block:
            @block.gpsimd
            def _(pool):
                fetch_sums(nc, pool, dr, v, acc, fetched, MSG)

            @block.sync
            def _(sp):
                for t in range(T):
                    sp.dma_start(wa[:, :, t], a['L0_gnn_Wa'][t].rearrange("(g p) d -> p g d", p=P)).then_inc(w_in, 16)
                sp.dma_start(ba[:], a['L0_gnn_ba']).then_inc(w_in, 16)
                sp.dma_start(gate[:], a['L0_gnn_skip'].rearrange("(o t) -> o t", o=1).to_broadcast([P, T])).then_inc(w_in, 16)
                with sp.Fori(0, NB) as b:
                    sp.wait_ge(o_done, b + 1)
                    sp.dma_start(tmb[:], dr["typerow"][:, ts(b, P)]).then_inc(tm_in, 16)

            @block.scalar
            def _(act):
                act.wait_ge(w_in, 16 * (T + 2))
                nc.scalar.activation(gate[:], gate[:], ACT.Exp, scale=-1.0).then_inc(gt, 1)
                act.wait_ge(pre, 1)
                with act.Fori(0, NB) as b:
                    act.wait_ge(tr_done, b + 1)
                    for t in range(T):
                        nc.scalar.activation(hm[:, t], flat(acc[:, ds(b, 1), 0:D]), ACT.Copy, scale=tsc_[:, t, ds(b, 1)]).then_inc(hm_done, 1)
                    act.wait_ge(hk_done, b + 1)
                    nc.scalar.activation(h[:], flat(xs[:, ds(b, 1)]), ACT.Relu, bias=shift[:, ds(b, 1)], scale=scale[:, ds(b, 1)]).then_inc(h_done, 1)

            @block.vector
            def _(dve):
                step = Chain(dve, sem("u_steps"))
                tt, tsc = nc.vector.tensor_tensor, nc.vector.tensor_scalar
                dve.sem_inc(hk_done, 1)
                dve.sem_inc(hT_done, 2)
                dve.sem_inc(o_out, 1)
                dve.wait_ge(gt, 1)
                step(tsc(gate[:], gate[:], 1.0, None, ALU.add))
                step(nc.vector.reciprocal(gate[:], gate[:]))
                step(nc.vector.memset(al[:], 0.0))
                for t in range(T):
                    step(tsc(tmpb[:], v["types"][:, :, t], gate[:, t:t + 1], None, ALU.mult))
                    step(tt(al[:], al[:], tmpb[:], ALU.add))
                step(tsc(om[:], al[:], -1.0, 1.0, ALU.mult, ALU.add))
                dve.wait_ge(fetched, 16 * NB)
                step(tsc(tmpb[:], acc[:, :, D], 1.0, None, ALU.max))
                step(nc.vector.reciprocal(inv[:], tmpb[:]))
                for t in range(T):
                    ins = tt(tsc_[:, t], inv[:], v["types"][:, :, t], ALU.mult)
                    if t < T - 1:
                        step(ins)
                ins.then_inc(pre, 1)
                with dve.Fori(0, NB) as b:
                    dve.wait_ge(tr_done, b + 2)
                    dve.wait_ge(o_done, b + 1)
                    nc.vector.tensor_copy(hT[:, 0:4].rearrange("p n q -> p (n q)"), psT[:, 0, :]).then_inc(hT_done, 1)
                    nc.vector.tensor_copy(hT[:, 4:6].rearrange("p n q -> p (n q)"), psT[:, 1, 0:2 * P]).then_inc(hT_done, 1)
                    dve.wait_ge(h_done, b + 1)
                    dve.wait_ge(o_out, b + 1)
                    tsc(hk[:], h[:], om[:, ds(b, 1)], None, ALU.mult).then_inc(hk_done, 1)
                    dve.wait_ge(hk_done, b + 2)
                    dve.wait_ge(o_done, b + 2)
                    nc.vector.scalar_tensor_tensor(out=flat(acc[:, ds(b, 1), 0:D]), in0=psO[:, 0, 0:D], scalar=al[:, ds(b, 1)], in1=hk[:],
                                                   op0=ALU.mult, op1=ALU.add).then_inc(o_out, 1)

            @block.tensor
            def _(pe):
                pe.sem_inc(tr_done, 1)
                pe.sem_inc(o_done, 1)
                pe.wait_ge(w_in, 16 * (T + 2))
                with pe.Fori(0, NB) as b:
                    pe.wait_ge(hm_done, 3 * (b + 1))
                    pe.wait_ge(hT_done, 2 * b + 2)
                    for n in range(6):
                        t, g = n // 2, n % 2
                        ins = nc.tensor.transpose(psT[:, n // 4, n % 4 * P:(n % 4 + 1) * P], hm[:, t, g * P:(g + 1) * P], c["ident"][:])
                    ins.then_inc(tr_done, 1)
                    pe.wait_ge(hT_done, 2 * b + 4)
                    pe.wait_ge(tm_in, 16 * (b + 1))
                    pe.wait_ge(o_out, b + 1)
                    for t in range(T):
                        for g in range(2):
                            nc.tensor.matmul(psO[:, 0, 0:D], hT[:, 2 * t + g], wa[:, g, t], start=(t == 0 and g == 0), stop=False)
                    nc.tensor.matmul(psO[:, 0, 0:D], tmb[:], ba[:], start=False, stop=True).then_inc(o_done, 1)


def normalise_nodes(nc, c, dr, v, xs, acc, scale, shift, scale2, shift2, a):
    with Stage(nc) as tmp:
        def sb(name, shape, dt=F32):
            return tmp.enter_context(nc.sbuf_tensor(name, shape, dt))

        def sem(name):
            return tmp.sem(name)
        gb = sb("ngb", [T, 2 * D])
        tmb = sb("ntmb", [T, 2, P])
        has = sb("nhas", [P, NB])
        h = sb("nh", [P, D])
        n_ = sb("nn", [P, D])
        psG = tmp.enter_context(nc.psum_tensor("npsG", [P, 512], F32))
        w_in, tm_in, g_done, h_done, x_done, st, ready = map(sem, ("n_w_in", "n_tm", "n_g", "n_h", "n_x", "n_st", "n_ready"))
        with nc.Block() as block:
            @block.sync
            def _(sp):
                sp.dma_start(gb[:, 0:D], a['L0_gnn_ln_g']).then_inc(w_in, 16)
                sp.dma_start(gb[:, D:2 * D], a['L0_gnn_ln_b']).then_inc(w_in, 16)
                with sp.Fori(0, NB) as b:
                    sp.wait_ge(g_done, b + 1)
                    sp.dma_start(tmb[:, 0], dr["typerow"][:, ts(b, P)]).then_inc(tm_in, 16)

            @block.scalar
            def _(act):
                with act.Fori(0, NB) as b:
                    act.wait_ge(x_done, b + 1)
                    nc.scalar.activation(h[:], flat(xs[:, ds(b, 1)]), ACT.Relu, bias=shift[:, ds(b, 1)], scale=scale[:, ds(b, 1)]).then_inc(h_done, 1)

            @block.tensor
            def _(pe):
                pe.sem_inc(g_done, 1)
                pe.wait_ge(w_in, 32)
                with pe.Fori(0, NB) as b:
                    pe.wait_ge(tm_in, 16 * (b + 1))
                    pe.wait_ge(x_done, b + 1)
                    nc.tensor.matmul(psG[:], tmb[:, 0], gb[:], start=True, stop=True).then_inc(g_done, 1)

            @block.vector
            def _(dve):
                nc.vector.tensor_scalar(has[:], acc[:, :, D], 0.5, None, ALU.is_gt).then_inc(x_done, 1)
                with dve.Fori(0, NB) as b:
                    def step(ins, n):
                        ins.then_inc(st, 1)
                        dve.wait_ge(st, b * 5 + n)
                    dve.wait_ge(x_done, b + 1)
                    step(nc.vector.tensor_scalar(n_[:], flat(acc[:, ds(b, 1), 0:D]), scale2[:, ds(b, 1)], shift2[:, ds(b, 1)], ALU.mult, ALU.add), 1)
                    dve.wait_ge(g_done, b + 2)
                    step(nc.vector.tensor_tensor(n_[:], n_[:], psG[:, 0:D], ALU.mult), 2)
                    step(nc.vector.tensor_tensor(n_[:], n_[:], psG[:, D:2 * D], ALU.add), 3)
                    dve.wait_ge(h_done, b + 1)
                    step(nc.vector.tensor_tensor(n_[:], n_[:], h[:], ALU.subtract), 4)
                    step(nc.vector.scalar_tensor_tensor(out=n_[:], in0=n_[:], scalar=has[:, ds(b, 1)], in1=h[:], op0=ALU.mult, op1=ALU.add), 5)
                    nc.vector.tensor_tensor(flat(xs[:, ds(b, 1)]), flat(xs[:, ds(b, 1)]), n_[:], ALU.add).then_inc(x_done, 1)


def project_layer1(nc, c, dr, xs, node, scale, shift, a):
    with Stage(nc) as tmp:
        def sb(name, shape, dt=F32):
            return tmp.enter_context(nc.sbuf_tensor(name, shape, dt))

        def sem(name):
            return tmp.sem(name)
        w = sb("wlin", [P, 2, D + 2 * H])
        wT = sb("w1T", [P, 2, D])
        am = sb("attm", [P, 2, 2 * H])
        h = sb("ph", [P, D])
        hT = sb("phT", [P, 2, P])
        out = sb("pout", [P, D + 2 * H])
        psT = tmp.enter_context(nc.psum_tensor("ppsT", [P, 512], F32))
        psW = tmp.enter_context(nc.psum_tensor("ppsW", [P, 2, 512], F32))
        psO = tmp.enter_context(nc.psum_tensor("ppsO", [P, 512], F32))
        z, w_in, wt, wt_out, wa, wa_out, h_done, tr, hT_done, o_done, o_out, kept, x_done = map(sem, (
            "p_z", "p_w_in", "p_wt", "p_wto", "p_wa", "p_wao", "p_h", "p_tr", "p_hT", "p_o", "p_oo", "p_kept", "p_x"))
        e_done = sem("p_e")
        with nc.Block() as block:
            @block.sync
            def _(sp):
                sp.dma_start(w[:, :, 0:D], a['L1_gnn_W'].rearrange("(g p) d -> p g d", p=P)).then_inc(w_in, 16)
                sp.wait_ge(z, 1)
                for n, t in enumerate((a['L1_gnn_att_src'], a['L1_gnn_att_dst'])):
                    for hd in range(H):
                        u = hd % 2
                        sp.dma_start(am[u * DK:(u + 1) * DK, hd // 2, n * H + hd:n * H + hd + 1], t[hd].rearrange("(d o) -> d o", o=1)).then_inc(w_in, 16)
                sp.sem_inc(kept, 16)
                with sp.Fori(0, NB) as b:
                    sp.wait_ge(o_out, b + 2)
                    sp.dma_start(dr["x1t"][ts(b, P), :], out[:, 0:ROW1]).then_inc(kept, 16)
                sp.wait_ge(kept, 16 * (NB + 1))

            @block.gpsimd
            def _(pool):
                nc.gpsimd.memset(am[:], 0.0).then_inc(z, 1)
                with pool.Fori(0, NB) as b:
                    pool.wait_ge(h_done, b + 1)
                    nc.gpsimd.tensor_tensor(flat(xs[:, ds(b, 1)]), flat(xs[:, ds(b, 1)]), h[:], ALU.add).then_inc(x_done, 1)

            @block.scalar
            def _(act):
                with act.Fori(0, NB) as b:
                    act.wait_ge(tr, b + 1)
                    act.wait_ge(x_done, b)
                    nc.scalar.activation(h[:], flat(xs[:, ds(b, 1)]), ACT.Relu, bias=shift[:, ds(b, 1)], scale=scale[:, ds(b, 1)]).then_inc(h_done, 1)
                    act.wait_ge(tr, b + 2)
                    act.wait_ge(o_done, b + 1)
                    nc.scalar.copy(hT[:].rearrange("p n q -> p (n q)"), psT[:, 0:2 * P]).then_inc(hT_done, 1)

            @block.vector
            def _(dve):
                dve.sem_inc(o_out, 1)
                for g in range(2):
                    dve.wait_ge(wt, g + 1)
                    nc.vector.tensor_copy(wT[:, g], psW[:, g, 0:D]).then_inc(wt_out, 1)
                dve.wait_ge(wa, 1)
                nc.vector.tensor_copy(w[:, :, D:D + 2 * H], psT[:, 0:4 * H].rearrange("p (g n) -> p g n", g=2)).then_inc(wa_out, 1)
                with dve.Fori(0, NB) as b:
                    dve.wait_ge(o_done, b + 2)
                    dve.wait_ge(kept, 16 * (b + 1))
                    nc.vector.tensor_copy(node[:, ds(b, 1), 0:H].rearrange("p o h -> p (o h)"), psO[:, D + H:D + 2 * H]).then_inc(e_done, 1)
                    nc.vector.tensor_copy(node[:, ds(b, 1), H:2 * H].rearrange("p o h -> p (o h)"), psO[:, D:D + H]).then_inc(e_done, 1)
                    nc.vector.tensor_copy(out[:], psO[:, 0:D + 2 * H]).then_inc(o_out, 1)
                step = Chain(dve, sem("p_steps"))
                dve.wait_ge(e_done, 2 * NB)
                step(nc.vector.tensor_tensor(node[:, :, H:2 * H], node[:, :, 0:H], node[:, :, H:2 * H], ALU.add))
                step(nc.vector.scalar_tensor_tensor(out=node[:, :, H:2 * H], in0=node[:, :, H:2 * H], scalar=SLOPE, in1=node[:, :, H:2 * H],
                                                    op0=ALU.mult, op1=ALU.max))

            @block.tensor
            def _(pe):
                pe.wait_ge(w_in, 16 * 9)
                for g in range(2):
                    for u in range(2):
                        ins = nc.tensor.transpose(psW[:, g, u * P:(u + 1) * P], w[:, u, g * P:(g + 1) * P], c["ident"][:])
                    ins.then_inc(wt, 1)
                pe.wait_ge(wt_out, 2)
                for u in range(2):
                    for g in range(2):
                        ins = nc.tensor.matmul(psT[:, u * 2 * H:(u + 1) * 2 * H], wT[:, g, u * P:(u + 1) * P], am[:, g], start=(g == 0), stop=(g == 1))
                ins.then_inc(wa, 1)
                pe.sem_inc(tr, 1)
                pe.sem_inc(o_done, 1)
                pe.wait_ge(wa_out, 1)
                with pe.Fori(0, NB) as b:
                    pe.wait_ge(h_done, b + 1)
                    pe.wait_ge(hT_done, b)
                    for g in range(2):
                        ins = nc.tensor.transpose(psT[:, g * P:(g + 1) * P], h[:, g * P:(g + 1) * P], c["ident"][:])
                    ins.then_inc(tr, 1)
                    pe.wait_ge(hT_done, b + 1)
                    pe.wait_ge(o_out, b + 1)
                    for g in range(2):
                        ins = nc.tensor.matmul(psO[:, 0:D + 2 * H], hT[:, g], w[:, g], start=(g == 0), stop=(g == 1))
                    ins.then_inc(o_done, 1)


def finish(nc, c, dr, v, xs, node, a, out):
    with Stage(nc) as tmp:
        def sb(name, shape, dt=F32):
            return tmp.enter_context(nc.sbuf_tensor(name, shape, dt))

        def sem(name):
            return tmp.sem(name)
        acc = sb("facc", [P, NB, MSG])
        xw = sb("fxw", [P, 2, D])
        zero = sb("fzero", [P, NB, H])
        den = sb("fden", [P, NB, H])
        vec = sb("fvec", [P, 3, D])
        t1 = sb("ft1", [P, D])
        mean = sb("fmean", [P, D])
        g_ = sb("fg", [P, D])
        sq = sb("fsq", [P, 2, D])
        pos = sb("fpos", [P, 2, D])
        ex = sb("fex", [P, 2, D])
        psS = tmp.enter_context(nc.psum_tensor("psS", [P, 2, 512], F32))
        fetched, w_in, x_in, pre, f_done, s_done, m_done, d_done, q_done, v_done, y_done, e_done, o_done, st, st2, st3 = map(sem, (
            "f_fetched", "f_w_in", "f_x_in", "f_pre", "f_done", "f_s", "f_m", "f_d", "f_q", "f_v", "f_y", "f_e", "f_o", "f_st", "f_st2", "f_st3"))
        saved = sem("f_saved")
        x_used = sem("f_x_used")
        last = c["ones"][0:NLAST]
        with nc.Block() as block:
            @block.gpsimd
            def _(pool):
                fetch_sums(nc, pool, dr, v, acc, fetched, MSG)

            @block.sync
            def _(sp):
                for n, t in enumerate((a['L1_gnn_bias'], a['L1_gnn_gamma'], a['L1_gnn_beta'])):
                    sp.dma_start(vec[:, n], t.rearrange("(o d) -> o d", o=1).to_broadcast([P, D])).then_inc(w_in, 16)
                with sp.Fori(0, NB) as b:
                    sp.wait_ge(x_used, b + 1)
                    sp.dma_start(xw[:, 0], dr["x1t"][ts(b, P), 0:D]).then_inc(x_in, 16)
                with sp.Fori(0, NB - 1) as b:
                    sp.wait_ge(o_done, b + 1)
                    sp.dma_start(out[ts(b, P), :], flat(xs[:, ds(b, 1)])).then_inc(saved, 16)
                sp.wait_ge(o_done, NB)
                sp.dma_start(out[(NB - 1) * P:N, :], xs[0:NLAST, NB - 1]).then_inc(saved, 16)
                sp.wait_ge(saved, 16 * NB)

            @block.scalar
            def _(act):
                with act.Fori(0, NB) as b:
                    act.wait_ge(d_done, b + 1)
                    act.wait_ge(v_done, b + 1)
                    nc.scalar.activation(sq[:, 0], flat(acc[:, ds(b, 1), 0:D]), ACT.Square).then_inc(q_done, 1)
                act.wait_ge(st2, 1)
                nc.scalar.activation(g_[:], g_[:], ACT.Sqrt, bias=c["eps"][:, 0:1]).then_inc(st3, 1)
                with act.Fori(0, NB) as b:
                    act.wait_ge(y_done, b + 1)
                    act.wait_ge(o_done, b)
                    nc.scalar.activation(ex[:, 0], pos[:, 1], ACT.Exp).then_inc(e_done, 1)

            @block.tensor
            def _(pe):
                def column_sum(bank, source, ready, done, finished):
                    def add(b, start, rows):
                        pe.wait_ge(ready, b + 1)
                        ins = nc.tensor.matmul(psS[:, bank, 0:D], c["ones"][0:rows], source(b, rows), start=start, stop=False,
                                               skip_group_check=True)
                        ins.then_inc(done, 1)
                    add(0, True, P)
                    with pe.Fori(1, NB - 1) as b:
                        add(b, False, P)
                    pe.wait_ge(ready, NB)
                    nc.tensor.matmul(psS[:, bank, 0:D], c["ones"][0:NLAST], source(NB - 1, NLAST), start=False, stop=True,
                                     skip_group_check=True).then_inc(finished, 1)
                pe.sem_inc(v_done, 1)
                column_sum(0, lambda b, n: acc[0:n, ds(b, 1), 0:D].rearrange("p o d -> p (o d)"), f_done, s_done, m_done)
                column_sum(1, lambda b, n: sq[0:n, 0], q_done, v_done, m_done)

            @block.vector
            def _(dve):
                step = Chain(dve, st)
                tt, tsc, stt = nc.vector.tensor_tensor, nc.vector.tensor_scalar, nc.vector.scalar_tensor_tensor
                dve.sem_inc(x_used, 1)
                dve.wait_ge(fetched, 16 * NB)
                dve.wait_ge(w_in, 48)
                step(tsc(zero[:], acc[:, :, D:D + H], 0.5, None, ALU.is_lt))
                step(tt(acc[:, :, D + H:MSG], acc[:, :, D + H:MSG], zero[:], ALU.add))
                step(tt(den[:], acc[:, :, D:D + H], acc[:, :, D + H:MSG], ALU.add))
                step(nc.vector.reciprocal(den[:], den[:]))
                step(tt(zero[:], acc[:, :, D + H:MSG], den[:], ALU.mult))

                def heads(ap):
                    return ap.rearrange("p (h d) -> p h d", h=H)

                def of_head(ap, b):
                    return ap[:, ds(b, 1)].rearrange("p o h -> p (o h)").unsqueeze(2).to_broadcast([P, H, DK])
                with dve.Fori(0, NB) as b:
                    def stp(ins, n):
                        ins.then_inc(pre, 1)
                        dve.wait_ge(pre, b * 3 + n)
                    rows = flat(acc[:, ds(b, 1), 0:D])
                    dve.wait_ge(x_in, 16 * (b + 1))
                    stp(tt(heads(t1[:]), heads(xw[:, 0]), of_head(zero, b), ALU.mult), 1)
                    dve.sem_inc(x_used, 1)
                    stp(tt(heads(rows), heads(rows), of_head(den, b), ALU.mult), 2)
                    stp(tt(rows, rows, t1[:], ALU.add), 3)
                    tt(rows, rows, vec[:, 0], ALU.add).then_inc(f_done, 1)
                dve.wait_ge(m_done, 1)
                step(tsc(mean[:], psS[:, 0, 0:D], 1.0 / N, None, ALU.mult))
                dve.wait_ge(f_done, NB)
                with dve.Fori(0, NB) as b:
                    rows = flat(acc[:, ds(b, 1), 0:D])
                    tt(rows, rows, mean[:], ALU.subtract).then_inc(d_done, 1)
                dve.wait_ge(m_done, 2)
                tsc(g_[:], psS[:, 1, 0:D], 1.0 / N, None, ALU.mult).then_inc(st2, 1)
                dve.wait_ge(st3, 1)
                step(nc.vector.reciprocal(g_[:], g_[:]))
                step(tt(g_[:], g_[:], vec[:, 1], ALU.mult))
                dve.wait_ge(d_done, NB)
                with dve.Fori(0, NB) as b:
                    def stq(ins, n):
                        ins.then_inc(x_used, 1)
                        dve.wait_ge(x_used, b * 3 + n + NB + 1)
                    rows = flat(acc[:, ds(b, 1), 0:D])
                    stq(tt(rows, rows, g_[:], ALU.mult), 1)
                    stq(tt(pos[:, 0], rows, vec[:, 2], ALU.add), 2)
                    dve.wait_ge(e_done, b)
                    tsc(pos[:, 1], pos[:, 0], 0.0, None, ALU.min).then_inc(y_done, 1)
                    dve.wait_ge(e_done, b + 1)
                    stq(stt(out=t1[:], in0=pos[:, 0], scalar=0.0, in1=ex[:, 0], op0=ALU.max, op1=ALU.add), 3)
                    x_ = flat(xs[:, ds(b, 1)])
                    stt(out=x_, in0=t1[:], scalar=-1.0, in1=x_, op0=ALU.add, op1=ALU.add).then_inc(o_done, 1)
                    dve.wait_ge(o_done, b + 1)


_INS = ['x', 'src', 'dst', 'edge_type_6', 'node_type_3', 'L0_gnn_Wk', 'L0_gnn_bk', 'L0_gnn_Wq', 'L0_gnn_bq',
        'L0_gnn_Wv', 'L0_gnn_bv', 'L0_gnn_Wa', 'L0_gnn_ba', 'L0_gnn_rel_pri', 'L0_gnn_rel_att', 'L0_gnn_rel_msg',
        'L0_gnn_skip', 'L0_gnn_ln_g', 'L0_gnn_ln_b', 'L1_gnn_W', 'L1_gnn_att_src', 'L1_gnn_att_dst', 'L1_gnn_bias',
        'L1_gnn_gamma', 'L1_gnn_beta']


def program(nc, out, a):
    with ExitStack() as ctx:
        def sb(name, shape, dt=F32):
            return ctx.enter_context(nc.sbuf_tensor(name, shape, dt))
        c = consts(nc, ctx)
        dr = scratch(nc)
        v = prepare_edges(nc, ctx, c, dr, a['src'], a['dst'], a['edge_type_6'], a['node_type_3'])
        xs = sb("xs", [P, NB, D])
        mv = sb("mv", [P, NB, 2])
        scale = sb("scale", [P, NB])
        shift = sb("shift", [P, NB])
        clear = ctx.enter_context(nc.semaphore("clear"))
        with nc.Block() as block:
            @block.vector
            def _(dve):
                nc.vector.memset(xs[:, NB - 1], 0.0).then_inc(clear, 1)
                dve.wait_ge(clear, 1)
        node_stats(nc, c, "x", xs, mv, scale, shift, a['x'])
        with nc.sbuf_tensor("qs", [P, NB, D], F32) as qs:
            project(nc, c, dr, v, xs, qs, scale, shift, a)
            edge_scores(nc, c, dr, v, 0, dr["kv"], v["kvi"], qs, 2 * D)
        softmax_by_relation(nc, c, dr)
        sum_messages(nc, c, dr, v, 0, dr["w0"], H)
        scale2 = sb("scale2", [P, NB])
        shift2 = sb("shift2", [P, NB])
        with nc.sbuf_tensor("acc", [P, NB, MSG], F32) as acc:
            update_nodes(nc, c, dr, v, xs, acc, mv, scale, shift, a)
            node_stats(nc, c, "out", acc, mv, scale2, shift2)
            normalise_nodes(nc, c, dr, v, xs, acc, scale, shift, scale2, shift2, a)
        node_stats(nc, c, "x1", xs, mv, scale, shift)
        node = sb("node", [P, NB, 2 * H])
        project_layer1(nc, c, dr, xs, node, scale, shift, a)
        edge_scores(nc, c, dr, v, 1, dr["x1t"], v["srci"], node, ROW1)
        softmax_weights(nc, c, dr)
        sum_messages(nc, c, dr, v, 1, dr["w1"], 2 * H)
        finish(nc, c, dr, v, xs, node, a, out)


def kernel(**inputs):
    import numpy as np
    import concourse.bacc as bacc
    from concourse.bass_utils import run_bass_kernel_spmd

    nc = bacc.Bacc("TRN2", target_bir_lowering=False, num_devices=1)
    arrays, args = {}, {}
    for name in _INS:
        a = np.ascontiguousarray(inputs[name])
        arrays[f"in_{name}"] = a
        args[name] = nc.dram_tensor(f"in_{name}", a.shape, mybir.dt.from_np(a.dtype), kind="ExternalInput").ap()
    out = nc.dram_tensor("out_0", (N, D), F32, kind="ExternalOutput").ap()
    program(nc, out, args)
    r = run_bass_kernel_spmd(nc, [arrays], core_ids=[0])
    return r.results[0]["out_0"]
```

```python
from contextlib import ExitStack

import concourse.bass as bass
from concourse import mybir
from concourse.alu_op_type import AluOpType as ALU

P = 128
N, D, H, DK, R, T = 6250, 256, 4, 64, 6, 3
E = 100000
NB = -(-N // P)
NP = NB * P
NLAST = N - (NB - 1) * P
SUP = 2 * P
NS = 392
EP = NS * SUP
PADDST = NP - 1
NV = NS + NB - 1
VT = 4
NT = NV // VT
NC = 2 * NV
LV = NV * SUP
GR = P // H
SL = LV // GR
CT = 8
CW = NC // CT
ROW1 = D + H
MSG = D + 2 * H
BIG = 1e30
EPS = 1e-5
SLOPE = 0.2
assert NV % VT == 0 and LV % GR == 0 and NC % CT == 0 and EP >= E + 1 and NS % 4 == 0

F32, BF16, I32, I16 = mybir.dt.float32, mybir.dt.bfloat16, mybir.dt.int32, mybir.dt.int16
ACT = mybir.ActivationFunctionType
AX = mybir.AxisListType
ds, ts = bass.ds, bass.ts

F_DST, F_KV, F_SRC, F_REL, F_FIRST, F_LAST, NF = 0, 1, 2, 3, 4, 5, 6


class Chain:

    def __init__(self, engine, sem):
        self.engine, self.sem, self.n = engine, sem, 0

    def __call__(self, ins):
        ins.then_inc(self.sem, 1)
        self.n += 1
        self.engine.wait_ge(self.sem, self.n)


class Stage(ExitStack):

    def __init__(self, nc):
        super().__init__()
        self.nc, self.sems = nc, []

    def sem(self, name):
        self.sems.append(self.nc.alloc_semaphore(name))
        return self.sems[-1]

    def __exit__(self, *e):
        if e[0] is None:
            self.nc.clear_and_free_semaphores(self.sems)
            with self.nc.Block():
                pass
        return super().__exit__(*e)


def scratch(nc):
    def d(name, shape, dt=F32):
        return nc.dram_tensor(name, shape, dt, kind="Internal").ap()
    return dict(
        dst_o=d("dst_o", (E, 1), I32), src_o=d("src_o", (E, 1), I32), rel_o=d("rel_o", (E, 1), I32),
        rec=d("rec", (NS, NF * SUP)),
        typerow=d("typerow", (T, NP)),
        kv=d("kv", (NP * R, 2 * D)),
        rel=d("rel_v", (LV,), BF16), first=d("first_v", (LV,), BF16), last=d("last_v", (LV,), BF16),
        att=d("att_v", (H, LV)), self_=d("self_v", (H, LV)),
        w0=d("w0_v", (H, LV)), w1=d("w1_v", (2 * H, LV)),
        val=d("val_v", (NC * P, D)),
        x1t=d("x1t", (NP, ROW1)),
    )


def consts(nc, ctx):
    def sb(name, shape, dt=F32):
        return ctx.enter_context(nc.sbuf_tensor(name, shape, dt))
    c = dict(ident=sb("ident", [P, P]), identb=sb("identb", [P, P], BF16), ones=sb("ones", [P, P]),
             iota=sb("iota", [P, P]), piota=sb("piota", [P, 1]), npiota=sb("npiota", [P, 1]),
             one=sb("one", [P, 1]), pint=sb("pint", [P, 1], I32), eps=sb("eps", [P, 1]),
             nbeg=sb("nbeg", [P, NB]))
    sem = nc.alloc_semaphore("const_done")
    with nc.Block() as block:
        @block.gpsimd
        def _(pool):
            done = Chain(pool, sem)
            done(nc.gpsimd.memset(c["ones"][:], 1.0))
            done(nc.gpsimd.memset(c["one"][:], 1.0))
            done(nc.gpsimd.memset(c["eps"][:], EPS))
            done(nc.gpsimd.iota(c["iota"][:], [[1, P]], base=0, channel_multiplier=0,
                                allow_small_or_imprecise_dtypes=True))
            done(nc.gpsimd.iota(c["piota"][:], [[0, 1]], base=0, channel_multiplier=1,
                                allow_small_or_imprecise_dtypes=True))
            done(nc.gpsimd.iota(c["npiota"][:], [[0, 1]], base=0, channel_multiplier=-1,
                                allow_small_or_imprecise_dtypes=True))
            done(nc.gpsimd.iota(c["pint"][:], [[0, 1]], base=0, channel_multiplier=1))
            done(nc.gpsimd.iota(c["nbeg"][:], [[P, NB]], base=0, channel_multiplier=0,
                                allow_small_or_imprecise_dtypes=True))
            done(nc.gpsimd.affine_select(out=c["ident"][:], in_=c["ones"][:], compare_op=ALU.is_equal, fill=0.0,
                                         base=0, pattern=[[-1, P]], channel_multiplier=1))
            done(nc.gpsimd.tensor_copy(c["identb"][:], c["ident"][:]))
    return c


def order_edges(nc, c, dr, src, dst, etype):
    EQ, EC = 125, E // 125
    PC = E // 16
    G = 8
    fields = (("dst_o", dst), ("src_o", src), ("rel_o", etype))
    with Stage(nc) as tmp:
        def sb(name, shape, dt=F32):
            return tmp.enter_context(nc.sbuf_tensor(name, shape, dt))
        cur = sb("o_cur", [EQ, 3, EC], I32)
        flag = sb("o_flag", [1, 1], I32)
        with Stage(nc) as chk:
            nxt = chk.enter_context(nc.sbuf_tensor("o_next", [EQ, EC], I32))
            down = chk.enter_context(nc.sbuf_tensor("o_down", [EQ, EC], F32))
            total = chk.enter_context(nc.sbuf_tensor("o_total", [EQ, 1], F32))
            ps = chk.enter_context(nc.psum_tensor("o_ps", [P, 512], F32))
            s_z, s_in, s_cp, s_t, s_p, s_st = (chk.sem(n) for n in ("o_z", "o_in", "o_cp", "o_t", "o_p", "o_st"))
            with nc.Block() as block:
                @block.gpsimd
                def _(pool):
                    nc.gpsimd.memset(nxt[:], N).then_inc(s_z, 1)

                @block.sync
                def _(sp):
                    for n, (_, a) in enumerate(fields):
                        sp.dma_start(cur[:, n], a.rearrange("(p k) -> p k", p=EQ)).then_inc(s_in, 16)
                    sp.wait_ge(s_z, 1)
                    sp.dma_start(nxt[0:EQ - 1], dst[1:E - EC + 1].rearrange("(p k) -> p k", k=EC)).then_inc(s_in, 16)
                    sp.dma_start(nxt[EQ - 1:EQ, 0:EC - 1], dst[E - EC + 1:E].rearrange("(p k) -> p k", p=1)).then_inc(s_in, 16)
                    for name, a in fields:
                        sp.dma_start(dr[name].rearrange("(p k) o -> p (k o)", p=EQ), a.rearrange("(p k) -> p k", p=EQ)).then_inc(s_cp, 16)
                    sp.wait_ge(s_cp, 48)

                @block.vector
                def _(dve):
                    step = Chain(dve, s_st)
                    dve.wait_ge(s_in, 80)
                    step(nc.vector.tensor_tensor(down[:], nxt[:], cur[:, 0], ALU.is_lt))
                    nc.vector.tensor_reduce(total[:], down[:], AX.X, ALU.add).then_inc(s_t, 1)
                    dve.wait_ge(s_p, 1)
                    step(nc.vector.tensor_scalar(flag[:], ps[0:1, 0:1], 1.0, None, ALU.min))

                @block.tensor
                def _(pe):
                    pe.wait_ge(s_t, 1)
                    nc.tensor.matmul(ps[0:1, 0:1], total[:], c["ones"][0:EQ, 0:1], start=True, stop=True).then_inc(s_p, 1)
        unordered = nc.values_load(flag[0:1, 0:1], min_val=0, max_val=1)
        with nc.If(unordered > 0):
            rank_edges(nc, dr, dst, fields, cur, EQ, EC, PC, G, tmp)


def rank_edges(nc, dr, dst, fields, cur, EQ, EC, PC, G, tmp):
    def sb(name, shape, dt=F32):
        return tmp.enter_context(nc.sbuf_tensor(name, shape, dt))
    key = sb("o_key", [EQ, EC])
    own = sb("o_own", [EQ, EC])
    rank = sb("o_rank", [EQ, EC])
    low = sb("o_low", [EQ, EC])
    tie = sb("o_tie", [EQ, EC])
    ranki = sb("o_ranki", [EQ, EC], I32)
    piece = sb("o_piece", [EQ, PC], I32)
    pf = sb("o_pf", [EQ, PC])
    fidx = sb("o_fidx", [EQ, PC])
    junk = sb("o_junk", [EQ, PC])
    before = sb("o_before", [EQ, PC])
    ids = sb("o_ids", [EQ, G], I32)
    vals = sb("o_vals", [EQ, 3, G], I32)
    s_init, s_in, s_free, s_conv, s_st, s_a, s_b, s_c, s_d, s_rank, s_ids, s_put, s_go = map(tmp.sem, (
        "o_init", "o_piece_in", "o_free", "o_converted", "o_steps", "o_a", "o_b", "o_c", "o_d", "o_rank", "o_ids", "o_put", "o_go"))
    with nc.Block() as block:
        @block.sync
        def _(sp):
            with sp.Fori(0, E // PC) as q:
                sp.wait_ge(s_free, q + 1)
                sp.dma_start(piece[:], dst[ts(q, PC)].rearrange("(o f) -> o f", o=1).to_broadcast([EQ, PC])).then_inc(s_in, 16)

        @block.vector
        def _(dve):
            step = Chain(dve, s_st)
            tt, tsc = nc.vector.tensor_tensor, nc.vector.tensor_scalar
            dve.wait_ge(s_init, 3)
            step(nc.vector.tensor_copy(key[:], cur[:, 0]))
            dve.sem_inc(s_free, 1)
            with dve.Fori(0, E // PC) as q:
                dve.wait_ge(s_in, 16 * (q + 1))
                nc.vector.tensor_copy(pf[:], piece[:]).then_inc(s_free, 1)
                dve.wait_ge(s_free, q + 2)
                dve.sem_inc(s_conv, 1)
                with dve.Fori(0, EC) as k:
                    n = q * EC + k + 1
                    mine = key[:, ds(k, 1)]
                    tsc(junk[:], pf[:], mine, None, ALU.is_lt).then_inc(s_a, 1)
                    dve.wait_ge(s_a, n)
                    nc.vector.tensor_reduce(low[:, ds(k, 1)], junk[:], AX.X, ALU.add).then_inc(s_b, 1)
                    tsc(before[:], fidx[:], own[:, ds(k, 1)], None, ALU.is_lt).then_inc(s_c, 1)
                    dve.wait_ge(s_c, 2 * n - 1)
                    dve.wait_ge(s_b, n)
                    nc.vector.scalar_tensor_tensor(out=junk[:], in0=pf[:], scalar=mine, in1=before[:], op0=ALU.is_equal, op1=ALU.mult).then_inc(s_c, 1)
                    dve.wait_ge(s_c, 2 * n)
                    nc.vector.tensor_reduce(tie[:, ds(k, 1)], junk[:], AX.X, ALU.add).then_inc(s_d, 1)
                    dve.wait_ge(s_d, n)
                def turn(ins, m):
                    ins.then_inc(s_rank, 1)
                    dve.wait_ge(s_rank, q * 3 + m)
                turn(tt(rank[:], rank[:], low[:], ALU.add), 1)
                turn(tt(rank[:], rank[:], tie[:], ALU.add), 2)
                turn(tsc(own[:], own[:], float(PC), None, ALU.subtract), 3)
            nc.vector.tensor_copy(ranki[:], rank[:]).then_inc(s_rank, 1)

        @block.scalar
        def _(act):
            act.wait_ge(s_rank, 3 * (E // PC) + 1)

        @block.tensor
        def _(pe):
            pe.wait_ge(s_rank, 3 * (E // PC) + 1)

        @block.gpsimd
        def _(pool):
            nc.gpsimd.memset(rank[:], 0.0).then_inc(s_init, 1)
            nc.gpsimd.iota(own[:], [[1, EC]], base=0, channel_multiplier=EC, allow_small_or_imprecise_dtypes=True).then_inc(s_init, 1)
            nc.gpsimd.iota(fidx[:], [[1, PC]], base=0, channel_multiplier=0, allow_small_or_imprecise_dtypes=True).then_inc(s_init, 1)
            pool.wait_ge(s_rank, 3 * (E // PC) + 1)
            pool.sem_inc(s_go, 1)
            with pool.Fori(0, EC // G) as i:
                nc.gpsimd.tensor_copy(ids[:], ranki[:, ts(i, G)]).then_inc(s_ids, 1)
                nc.gpsimd.tensor_copy(vals[:], cur[:, :, ts(i, G)]).then_inc(s_ids, 1)
                pool.wait_ge(s_ids, 2 * i + 2)
                pool.sem_inc(s_go, 1)
                for k in range(G):
                    for n, (name, _) in enumerate(fields):
                        nc.gpsimd.indirect_dma_start(out=dr[name], out_offset=bass.IndirectOffsetOnAxis(ap=ids[:, k:k + 1], axis=0),
                                                     in_=vals[:, n, k:k + 1], in_offset=None).then_inc(s_put, 16)
                pool.wait_ge(s_put, 16 * 3 * G * (i + 1))
                pool.sem_inc(s_go, 1)


def prepare_edges(nc, ctx, c, dr, src, dst, etype, ntype):
    def keep(name, shape, dt=F32):
        return ctx.enter_context(nc.sbuf_tensor(name, shape, dt))
    v = dict(dr=keep("dr", [P, NC]), kvi=keep("kvi", [P, NC], I32), srci=keep("srci", [P, NC], I32),
             same=keep("same", [P, NV]), blk=keep("blk", [1, NV], I32), drrow=keep("drrow", [P, VT, SUP], BF16),
             types=keep("types", [P, NB, T]))
    Q = NS // 4
    full, rest = divmod(E, SUP)
    tail = full - 3 * Q
    with Stage(nc) as tmp:
        def sb(name, shape, dt=F32):
            return tmp.enter_context(nc.sbuf_tensor(name, shape, dt))

        def sem(name):
            return tmp.sem(name)
        ei = sb("ei", [Q, 3, 4, SUP], I32)
        e_prev = sb("e_prev", [Q, 4, SUP], I32)
        e_next = sb("e_next", [Q, 4, SUP], I32)
        ef = sb("ef", [Q, 4, NF, SUP])
        fprev = sb("fprev", [Q, 4, SUP])
        fnext = sb("fnext", [Q, 4, SUP])
        below = sb("below", [Q, NB])
        junk = sb("junk", [Q, 4, SUP])
        esi = sb("esi", [P, 1], I32)
        turn = sb("turn", [P, 1])
        pplus = sb("pplus", [P, 1])
        viota = sb("viota", [P, NV])
        cmp = sb("cmp", [P, NV])
        bfull = sb("bfull", [P, NV])
        bvt = sb("bvt", [P, VT])
        cvf = sb("cvf", [P, VT])
        cvi = sb("cvi", [P, VT], I32)
        viota4 = sb("viota4", [P, VT])
        b128 = sb("b128", [P, VT])
        rv = sb("rv", [P, VT, NF, SUP])
        dq = sb("dq", [P, VT, SUP])
        va = sb("va", [P, VT, SUP])
        vb = sb("vb", [P, VT, SUP])
        vrow = sb("vrow", [P, 3, VT, SUP], BF16)
        ti = sb("ti", [NB, P], I32)
        tf = sb("tf", [NB, P])
        tm = sb("tm", [NB, T, P])
        psum = tmp.enter_context(nc.psum_tensor("ps_prep", [P, 4, 512], F32))
        s_init, s_dma, s_vec, s_rec, s_cnt, s_ps, s_idx = map(sem, ("prep_init", "prep_load", "prep_vec", "prep_rec",
                                                                   "prep_cnt", "prep_ps", "prep_idx"))
        s_got, s_wr, s_tr, s_cp, s_ty = map(sem, ("prep_got", "prep_wr", "prep_tr", "prep_cp", "prep_ty"))
        s_cmp = sem("prep_cmp")
        flat = [dst, src, etype]
        with nc.Block() as block:
            @block.gpsimd
            def _(pool):
                init = Chain(pool, s_init)
                init(nc.gpsimd.memset(ei[:, 0], PADDST))
                init(nc.gpsimd.memset(ei[:, 1], 0))
                init(nc.gpsimd.memset(ei[:, 2], 0))
                init(nc.gpsimd.memset(e_prev[:], PADDST))
                init(nc.gpsimd.memset(e_prev[0:1, 0, 0:1], -1))
                init(nc.gpsimd.memset(e_next[:], PADDST))
                init(nc.gpsimd.memset(ti[:], T))
                init(nc.gpsimd.iota(viota[:], [[1, NV]], base=0, channel_multiplier=0,
                                    allow_small_or_imprecise_dtypes=True))
                init(nc.gpsimd.iota(viota4[:], [[1, VT]], base=0, channel_multiplier=VT,
                                    allow_small_or_imprecise_dtypes=True))
                init(nc.gpsimd.iota(pplus[:], [[0, 1]], base=1, channel_multiplier=1,
                                    allow_small_or_imprecise_dtypes=True))
                pool.wait_ge(s_rec, 4 * NF * 16)
                pool.wait_ge(s_idx, 1)
                for t in range(VT):
                    nc.gpsimd.indirect_dma_start(
                        out=rv[0:NT, t].rearrange("p f s -> p (f s)"), out_offset=None, in_=dr["rec"],
                        in_offset=bass.IndirectOffsetOnAxis(ap=cvi[0:NT, t:t + 1], axis=0)).then_inc(s_got, 16)
                pool.wait_ge(s_got, 64)

            @block.sync
            def _(sp):
                sp.wait_ge(s_init, 10)
                for n, a in enumerate(flat):
                    sp.dma_start(ei[:, n, 0:3], a[0:3 * Q * SUP].rearrange("(t q s) -> q t s", t=3, s=SUP)).then_inc(s_dma, 16)
                    sp.dma_start(ei[0:tail, n, 3], a[3 * Q * SUP:full * SUP].rearrange("(q s) -> q s", s=SUP)).then_inc(s_dma, 16)
                    sp.dma_start(ei[tail:tail + 1, n, 3, 0:rest], a[full * SUP:E].rearrange("(q s) -> q s", q=1)).then_inc(s_dma, 16)
                sp.dma_start(e_prev[0:1, 0, 1:SUP], dst[0:SUP - 1].rearrange("(q s) -> q s", q=1)).then_inc(s_dma, 16)
                sp.dma_start(e_prev[1:Q, 0], dst[SUP - 1:Q * SUP - 1].rearrange("(q s) -> q s", s=SUP)).then_inc(s_dma, 16)
                sp.dma_start(e_prev[:, 1:3], dst[Q * SUP - 1:3 * Q * SUP - 1].rearrange("(t q s) -> q t s", t=2, s=SUP)).then_inc(s_dma, 16)
                sp.dma_start(e_prev[0:tail, 3], dst[3 * Q * SUP - 1:full * SUP - 1].rearrange("(q s) -> q s", s=SUP)).then_inc(s_dma, 16)
                sp.dma_start(e_prev[tail:tail + 1, 3, 0:rest + 1], dst[full * SUP - 1:E].rearrange("(q s) -> q s", q=1)).then_inc(s_dma, 16)
                sp.dma_start(e_next[:, 0:3], dst[1:3 * Q * SUP + 1].rearrange("(t q s) -> q t s", t=3, s=SUP)).then_inc(s_dma, 16)
                sp.dma_start(e_next[0:tail, 3], dst[3 * Q * SUP + 1:full * SUP + 1].rearrange("(q s) -> q s", s=SUP)).then_inc(s_dma, 16)
                sp.dma_start(e_next[tail:tail + 1, 3, 0:rest - 1], dst[full * SUP + 1:E].rearrange("(q s) -> q s", q=1)).then_inc(s_dma, 16)
                sp.dma_start(ti[0:NB - 1, :], ntype[0:(NB - 1) * P].rearrange("(b p) -> b p", p=P)).then_inc(s_dma, 16)
                sp.dma_start(ti[NB - 1:NB, 0:NLAST], ntype[(NB - 1) * P:N].rearrange("(b p) -> b p", b=1)).then_inc(s_dma, 16)
                sp.wait_ge(s_vec, 1)
                for t in range(4):
                    for f in range(NF):
                        sp.dma_start(dr["rec"][t * Q:(t + 1) * Q, f * SUP:(f + 1) * SUP], ef[:, t, f]).then_inc(s_rec, 16)
                sp.dma_start(dr["typerow"].rearrange("t (b p) -> b t p", p=P), tm[:]).then_inc(s_ty, 16)
                sp.wait_ge(s_vec, 2)
                for n, name in enumerate(("rel", "first", "last")):
                    sp.dma_start(dr[name].rearrange("(i t s) -> i t s", t=VT, s=SUP), vrow[0:NT, n]).then_inc(s_wr, 16)
                sp.wait_ge(s_wr, 48)
                sp.wait_ge(s_ty, 16)

            @block.vector
            def _(dve):
                step = Chain(dve, sem("prep_steps"))
                tt, tsc = nc.vector.tensor_tensor, nc.vector.tensor_scalar
                dve.wait_ge(s_init, 10)
                dve.wait_ge(s_dma, 19 * 16)
                step(nc.vector.tensor_copy(ef[:, :, F_DST], ei[:, 0]))
                step(tsc(ef[:, :, F_KV], ei[:, 1], float(R), None, ALU.mult))
                step(nc.vector.tensor_copy(ef[:, :, F_REL], ei[:, 2]))
                step(tt(ef[:, :, F_KV], ef[:, :, F_KV], ef[:, :, F_REL], ALU.add))
                step(nc.vector.tensor_copy(ef[:, :, F_SRC], ei[:, 1]))
                step(nc.vector.tensor_copy(fprev[:], e_prev[:]))
                step(nc.vector.tensor_copy(fnext[:], e_next[:]))
                step(tt(ef[:, :, F_FIRST], ef[:, :, F_DST], fprev[:], ALU.not_equal))
                step(tt(ef[:, :, F_LAST], ef[:, :, F_DST], fnext[:], ALU.not_equal))
                step(nc.vector.tensor_copy(tf[:], ti[:]))
                for t in range(T):
                    step(tsc(tm[:, t], tf[:], float(t), None, ALU.is_equal))
                nc.vector.memset(below[:, NB - 1:NB], 0.0).then_inc(s_vec, 1)
                for b in range(NB - 1):
                    step(nc.vector.tensor_scalar(junk[:], ef[:, :, F_DST], float((b + 1) * P), None, ALU.is_lt,
                                                 ALU.add, accum_out=below[:, b:b + 1]))
                nc.vector.memset(cmp[:], 0.0).then_inc(s_cnt, 1)
                dve.wait_ge(s_ps, 1)
                step(nc.vector.tensor_copy(esi[0:NB - 1], psum[0:NB - 1, 0, 0:1]))
                step(tsc(esi[0:NB - 1], esi[0:NB - 1], SUP.bit_length() - 1, None, ALU.arith_shift_right))
                step(nc.vector.tensor_copy(turn[0:NB - 1], esi[0:NB - 1]))
                step(tsc(turn[0:NB - 1], turn[0:NB - 1], float(NS - 1), pplus[0:NB - 1, 0:1], ALU.min, ALU.add))
                tsc(cmp[0:NB - 1], viota[0:NB - 1], turn[0:NB - 1, 0:1], None, ALU.is_ge).then_inc(s_cmp, 1)
                dve.wait_ge(s_ps, 2)
                step(nc.vector.tensor_copy(bfull[:], psum[:, 1, 0:NV]))
                step(nc.vector.tensor_copy(bvt[0:NT], psum[0:NT, 2, 0:VT]))
                step(tt(cvf[0:NT], viota4[0:NT], bvt[0:NT], ALU.subtract))
                nc.vector.tensor_copy(cvi[0:NT], cvf[0:NT]).then_inc(s_idx, 1)
                step(nc.vector.memset(v["same"][:, 0:1], 0.0))
                step(tt(v["same"][:, 1:NV], bfull[:, 1:NV], bfull[:, 0:NV - 1], ALU.is_equal))
                step(nc.vector.tensor_copy(v["blk"][:], bfull[0:1, :]))
                step(tsc(b128[0:NT], bvt[0:NT], float(P), None, ALU.mult))
                dve.wait_ge(s_got, 64)
                r = rv[0:NT]
                for t in range(VT):
                    step(tsc(dq[0:NT, t], r[:, t, F_DST], b128[0:NT, t:t + 1], None, ALU.subtract))
                step(tsc(va[0:NT], dq[0:NT], 0.0, None, ALU.is_ge))
                step(tsc(vb[0:NT], dq[0:NT], float(P), None, ALU.is_lt))
                step(tt(va[0:NT], va[0:NT], vb[0:NT], ALU.mult))
                step(tsc(dq[0:NT], dq[0:NT], 1.0, None, ALU.add))
                step(tt(dq[0:NT], dq[0:NT], va[0:NT], ALU.mult))
                step(tsc(dq[0:NT], dq[0:NT], 1.0, None, ALU.subtract))
                step(nc.vector.tensor_copy(v["drrow"][0:NT], dq[0:NT]))
                step(tsc(vb[0:NT], r[:, :, F_REL], 1.0, None, ALU.add))
                step(tt(vb[0:NT], vb[0:NT], va[0:NT], ALU.mult))
                step(tsc(vrow[0:NT, 0], vb[0:NT], 1.0, None, ALU.subtract))
                step(tt(vrow[0:NT, 1], r[:, :, F_FIRST], va[0:NT], ALU.mult))
                tt(vrow[0:NT, 2], r[:, :, F_LAST], va[0:NT], ALU.mult).then_inc(s_vec, 1)
                for n in range(6):
                    dve.wait_ge(s_tr, n + 1)
                    o = (v["dr"], v["kvi"], v["srci"])[n // 2].rearrange("p (i t j) -> p t j i", t=VT, j=2)
                    k = n % 2
                    for q in range(2):
                        src_ = psum[:, 2 * (n % 2) + q, 0:2 * NT].rearrange("p (j i) -> p j i", j=2)
                        ins = nc.vector.tensor_copy(o[:, 2 * k + q], src_)
                        if q == 0:
                            step(ins)
                    ins.then_inc(s_cp, 1)
                dve.wait_ge(s_tr, 7)
                step(nc.vector.tensor_copy(v["types"][:].rearrange("p b t -> p t b"),
                                           psum[:, 0, 0:T * NB].rearrange("p (t b) -> p t b", t=T)))

            @block.tensor
            def _(pe):
                mm = nc.tensor.matmul
                pe.wait_ge(s_cnt, 1)
                mm(psum[0:NB - 1, 0, 0:1], below[:, 0:NB - 1], c["ones"][0:Q, 0:1], start=True, stop=True).then_inc(s_ps, 1)
                pe.wait_ge(s_cmp, 1)
                mm(psum[:, 1, 0:NV], c["ones"][0:NB - 1, :], cmp[0:NB - 1, :], start=True, stop=True)
                for t in range(VT):
                    ins = mm(psum[0:NT, 2, t:t + 1], cmp[0:NB - 1, t::VT], c["ones"][0:NB - 1, 0:1], start=True, stop=True)
                ins.then_inc(s_ps, 1)
                pe.wait_ge(s_vec, 2)
                for n in range(6):
                    if n >= 2:
                        pe.wait_ge(s_cp, n - 1)
                    for q in range(2):
                        t = 2 * (n % 2) + q
                        for j in range(2):
                            a = (dq[0:NT, t], rv[0:NT, t, F_KV], rv[0:NT, t, F_SRC])[n // 2][:, j * P:(j + 1) * P]
                            ins = nc.tensor.transpose(psum[:, 2 * (n % 2) + q, j * NT:(j + 1) * NT], a, c["ident"][0:NT, 0:NT])
                    ins.then_inc(s_tr, 1)
                pe.wait_ge(s_cp, 6)
                for t in range(T):
                    ins = nc.tensor.transpose(psum[:, 0, t * NB:(t + 1) * NB], tm[:, t], c["ident"][0:NB, 0:NB])
                ins.then_inc(s_tr, 1)
    return v


def node_stats(nc, c, tag, xs, mv, scale, shift, load=None):
    with Stage(nc) as tmp:
        stats = tmp.enter_context(nc.sbuf_tensor(f"stats_{tag}", [P, NB, 6], F32))
        std = tmp.enter_context(nc.sbuf_tensor(f"std_{tag}", [P, NB], F32))
        s_in, s_st, s_ag, s_sq, s_step = (tmp.sem(f"{n}_{tag}")
                                          for n in ("st_in", "st_bn", "st_ag", "st_sq", "st_step"))
        with nc.Block() as block:
            if load is not None:
                @block.sync
                def _(sp):
                    sp.dma_start(xs[:, 0:NB - 1], load[0:(NB - 1) * P].rearrange("(b p) d -> p b d", p=P)).then_inc(s_in, 16)
                    sp.dma_start(xs[0:NLAST, NB - 1], load[(NB - 1) * P:N]).then_inc(s_in, 16)

            @block.vector
            def _(dve):
                if load is not None:
                    dve.wait_ge(s_in, 32)
                for b in range(NB):
                    nc.vector.bn_stats(stats[:, b], xs[:, b, 0:D]).then_inc(s_st, 1)
                for b in range(NB):
                    dve.wait_ge(s_st, b + 1)
                    nc.vector.bn_aggr(mv[:, b], stats[:, b]).then_inc(s_ag, 1)
                step = Chain(dve, s_step)
                dve.wait_ge(s_sq, 1)
                step(nc.vector.reciprocal(scale[:], std[:]))
                step(nc.vector.scalar_tensor_tensor(out=shift[:], in0=mv[:, :, 0], scalar=-1.0, in1=scale[:],
                                                    op0=ALU.mult, op1=ALU.mult))

            @block.scalar
            def _(act):
                act.wait_ge(s_ag, NB)
                nc.scalar.activation(std[:], mv[:, :, 1], ACT.Sqrt, bias=c["eps"][:, 0:1]).then_inc(s_sq, 1)


def project(nc, c, dr, v, xs, qs, scale, shift, a):
    with Stage(nc) as tmp:
        def sb(name, shape, dt=F32):
            return tmp.enter_context(nc.sbuf_tensor(name, shape, dt))

        def sem(name):
            return tmp.sem(name)
        wkv = sb("wkv", [P, 2, T, 2, D])
        wq = sb("wq", [P, 2, T, D])
        bkv = sb("bkv", [T, 2, D])
        bq = sb("bq", [T, D])
        rel = sb("relw", [P, 2, 2, R, P])
        pri = sb("pri", [P, R, H])
        tsc_ = sb("tscale", [P, T, NB])
        tsh_ = sb("tshift", [P, T, NB])
        tmb = sb("tmb", [T, P])
        types_ = sb("typerows", [T, NB, P])
        hm = sb("hm", [P, T, D])
        hT = sb("hT", [P, T * 2, P])
        kvT = sb("kvT", [P, 4, P])
        stage = sb("stage", [P, 2, R, D])
        psT = tmp.enter_context(nc.psum_tensor("psT", [P, 2, 512], F32))
        psKV = tmp.enter_context(nc.psum_tensor("psKV", [P, 512], F32))
        psQ = tmp.enter_context(nc.psum_tensor("psQ", [P, 512], F32))
        psR = tmp.enter_context(nc.psum_tensor("psR", [P, 4, 512], F32))
        w_in, z_done, pri_done, mk_done = map(sem, ("w_in", "z_done", "pri_done", "mk_done"))
        hm_done, tr_done, hT_done, kv_done, kvT_done, q_done, q_out = map(sem, (
            "hm_done", "tr_done", "hT_done", "kv_done", "kvT_done", "q_done", "q_out"))
        rel_done, rel_dve, rel_act, tm_in, k_wr, v_wr = map(sem, ("rel_done", "rel_dve", "rel_act", "tm_in", "k_wr", "v_wr"))
        with nc.Block() as block:
            @block.gpsimd
            def _(pool):
                nc.gpsimd.memset(rel[:], 0.0).then_inc(z_done, 1)
                pool.wait_ge(w_in, (9 + 4 + 8 + 1) * 16)
                with pool.Fori(0, NB) as b:
                    pool.wait_ge(q_done, b + 1)
                    nc.gpsimd.tensor_copy(tmb[:], types_[:, ds(b, 1)].rearrange("t o p -> t (o p)")).then_inc(tm_in, 1)

            @block.sync
            def _(sp):
                sp.sem_inc(k_wr, 16)
                sp.sem_inc(v_wr, 16)
                for t in range(T):
                    for o, w in ((wkv[:, :, t, 0], a['L0_gnn_Wk']), (wkv[:, :, t, 1], a['L0_gnn_Wv']), (wq[:, :, t], a['L0_gnn_Wq'])):
                        sp.dma_start(o, w[t].rearrange("(g p) d -> p g d", p=P)).then_inc(w_in, 16)
                sp.dma_start(bkv[:, 0], a['L0_gnn_bk']).then_inc(w_in, 16)
                sp.dma_start(bkv[:, 1], a['L0_gnn_bv']).then_inc(w_in, 16)
                sp.dma_start(bq[:], a['L0_gnn_bq']).then_inc(w_in, 16)
                sp.dma_start(pri[:].rearrange("p r h -> p (r h)"), a['L0_gnn_rel_pri'].rearrange("(o r) h -> o (r h)", o=1).to_broadcast([P, R * H])).then_inc(w_in, 16)
                sp.wait_ge(z_done, 1)
                for n, w in enumerate((a['L0_gnn_rel_att'], a['L0_gnn_rel_msg'])):
                    for g in range(2):
                        for u in range(2):
                            sp.dma_start(rel[u * DK:(u + 1) * DK, n, g, :, u * DK:(u + 1) * DK],
                                         w[:, 2 * g + u].rearrange("r d e -> d r e")).then_inc(w_in, 16)

                sp.dma_start(types_[:], dr["typerow"].rearrange("t (b p) -> t b p", p=P)).then_inc(w_in, 16)

                def block_io(b):
                    for n, s in ((0, k_wr), (1, v_wr)):
                        sp.wait_ge(rel_dve, 4 * b + 2 * n + 4)
                        sp.wait_ge(rel_act, 4 * b + 2 * n + 4)
                        sp.dma_start(dr["kv"].rearrange("(b p r) d -> b p r d", p=P, r=R)[ds(b, 1), :, :, n * D:(n + 1) * D]
                                     .rearrange("o p r d -> (o p) r d"), stage[:, n]).then_inc(s, 16)
                block_io(0)
                with sp.Fori(1, NB) as b:
                    block_io(b)
                sp.wait_ge(k_wr, 16 * (NB + 1))
                sp.wait_ge(v_wr, 16 * (NB + 1))

            @block.scalar
            def _(act):
                act.sem_inc(rel_act, 2)
                act.sem_inc(kvT_done, 1)

                def masked(b):
                    for t in range(T):
                        nc.scalar.activation(hm[:, t], xs[:, ds(b, 1)].rearrange("p o d -> p (o d)"), ACT.Relu,
                                             bias=tsh_[:, t, ds(b, 1)], scale=tsc_[:, t, ds(b, 1)]).then_inc(hm_done, 1)
                act.wait_ge(mk_done, 1)
                masked(0)

                def rest(b, more):
                    act.wait_ge(kv_done, b + 1)
                    act.wait_ge(rel_done, 8 * b + 1)
                    nc.scalar.copy(kvT[:].rearrange("p n q -> p (n q)"), psKV[:]).then_inc(kvT_done, 1)
                    if more:
                        act.wait_ge(tr_done, b + 1)
                        masked(b + 1)
                    for m in range(1, 8, 2):
                        n, g, u = m // 4, m // 2 % 2, m % 2
                        act.wait_ge(rel_done, 8 * b + m + 2)
                        if m < 2 or m == 5:
                            act.wait_ge((k_wr, v_wr)[n], 16 * (b + 1))
                        nc.scalar.copy(stage[:, n, 3 * u:3 * u + 3, g * P:(g + 1) * P],
                                       psR[:, m % 4, 0:3 * P].rearrange("p (r e) -> p r e", r=3)).then_inc(rel_act, 1)
                with act.Fori(0, NB - 1) as b:
                    rest(b, True)
                rest(NB - 1, False)

            @block.vector
            def _(dve):
                step = Chain(dve, sem("proj_steps"))
                dve.sem_inc(rel_dve, 2)
                for t in range(T):
                    step(nc.vector.tensor_tensor(tsc_[:, t], scale[:], v["types"][:, :, t], ALU.mult))
                    step(nc.vector.tensor_tensor(tsh_[:, t], shift[:], v["types"][:, :, t], ALU.mult))
                nc.vector.memset(hT[0:1, 0, 0:1], 0.0).then_inc(mk_done, 1)
                dve.wait_ge(w_in, (9 + 4 + 8 + 1) * 16)
                step(nc.vector.tensor_scalar(pri[:], pri[:], float(DK) ** -0.5, None, ALU.mult))
                for g in range(2):
                    for u in range(2):
                        w = rel[u * DK:(u + 1) * DK, 0, g, :, u * DK:(u + 1) * DK]
                        nc.vector.tensor_tensor(w, w, pri[u * DK:(u + 1) * DK, :, 2 * g + u].unsqueeze(2).to_broadcast([DK, R, DK]),
                                                ALU.mult).then_inc(pri_done, 1)

                def turn_(b):
                    dve.wait_ge(tr_done, b + 1)
                    dve.wait_ge(q_done, b + 1)
                    nc.vector.tensor_copy(hT[:, 0:4].rearrange("p n q -> p (n q)"), psT[:, 0, :]).then_inc(hT_done, 1)
                    nc.vector.tensor_copy(hT[:, 4:6].rearrange("p n q -> p (n q)"), psT[:, 1, 0:2 * P]).then_inc(hT_done, 1)

                def rest(b):
                    for m in range(0, 8, 2):
                        n, g, u = m // 4, m // 2 % 2, m % 2
                        dve.wait_ge(rel_done, 8 * b + m + 2)
                        if m in (0, 4):
                            dve.wait_ge((k_wr, v_wr)[n], 16 * (b + 1))
                        nc.vector.tensor_copy(stage[:, n, 3 * u:3 * u + 3, g * P:(g + 1) * P],
                                              psR[:, m % 4, 0:3 * P].rearrange("p (r e) -> p r e", r=3)).then_inc(rel_dve, 1)
                        if m == 2:
                            dve.wait_ge(q_done, b + 2)
                            nc.vector.tensor_copy(qs[:, ds(b, 1)].rearrange("p o d -> p (o d)"), psQ[:, 0:D]).then_inc(q_out, 1)
                turn_(0)
                with dve.Fori(0, NB - 1) as b:
                    turn_(b + 1)
                    rest(b)
                rest(NB - 1)

            @block.tensor
            def _(pe):
                pe.sem_inc(rel_done, 1)
                pe.sem_inc(q_done, 1)

                def transposes(b, first=False):
                    pe.wait_ge(hm_done, 3 * (b + 1))
                    if not first:
                        pe.wait_ge(hT_done, 2 * b)
                    for n in range(6):
                        t, g = n // 2, n % 2
                        ins = nc.tensor.transpose(psT[:, n // 4, n % 4 * P:(n % 4 + 1) * P], hm[:, t, g * P:(g + 1) * P], c["ident"][:])
                    ins.then_inc(tr_done, 1)

                def block_(b, more, first=False):
                    pe.wait_ge(hT_done, 2 * (b + 1))
                    pe.wait_ge(tm_in, b + 1)
                    pe.wait_ge(kvT_done, b + 1)
                    for n in range(4):
                        for t in range(T):
                            for g in range(2):
                                nc.tensor.matmul(psKV[:, n * P:(n + 1) * P], wkv[:, g, t, n // 2, n % 2 * P:(n % 2 + 1) * P],
                                                 hT[:, 2 * t + g], start=(t == 0 and g == 0), stop=False)
                        ins = nc.tensor.matmul(psKV[:, n * P:(n + 1) * P], bkv[:, n // 2, n % 2 * P:(n % 2 + 1) * P], tmb[:],
                                               start=False, stop=True)
                    ins.then_inc(kv_done, 1)
                    if not first:
                        pe.wait_ge(q_out, b)
                    for t in range(T):
                        for g in range(2):
                            nc.tensor.matmul(psQ[:, 0:D], hT[:, 2 * t + g], wq[:, g, t], start=(t == 0 and g == 0), stop=False)
                    nc.tensor.matmul(psQ[:, 0:D], tmb[:], bq[:], start=False, stop=True).then_inc(q_done, 1)
                    if more:
                        transposes(b + 1)
                    pe.wait_ge(kvT_done, b + 2)
                    for m in range(8):
                        n, g, u = m // 4, m // 2 % 2, m % 2
                        pe.wait_ge((rel_dve, rel_act)[m % 2], 4 * b + m // 2 + 1)
                        nc.tensor.matmul(psR[:, m % 4, 0:3 * P], kvT[:, 2 * n + g],
                                         rel[:, n, g, 3 * u:3 * u + 3].rearrange("p r e -> p (r e)"),
                                         start=True, stop=True).then_inc(rel_done, 1)
                pe.wait_ge(w_in, (9 + 4 + 8 + 1) * 16)
                pe.wait_ge(pri_done, 4)
                transposes(0, True)
                block_(0, True, True)
                with pe.Fori(1, NB - 1) as b:
                    block_(b, True)
                block_(NB - 1, False)


GS = 4
SLOTS = 4 * GS
NI = NC // SLOTS


def edge_scores(nc, c, dr, v, layer, table, index, node, width):
    L = layer
    vcol = D if L == 0 else 0
    cols = D if L == 0 else 2 * H
    with Stage(nc) as tmp:
        def sb(name, shape, dt=F32):
            return tmp.enter_context(nc.sbuf_tensor(f"{name}{L}", shape, dt))

        def sem(name):
            return tmp.sem(f"{name}{L}")
        rows = sb("rows", [P, SLOTS, width])
        ids = sb("ids", [P, SLOTS], I32)
        off = sb("off", [P, 2, SUP])
        hot = sb("hot", [P, 2, SUP])
        prod = sb("prod", [P, 4, D])
        sc = sb("sc", [P, SLOTS, H])
        att = sb("att", [P, H, NC])
        own = sb("own", [P, H, NC]) if L == 1 else None
        stage = sb("stage_att", [CW, 2, H, P])
        psB = tmp.enter_context(nc.psum_tensor(f"psB{L}", [P, 2, 512], F32))
        psD = tmp.enter_context(nc.psum_tensor(f"psD{L}", [P, 4, 512], F32))
        psX = tmp.enter_context(nc.psum_tensor(f"psX{L}", [P, 2, 512], F32))
        got = [sem(f"got{k}_") for k in range(SLOTS)]
        kept = [sem(f"kept{g}_") for g in range(SLOTS // GS)]
        ids_done, go, used, bc_done, off_done, hot_done, dst_done, prod_done, sc_done, sc_kept = map(sem, (
            "ids_done", "go", "used", "bc_done", "off_done", "hot_done", "dst_done", "prod_done", "sc_done", "sc_kept"))
        tr_done, tr_out = map(sem, ("atr_done", "atr_out"))
        wr = [sem("awr0_"), sem("awr1_")]
        NX = CT * (1 + (L == 1))
        with nc.Block() as block:
            @block.gpsimd
            def _(pool):
                with pool.Fori(0, NI) as i:
                    for g in range(SLOTS // GS):
                        pool.wait_ge(used, i * SLOTS + (g + 1) * GS)
                        pool.sem_inc(go, 1)
                        pool.wait_ge(kept[g], 16 * (i + 1))
                        pool.sem_inc(go, 1)
                        nc.gpsimd.tensor_copy(ids[:, g * GS:(g + 1) * GS],
                                              index[:, ts(i * (SLOTS // GS) + g, GS)]).then_inc(ids_done, 1)
                        pool.wait_ge(ids_done, i * (SLOTS // GS) + g + 1)
                        pool.sem_inc(go, 1)
                        for k in range(g * GS, (g + 1) * GS):
                            nc.gpsimd.indirect_dma_start(
                                out=rows[:, k], out_offset=None, in_=table,
                                in_offset=bass.IndirectOffsetOnAxis(ap=ids[:, k:k + 1], axis=0)).then_inc(got[k], 16)

            @block.sync
            def _(sp):
                for s in kept:
                    sp.sem_inc(s, 16)
                with sp.Fori(0, NI) as i:
                    for g in range(SLOTS // GS):
                        for k in range(g * GS, (g + 1) * GS):
                            sp.wait_ge(got[k], 16 * (i + 1))
                        o = dr["val"].rearrange("(i k p) d -> i p k d", k=GS, p=P)[ds(i * (SLOTS // GS) + g, 1)]
                        sp.dma_start(o.rearrange("o p k d -> (o p) k d"), rows[:, g * GS:(g + 1) * GS, vcol:vcol + D]).then_inc(kept[g], 16)
                for n in range(NX):
                    a = dr["att"] if n < CT else dr["self_"]
                    sp.wait_ge(tr_out, n + 1)
                    sp.dma_start(a.rearrange("h (t c p) -> t c h p", t=CT, p=P)[n % CT], stage[:, n % 2]).then_inc(wr[n % 2], 16)
                for s in kept:
                    sp.wait_ge(s, 16 * (NI + 1))
                for s in wr:
                    sp.wait_ge(s, 16 * (NX // 2))

            @block.tensor
            def _(pe):
                pe.sem_inc(dst_done, 4)
                with pe.Fori(0, NI) as i:
                    blk = [pe.value_load(v["blk"][0:1, ds(i * (SLOTS // 2) + t, 1)], min_val=0, max_val=NB - 1)
                           for t in range(SLOTS // 2)]

                    def spread_places(t):
                        pe.wait_ge(off_done, i * (SLOTS // 2) + t + 1)
                        row = c["identb"][0:NT, ds(i * (SLOTS // 2 // VT) + t // VT, 1)].to_broadcast([NT, P])
                        nc.tensor.matmul(psB[:, t % 2, 0:SUP], row, v["drrow"][0:NT, t % VT], start=True, stop=True).then_inc(bc_done, 1)
                    spread_places(0)
                    for t in range(SLOTS // 2):
                        if t + 1 < SLOTS // 2:
                            spread_places(t + 1)
                        pe.wait_ge(hot_done, i * (SLOTS // 2) + t + 1)
                        for j in range(2):
                            k = 2 * t + j
                            pe.wait_ge(prod_done, i * SLOTS + k + 1)
                            nc.tensor.matmul(psD[:, k % 4, 0:cols], hot[:, t % 2, j * P:(j + 1) * P],
                                             node[:, ds(blk[t], 1)].rearrange("p o d -> p (o d)"), start=True, stop=True).then_inc(dst_done, 1)
                for n in range(NX):
                    a = att if n < CT else own
                    if n == 0:
                        pe.wait_ge(sc_kept, 2 * NI if L == 1 else NI)
                    if n >= 2:
                        pe.wait_ge(tr_out, n - 1)
                    for h in range(H):
                        ins = nc.tensor.transpose(psX[0:CW, n % 2, h * P:(h + 1) * P], a[:, h, n % CT * CW:(n % CT + 1) * CW], c["ident"][:])
                    ins.then_inc(tr_done, 1)

            @block.scalar
            def _(act):
                act.sem_inc(off_done, 2)
                with act.Fori(0, NI) as i:
                    for t in range(SLOTS // 2):
                        V = i * (SLOTS // 2) + t
                        act.wait_ge(bc_done, V + 1)
                        nc.scalar.activation(off[:, t % 2], psB[:, t % 2, 0:SUP], ACT.Abs, bias=c["npiota"][:, 0:1]).then_inc(off_done, 1)
                        act.wait_ge(off_done, V + 3)
                        act.wait_ge(dst_done, 2 * V)
                        nc.scalar.activation(hot[:, t % 2], off[:, t % 2], ACT.Relu, bias=1.0, scale=-1.0).then_inc(hot_done, 1)

            @block.vector
            def _(dve):
                dve.sem_inc(used, SLOTS)
                dve.sem_inc(prod_done, 4)
                dve.sem_inc(sc_done, 4)
                with dve.Fori(0, NI) as i:
                    K = i * SLOTS

                    def reduce_(k):
                        dve.wait_ge(prod_done, K + k + 5)
                        nc.vector.tensor_reduce(sc[:, k], prod[:, k % 4].rearrange("p (h d) -> p h d", h=H), AX.X, ALU.add).then_inc(sc_done, 1)
                    for k in range(SLOTS):
                        dve.wait_ge(got[k], 16 * (i + 1))
                        dve.wait_ge(dst_done, K + k + 5)
                        if L == 0:
                            dve.wait_ge(sc_done, K + k + 1)
                            ins = nc.vector.tensor_tensor(prod[:, k % 4], rows[:, k, 0:D], psD[:, k % 4, 0:D], ALU.mult)
                            ins.then_inc(prod_done, 1)
                            if k:
                                reduce_(k - 1)
                        else:
                            nc.vector.tensor_tensor(sc[:, k], rows[:, k, D:D + H], psD[:, k % 4, 0:H], ALU.add).then_inc(sc_done, 1)
                            nc.vector.tensor_copy(own[:, :, ds(K + k, 1)].rearrange("p h o -> p (h o)"), psD[:, k % 4, H:2 * H]).then_inc(prod_done, 1)
                        if k % GS == GS - 1:
                            if L == 0:
                                dve.wait_ge(prod_done, K + k + 5)
                            else:
                                dve.wait_ge(sc_done, K + k + 5)
                            dve.sem_inc(used, GS)
                    if L == 0:
                        reduce_(SLOTS - 1)
                    dve.wait_ge(sc_done, K + SLOTS + 4)
                    nc.vector.tensor_copy(att[:, :, ts(i, SLOTS)], sc[:].rearrange("p k h -> p h k")).then_inc(sc_kept, 1)
                    dve.wait_ge(sc_kept, i + 1)
                if L == 1:
                    dve.wait_ge(prod_done, NC + 4)
                    dve.sem_inc(sc_kept, NI)
                for n in range(NX):
                    dve.wait_ge(tr_done, n + 1)
                    if n >= 2:
                        dve.wait_ge(wr[n % 2], 16 * (n // 2))
                    nc.vector.tensor_copy(stage[:, n % 2].rearrange("c h p -> c (h p)"), psX[0:CW, n % 2]).then_inc(tr_out, 1)


def run_flags(nc, dr, sp, sem, tiles):
    for tile, name in tiles:
        for h in range(H):
            sp.dma_start(tile[h * GR:(h + 1) * GR], dr[name].rearrange("(g s) -> g s", s=SL)).then_inc(sem, 16)


class Carry:

    def __init__(self, nc, c, tmp, tag):
        def sb(name, shape, dt=F32):
            return tmp.enter_context(nc.sbuf_tensor(f"{name}_{tag}", shape, dt))
        self.nc, self.c = nc, c
        self.edge = sb("edge", [P, 2])
        self.row = sb("crow", [1, 2, P])
        self.flag = sb("cflag", [1, 2, P])
        self.got = sb("cgot", [1, 2, P + 1])
        self.back = sb("cback", [P, 2])
        self.ps = tmp.enter_context(nc.psum_tensor(f"ps_carry_{tag}", [P, 512], F32))
        self.psb = tmp.enter_context(nc.psum_tensor(f"ps_cback_{tag}", [P, 512], F32))
        self.out, self.inn, self.ret, self.done = (tmp.sem(f"{n}_{tag}")
                                                   for n in ("c_edge", "c_row", "c_got", "c_back"))
        self.n = self.m = 0

    def to_row(self, step, dve, a, b, o):
        nc = self.nc
        step(nc.vector.tensor_copy(self.edge[:, 0:1], a))
        nc.vector.tensor_copy(self.edge[:, 1:2], b).then_inc(self.out, 1)
        self.n += 1
        dve.wait_ge(self.inn, self.n)
        step(nc.vector.tensor_copy(o[:].rearrange("a b p -> a (b p)"), self.ps[0:1, 0:2 * P]))

    def carry(self, step, dve, a, b, neutral, op0, op1):
        nc = self.nc
        self.to_row(step, dve, a, b, self.row)
        step(nc.vector.memset(self.got[:], neutral))
        step(nc.vector.tensor_tensor_scan(self.got[0:1, 0, 1:P + 1], self.flag[0:1, 0], self.row[0:1, 0], neutral, op0, op1))
        nc.vector.tensor_tensor_scan(self.got[0:1, 1, 0:P][:, ::-1], self.flag[0:1, 1][:, ::-1], self.row[0:1, 1][:, ::-1],
                                     neutral, op0, op1).then_inc(self.ret, 1)
        self.m += 1
        dve.wait_ge(self.done, self.m)
        step(nc.vector.tensor_copy(self.back[:], self.psb[:, 0:2]))

    def tensor(self, pe, plan):
        nc, n, m = self.nc, 0, 0
        for back in plan:
            n += 1
            pe.wait_ge(self.out, n)
            nc.tensor.transpose(self.ps[0:1, 0:P], self.edge[:, 0:1], self.c["ident"][:])
            nc.tensor.transpose(self.ps[0:1, P:2 * P], self.edge[:, 1:2], self.c["ident"][:]).then_inc(self.inn, 1)
            if back:
                m += 1
                pe.wait_ge(self.ret, m)
                nc.tensor.matmul(self.psb[:, 0:1], self.got[0:1, 0, 0:P], self.c["one"][0:1], start=True, stop=True)
                nc.tensor.matmul(self.psb[:, 1:2], self.got[0:1, 1, 1:P + 1], self.c["one"][0:1], start=True, stop=True).then_inc(self.done, 1)


def softmax_by_relation(nc, c, dr):
    with Stage(nc) as tmp:
        def sb(name, shape, dt=F32):
            return tmp.enter_context(nc.sbuf_tensor(name, shape, dt))
        att, am, fw, bw, sel = (sb(n, [P, SL]) for n in ("s_att", "s_am", "s_fw", "s_bw", "s_sel"))
        rel, fi, la, pf, sf, mk = (sb(n, [P, SL], BF16) for n in ("s_rel", "s_fi", "s_la", "s_pf", "s_sf", "s_mk"))
        s_in, s_e, s_x, s_w, s_out, s_fl = (tmp.sem(n) for n in ("sm_in", "sm_e", "sm_x", "sm_w", "sm_out", "sm_st"))
        cy = Carry(nc, c, tmp, "r")
        view = "h (g s) -> (h g) s"
        with nc.Block() as block:
            @block.sync
            def _(sp):
                sp.dma_start(att[:], dr["att"].rearrange(view, g=GR)).then_inc(s_in, 16)
                run_flags(nc, dr, sp, s_in, ((rel, "rel"), (fi, "first"), (la, "last")))
                sp.wait_ge(s_w, 1)
                sp.dma_start(dr["w0"].rearrange(view, g=GR), att[:]).then_inc(s_out, 16)
                sp.wait_ge(s_out, 16)

            @block.scalar
            def _(act):
                act.wait_ge(s_e, 1)
                nc.scalar.activation(att[:], att[:], ACT.Exp).then_inc(s_x, 1)

            @block.tensor
            def _(pe):
                cy.tensor(pe, ([False] + [True] * R) * 2)

            @block.vector
            def _(dve):
                step = Chain(dve, s_fl)
                tt, tsc, stt, scan = (nc.vector.tensor_tensor, nc.vector.tensor_scalar, nc.vector.scalar_tensor_tensor,
                                      nc.vector.tensor_tensor_scan)
                dve.wait_ge(s_in, 16 * (1 + 3 * H))
                step(tsc(fi[:], fi[:], -BIG, None, ALU.mult))
                step(tsc(la[:], la[:], -BIG, None, ALU.mult))
                step(scan(pf[:], fi[:], fi[:], 0.0, ALU.add, ALU.min))
                step(scan(sf[:][:, ::-1], la[:][:, ::-1], la[:][:, ::-1], 0.0, ALU.add, ALU.min))
                cy.to_row(step, dve, pf[:, SL - 1:SL], sf[:, 0:1], cy.flag)
                step(nc.vector.memset(sel[:], 0.0))
                for r in range(R):
                    step(tsc(mk[:], rel[:], float(r), -BIG, ALU.not_equal, ALU.mult))
                    step(tt(am[:], att[:], mk[:], ALU.add))
                    step(scan(fw[:], fi[:], am[:], -BIG, ALU.add, ALU.max))
                    step(scan(bw[:][:, ::-1], la[:][:, ::-1], am[:][:, ::-1], -BIG, ALU.add, ALU.max))
                    cy.carry(step, dve, fw[:, SL - 1:SL], bw[:, 0:1], -BIG, ALU.add, ALU.max)
                    step(tt(fw[:], fw[:], bw[:], ALU.max))
                    step(stt(out=fw[:], in0=pf[:], scalar=cy.back[:, 0:1], in1=fw[:], op0=ALU.add, op1=ALU.max))
                    step(stt(out=fw[:], in0=sf[:], scalar=cy.back[:, 1:2], in1=fw[:], op0=ALU.add, op1=ALU.max))
                    step(tsc(mk[:], rel[:], float(r), None, ALU.is_equal))
                    step(nc.vector.copy_predicated(sel[:], mk[:].bitcast(I16), fw[:]))
                tt(att[:], att[:], sel[:], ALU.subtract).then_inc(s_e, 1)
                step(tsc(fi[:], fi[:], 0.0, None, ALU.is_equal))
                step(tsc(la[:], la[:], 0.0, None, ALU.is_equal))
                step(tsc(pf[:], pf[:], 0.0, None, ALU.is_equal))
                step(tsc(sf[:], sf[:], 0.0, None, ALU.is_equal))
                cy.to_row(step, dve, pf[:, SL - 1:SL], sf[:, 0:1], cy.flag)
                step(nc.vector.memset(sel[:], 1.0))
                dve.wait_ge(s_x, 1)
                for r in range(R):
                    step(tsc(mk[:], rel[:], float(r), None, ALU.is_equal))
                    step(tt(am[:], att[:], mk[:], ALU.mult))
                    step(scan(fw[:], fi[:], am[:], 0.0, ALU.mult, ALU.add))
                    step(scan(bw[:][:, ::-1], la[:][:, ::-1], am[:][:, ::-1], 0.0, ALU.mult, ALU.add))
                    cy.carry(step, dve, fw[:, SL - 1:SL], bw[:, 0:1], 0.0, ALU.mult, ALU.add)
                    step(tt(bw[:], bw[:], am[:], ALU.subtract))
                    step(tt(fw[:], fw[:], bw[:], ALU.add))
                    step(stt(out=fw[:], in0=pf[:], scalar=cy.back[:, 0:1], in1=fw[:], op0=ALU.mult, op1=ALU.add))
                    step(stt(out=fw[:], in0=sf[:], scalar=cy.back[:, 1:2], in1=fw[:], op0=ALU.mult, op1=ALU.add))
                    step(nc.vector.copy_predicated(sel[:], mk[:].bitcast(I16), fw[:]))
                step(nc.vector.reciprocal(sel[:], sel[:]))
                tt(att[:], att[:], sel[:], ALU.mult).then_inc(s_w, 1)


def softmax_weights(nc, c, dr):
    with Stage(nc) as tmp:
        def sb(name, shape, dt=F32):
            return tmp.enter_context(nc.sbuf_tensor(name, shape, dt))
        att, own, fw, bw = (sb(n, [P, SL]) for n in ("t_att", "t_own", "t_fw", "t_bw"))
        rel, fi, la, pf, sf = (sb(n, [P, SL], BF16) for n in ("t_rel", "t_fi", "t_la", "t_pf", "t_sf"))
        s_in, s_e, s_x, s_w, s_out, s_fl = (tmp.sem(n) for n in ("tm_in_", "tm_e", "tm_x", "tm_w", "tm_out", "tm_st"))
        cy = Carry(nc, c, tmp, "w")
        view = "h (g s) -> (h g) s"
        with nc.Block() as block:
            @block.sync
            def _(sp):
                sp.dma_start(att[:], dr["att"].rearrange(view, g=GR)).then_inc(s_in, 16)
                sp.dma_start(own[:], dr["self_"].rearrange(view, g=GR)).then_inc(s_in, 16)
                run_flags(nc, dr, sp, s_in, ((rel, "rel"), (fi, "first"), (la, "last")))
                sp.wait_ge(s_x, 1)
                sp.dma_start(dr["w1"][0:H].rearrange(view, g=GR), att[:]).then_inc(s_out, 16)
                sp.wait_ge(s_w, 1)
                sp.dma_start(dr["w1"][H:2 * H].rearrange(view, g=GR), own[:]).then_inc(s_out, 16)
                sp.wait_ge(s_out, 32)

            @block.scalar
            def _(act):
                act.wait_ge(s_e, 1)
                nc.scalar.activation(att[:], att[:], ACT.Exp).then_inc(s_x, 1)
                act.wait_ge(s_e, 2)
                nc.scalar.activation(own[:], own[:], ACT.Exp).then_inc(s_x, 1)

            @block.tensor
            def _(pe):
                cy.tensor(pe, [False, True])

            @block.vector
            def _(dve):
                step = Chain(dve, s_fl)
                tt, tsc, stt, scan = (nc.vector.tensor_tensor, nc.vector.tensor_scalar, nc.vector.scalar_tensor_tensor,
                                      nc.vector.tensor_tensor_scan)
                dve.wait_ge(s_in, 16 * (2 + 3 * H))
                step(stt(out=att[:], in0=att[:], scalar=SLOPE, in1=att[:], op0=ALU.mult, op1=ALU.max))
                step(tsc(rel[:], rel[:], 0.0, -BIG, ALU.is_lt, ALU.mult))
                step(tt(bw[:], att[:], own[:], ALU.max))
                step(tt(bw[:], bw[:], rel[:], ALU.add))
                step(tsc(la[:], la[:], -BIG, None, ALU.mult))
                step(tsc(rel[:], fi[:], 1.0, None, ALU.mult))
                step(tsc(fi[:], fi[:], -BIG, None, ALU.mult))
                step(scan(pf[:], fi[:], fi[:], 0.0, ALU.add, ALU.min))
                step(scan(sf[:][:, ::-1], la[:][:, ::-1], la[:][:, ::-1], 0.0, ALU.add, ALU.min))
                cy.to_row(step, dve, pf[:, SL - 1:SL], sf[:, 0:1], cy.flag)
                step(scan(fw[:], fi[:], bw[:], -BIG, ALU.add, ALU.max))
                step(scan(bw[:][:, ::-1], la[:][:, ::-1], bw[:][:, ::-1], -BIG, ALU.add, ALU.max))
                cy.carry(step, dve, fw[:, SL - 1:SL], bw[:, 0:1], -BIG, ALU.add, ALU.max)
                step(tt(fw[:], fw[:], bw[:], ALU.max))
                step(stt(out=fw[:], in0=pf[:], scalar=cy.back[:, 0:1], in1=fw[:], op0=ALU.add, op1=ALU.max))
                step(stt(out=fw[:], in0=sf[:], scalar=cy.back[:, 1:2], in1=fw[:], op0=ALU.add, op1=ALU.max))
                step(tt(att[:], att[:], fw[:], ALU.subtract))
                tsc(att[:], att[:], 0.0, None, ALU.min).then_inc(s_e, 1)
                step(tt(own[:], own[:], fw[:], ALU.subtract))
                tsc(own[:], own[:], 0.0, None, ALU.min).then_inc(s_e, 1)
                dve.wait_ge(s_x, 2)
                tt(own[:], own[:], rel[:], ALU.mult).then_inc(s_w, 1)


def sum_messages(nc, c, dr, v, layer, weights, nh, acc):
    L = layer
    width = D + nh
    V8 = SLOTS // 2
    with Stage(nc) as tmp:
        def sb(name, shape, dt=F32):
            return tmp.enter_context(nc.sbuf_tensor(f"{name}{L}", shape, dt))

        def sem(name):
            return tmp.sem(f"{name}{L}")
        win = sb("win", [CW, 2, nh, P])
        w = sb("wgt", [P, NC, nh])
        rows = sb("vrows", [P, SLOTS, D])
        wv = sb("wv", [P, SLOTS, width])
        hot = sb("vhot", [P, SLOTS, P])
        run = sb("run", [P, V8, MSG])
        psW = tmp.enter_context(nc.psum_tensor(f"psW{L}", [P, 2, 1024], F32))
        psM = tmp.enter_context(nc.psum_tensor(f"psM{L}", [P, 4, 512], F32))
        w_in = [sem("w_in0_"), sem("w_in1_")]
        loaded = [sem(f"loaded{g}_") for g in range(4)]
        wv_done = [sem("wv_even_"), sem("wv_odd_")]
        w_tr, w_out, ww_done, hot_done, m_done, run_done, kept = map(sem, (
            "w_tr", "w_out", "ww_done", "vhot_done", "m_done", "run_done", "sum_kept"))
        NG = SLOTS // GS

        def weigh(engine, ops, i, g):
            engine.wait_ge(loaded[g], 16 * (i + 1))
            engine.wait_ge(m_done, i * V8 + 2 * g + 2)
            ops.tensor_tensor(
                wv[:, g * GS:(g + 1) * GS, 0:D].rearrange("p k (h d) -> p k h d", h=H),
                rows[:, g * GS:(g + 1) * GS].rearrange("p k (h d) -> p k h d", h=H),
                w[:, ts(i * NG + g, GS), 0:H].unsqueeze(3).to_broadcast([P, GS, H, DK]), ALU.mult).then_inc(wv_done[g % 2], 1)

        with nc.Block() as block:
            @block.sync
            def _(sp):
                for t in range(CT):
                    if t >= 2:
                        sp.wait_ge(w_tr, t - 1)
                    sp.dma_start(win[:, t % 2], weights.rearrange("h (t c p) -> t c h p", t=CT, p=P)[t]).then_inc(w_in[t % 2], 16)
                with sp.Fori(0, NI) as i:
                    for g in range(NG):
                        sp.wait_ge(wv_done[g % 2], i * (NG // 2) + g // 2 + 1)
                        o = dr["val"].rearrange("(i k p) d -> i p k d", k=GS, p=P)[ds(i * NG + g, 1)]
                        sp.dma_start(rows[:, g * GS:(g + 1) * GS], o.rearrange("o p k d -> (o p) k d")).then_inc(loaded[g], 16)

            @block.scalar
            def _(act):
                act.sem_inc(kept, V8)
                act.wait_ge(w_out, CT)

                def beside(i, g):
                    act.wait_ge(m_done, i * V8 + 2 * g + 2)
                    nc.scalar.copy(wv[:, g * GS:(g + 1) * GS, D:width], w[:, ts(i * NG + g, GS)]).then_inc(ww_done, 1)

                def keep(i, visits):
                    for t in visits:
                        V = i * V8 + t
                        blk = act.value_load(v["blk"][0:1, ds(V, 1)], min_val=0, max_val=NB - 1)
                        act.wait_ge(run_done, V + 5)
                        act.wait_ge(kept, V + V8)
                        nc.scalar.copy(acc[:, ds(blk, 1)].rearrange("p o d -> p (o d)"), run[:, t]).then_inc(kept, 1)

                def turn(i, first=False):
                    for g in range(NG):
                        beside(i, g)
                        if g >= 2:
                            keep(i, (2 * g - 4, 2 * g - 3))
                        elif not first:
                            keep(i - 1, (2 * g + 4, 2 * g + 5))
                turn(0, True)
                with act.Fori(1, NI) as i:
                    turn(i)
                keep(NI - 1, range(4, V8))

            @block.gpsimd
            def _(pool):
                pool.sem_inc(wv_done[1], NG // 2)
                pool.wait_ge(w_out, CT)
                with pool.Fori(0, NI) as i:
                    for g in range(1, NG, 2):
                        weigh(pool, nc.gpsimd, i, g)

            @block.tensor
            def _(pe):
                pe.sem_inc(m_done, V8)
                for t in range(CT):
                    pe.wait_ge(w_in[t % 2], 16 * (t // 2 + 1))
                    if t >= 2:
                        pe.wait_ge(w_out, t - 1)
                    for h in range(nh):
                        ins = nc.tensor.transpose(psW[:, t % 2, h * P:h * P + CW], win[:, t % 2, h], c["ident"][0:CW, 0:CW])
                    ins.then_inc(w_tr, 1)
                with pe.Fori(0, NI) as i:
                    for t in range(V8):
                        if t % 2 == 0:
                            pe.wait_ge(hot_done, i * NG + t // 2 + 1)
                            pe.wait_ge(wv_done[t // 2 % 2], (i + 1) * (NG // 2) + t // 4 + 1)
                            pe.wait_ge(ww_done, i * NG + t // 2 + 1)
                        pe.wait_ge(run_done, i * V8 + t + 1)
                        for j in range(2):
                            ins = nc.tensor.matmul(psM[:, t % 4, 0:width], hot[:, 2 * t + j], wv[:, 2 * t + j], start=(j == 0), stop=(j == 1))
                        ins.then_inc(m_done, 1)

            @block.vector
            def _(dve):
                dve.sem_inc(wv_done[0], NG // 2)
                for t in range(CT):
                    dve.wait_ge(w_tr, t + 1)
                    nc.vector.tensor_copy(w[:, t * CW:(t + 1) * CW].rearrange("p c h -> p h c"),
                                          psW[:, t % 2].rearrange("p (h c) -> p h c", c=P)[:, 0:nh, 0:CW]).then_inc(w_out, 1)
                dve.sem_inc(run_done, 3)
                nc.vector.memset(run[:], 0.0).then_inc(run_done, 1)
                dve.wait_ge(w_out, CT)

                def add(i, t):
                    V = i * V8 + t
                    dve.wait_ge(m_done, V + 1 + V8)
                    dve.wait_ge(run_done, V + 4)
                    dve.wait_ge(kept, V + 1)
                    nc.vector.scalar_tensor_tensor(out=run[:, t, 0:width], in0=run[:, (t - 1) % V8, 0:width], scalar=v["same"][:, ds(V, 1)],
                                                   in1=psM[:, t % 4, 0:width], op0=ALU.mult, op1=ALU.add).then_inc(run_done, 1)
                def turn(i, first=False):
                    for g in range(NG):
                        if g % 2 == 0:
                            weigh(dve, nc.vector, i, g)
                        dve.wait_ge(m_done, i * V8 + 2 * g + 2)
                        nc.vector.tensor_tensor(hot[:, g * GS:(g + 1) * GS], c["iota"][:].unsqueeze(1).to_broadcast([P, GS, P]),
                                                v["dr"][:, ts(i * NG + g, GS)].unsqueeze(2).to_broadcast([P, GS, P]),
                                                ALU.is_equal).then_inc(hot_done, 1)
                        if g >= 2:
                            add(i, 2 * g - 4)
                            add(i, 2 * g - 3)
                        elif not first:
                            add(i - 1, 2 * g + 4)
                            add(i - 1, 2 * g + 5)
                turn(0, True)
                with dve.Fori(1, NI) as i:
                    turn(i)
                for t in range(V8 - 4, V8):
                    add(NI - 1, t)


def flat(ap):
    return ap.rearrange("p o d -> p (o d)")


def update_nodes(nc, c, dr, v, xs, acc, mv, scale, shift, a):
    with Stage(nc) as tmp:
        def sb(name, shape, dt=F32):
            return tmp.enter_context(nc.sbuf_tensor(name, shape, dt))

        def sem(name):
            return tmp.sem(name)
        wa = sb("wa", [P, 2, T, D])
        ba = sb("ba", [T, D])
        gate = sb("gate", [P, T])
        tmb = sb("utmb", [T, P])
        types_ = sb("utyperows", [T, NB, P])
        tsc_ = sb("utscale", [P, T, NB])
        inv = sb("uinv", [P, NB])
        al = sb("ual", [P, NB])
        om = sb("uom", [P, NB])
        tmpb = sb("utmp", [P, NB])
        hm = sb("uhm", [P, T, D])
        h = sb("uh", [P, D])
        hk = sb("uhk", [P, D])
        hT = sb("uhT", [P, T * 2, P])
        psT = tmp.enter_context(nc.psum_tensor("upsT", [P, 2, 512], F32))
        psO = tmp.enter_context(nc.psum_tensor("upsO", [P, 2, 512], F32))
        w_in, pre, hm_done, tr_done, hT_done, o_done, o_out, tm_in, h_done, hk_done, gt = map(sem, (
            "u_w_in", "u_pre", "u_hm", "u_tr", "u_hT", "u_o", "u_oo", "u_tm", "u_h", "u_hk", "u_gate"))
        with nc.Block() as block:
            @block.gpsimd
            def _(pool):
                pool.wait_ge(w_in, 16 * (T + 3))
                with pool.Fori(0, NB) as b:
                    pool.wait_ge(o_done, b + 1)
                    nc.gpsimd.tensor_copy(tmb[:], types_[:, ds(b, 1)].rearrange("t o p -> t (o p)")).then_inc(tm_in, 1)

            @block.sync
            def _(sp):
                sp.dma_start(types_[:], dr["typerow"].rearrange("t (b p) -> t b p", p=P)).then_inc(w_in, 16)
                for t in range(T):
                    sp.dma_start(wa[:, :, t], a['L0_gnn_Wa'][t].rearrange("(g p) d -> p g d", p=P)).then_inc(w_in, 16)
                sp.dma_start(ba[:], a['L0_gnn_ba']).then_inc(w_in, 16)
                sp.dma_start(gate[:], a['L0_gnn_skip'].rearrange("(o t) -> o t", o=1).to_broadcast([P, T])).then_inc(w_in, 16)

            @block.scalar
            def _(act):
                act.wait_ge(w_in, 16 * (T + 3))
                nc.scalar.activation(gate[:], gate[:], ACT.Exp, scale=-1.0).then_inc(gt, 1)
                act.wait_ge(pre, 1)
                with act.Fori(0, NB) as b:
                    act.wait_ge(tr_done, b + 1)
                    for t in range(T):
                        nc.scalar.activation(hm[:, t], flat(acc[:, ds(b, 1), 0:D]), ACT.Copy, scale=tsc_[:, t, ds(b, 1)]).then_inc(hm_done, 1)
                    act.wait_ge(hk_done, b + 1)
                    nc.scalar.activation(h[:], flat(xs[:, ds(b, 1)]), ACT.Relu, bias=shift[:, ds(b, 1)], scale=scale[:, ds(b, 1)]).then_inc(h_done, 1)

            @block.vector
            def _(dve):
                step = Chain(dve, sem("u_steps"))
                tt, tsc = nc.vector.tensor_tensor, nc.vector.tensor_scalar
                dve.sem_inc(hk_done, 1)
                dve.sem_inc(hT_done, 2)
                dve.sem_inc(o_out, 1)
                dve.wait_ge(gt, 1)
                step(tsc(gate[:], gate[:], 1.0, None, ALU.add))
                step(nc.vector.reciprocal(gate[:], gate[:]))
                step(nc.vector.memset(al[:], 0.0))
                for t in range(T):
                    step(tsc(tmpb[:], v["types"][:, :, t], gate[:, t:t + 1], None, ALU.mult))
                    step(tt(al[:], al[:], tmpb[:], ALU.add))
                step(tsc(om[:], al[:], -1.0, 1.0, ALU.mult, ALU.add))
                step(tsc(tmpb[:], acc[:, :, D], 1.0, None, ALU.max))
                step(nc.vector.reciprocal(inv[:], tmpb[:]))
                for t in range(T):
                    ins = tt(tsc_[:, t], inv[:], v["types"][:, :, t], ALU.mult)
                    if t < T - 1:
                        step(ins)
                ins.then_inc(pre, 1)
                with dve.Fori(0, NB) as b:
                    dve.wait_ge(tr_done, b + 2)
                    dve.wait_ge(o_done, b + 1)
                    nc.vector.tensor_copy(hT[:, 0:4].rearrange("p n q -> p (n q)"), psT[:, 0, :]).then_inc(hT_done, 1)
                    nc.vector.tensor_copy(hT[:, 4:6].rearrange("p n q -> p (n q)"), psT[:, 1, 0:2 * P]).then_inc(hT_done, 1)
                    dve.wait_ge(h_done, b + 1)
                    dve.wait_ge(o_out, b + 1)
                    tsc(hk[:], h[:], om[:, ds(b, 1)], None, ALU.mult).then_inc(hk_done, 1)
                    dve.wait_ge(hk_done, b + 2)
                    dve.wait_ge(o_done, b + 2)
                    nc.vector.scalar_tensor_tensor(out=flat(acc[:, ds(b, 1), 0:D]), in0=psO[:, 0, 0:D], scalar=al[:, ds(b, 1)], in1=hk[:],
                                                   op0=ALU.mult, op1=ALU.add).then_inc(o_out, 1)

            @block.tensor
            def _(pe):
                pe.sem_inc(tr_done, 1)
                pe.sem_inc(o_done, 1)
                pe.wait_ge(w_in, 16 * (T + 3))
                with pe.Fori(0, NB) as b:
                    pe.wait_ge(hm_done, 3 * (b + 1))
                    pe.wait_ge(hT_done, 2 * b + 2)
                    for n in range(6):
                        t, g = n // 2, n % 2
                        ins = nc.tensor.transpose(psT[:, n // 4, n % 4 * P:(n % 4 + 1) * P], hm[:, t, g * P:(g + 1) * P], c["ident"][:])
                    ins.then_inc(tr_done, 1)
                    pe.wait_ge(hT_done, 2 * b + 4)
                    pe.wait_ge(tm_in, b + 1)
                    pe.wait_ge(o_out, b + 1)
                    for t in range(T):
                        for g in range(2):
                            nc.tensor.matmul(psO[:, 0, 0:D], hT[:, 2 * t + g], wa[:, g, t], start=(t == 0 and g == 0), stop=False)
                    nc.tensor.matmul(psO[:, 0, 0:D], tmb[:], ba[:], start=False, stop=True).then_inc(o_done, 1)


def normalise_nodes(nc, c, dr, v, xs, acc, scale, shift, scale2, shift2, a):
    with Stage(nc) as tmp:
        def sb(name, shape, dt=F32):
            return tmp.enter_context(nc.sbuf_tensor(name, shape, dt))

        def sem(name):
            return tmp.sem(name)
        gb = sb("ngb", [T, 2 * D])
        types_ = sb("ntyperows", [T, NB, P])
        tmb = sb("ntmb", [T, P])
        has = sb("nhas", [P, NB])
        h = sb("nh", [P, D])
        z = sb("nz", [P, D])
        n_ = sb("nn", [P, D])
        y = sb("ny", [P, D])
        psG = tmp.enter_context(nc.psum_tensor("npsG", [P, 512], F32))
        w_in, tm_in, g_done, h_done, z_done, z_free, h_free, has_done, st, y_done, x_done = map(sem, (
            "n_w_in", "n_tm", "n_g", "n_h", "n_z", "n_zf", "n_hf", "n_has", "n_st", "n_y", "n_x"))
        with nc.Block() as block:
            @block.sync
            def _(sp):
                sp.dma_start(gb[:, 0:D], a['L0_gnn_ln_g']).then_inc(w_in, 16)
                sp.dma_start(gb[:, D:2 * D], a['L0_gnn_ln_b']).then_inc(w_in, 16)
                sp.dma_start(types_[:], dr["typerow"].rearrange("t (b p) -> t b p", p=P)).then_inc(w_in, 16)

            @block.gpsimd
            def _(pool):
                pool.sem_inc(x_done, 1)
                pool.wait_ge(w_in, 48)
                nc.gpsimd.tensor_copy(tmb[:], types_[:, 0]).then_inc(tm_in, 1)

                def one(b, more):
                    if more:
                        pool.wait_ge(g_done, b + 1)
                        nc.gpsimd.tensor_copy(tmb[:], types_[:, ds(b + 1, 1)].rearrange("t o p -> t (o p)")).then_inc(tm_in, 1)
                    pool.wait_ge(y_done, b + 1)
                    nc.gpsimd.tensor_tensor(flat(xs[:, ds(b, 1)]), flat(xs[:, ds(b, 1)]), y[:], ALU.add).then_inc(x_done, 1)
                with pool.Fori(0, NB - 1) as b:
                    one(b, True)
                one(NB - 1, False)

            @block.scalar
            def _(act):
                with act.Fori(0, NB) as b:
                    act.wait_ge(z_free, b + 1)
                    nc.scalar.activation(z[:], flat(acc[:, ds(b, 1), 0:D]), ACT.Identity, bias=shift2[:, ds(b, 1)], scale=scale2[:, ds(b, 1)]).then_inc(z_done, 1)
                    act.wait_ge(h_free, b + 1)
                    nc.scalar.activation(h[:], flat(xs[:, ds(b, 1)]), ACT.Relu, bias=shift[:, ds(b, 1)], scale=scale[:, ds(b, 1)]).then_inc(h_done, 1)

            @block.tensor
            def _(pe):
                pe.wait_ge(w_in, 48)
                with pe.Fori(0, NB) as b:
                    pe.wait_ge(tm_in, b + 1)
                    pe.wait_ge(has_done, b + 1)
                    nc.tensor.matmul(psG[:], tmb[:], gb[:], start=True, stop=True).then_inc(g_done, 1)

            @block.vector
            def _(dve):
                tt = nc.vector.tensor_tensor
                dve.sem_inc(z_free, 1)
                dve.sem_inc(h_free, 1)
                nc.vector.tensor_scalar(has[:], acc[:, :, D], 0.5, None, ALU.is_gt).then_inc(has_done, 1)
                dve.wait_ge(has_done, 1)
                with dve.Fori(0, NB) as b:
                    dve.wait_ge(z_done, b + 1)
                    dve.wait_ge(g_done, b + 1)
                    tt(n_[:], z[:], psG[:, 0:D], ALU.mult).then_inc(z_free, 1)
                    dve.wait_ge(z_free, b + 2)
                    tt(n_[:], n_[:], psG[:, D:2 * D], ALU.add).then_inc(has_done, 1)
                    dve.wait_ge(has_done, b + 2)
                    dve.wait_ge(h_done, b + 1)
                    tt(n_[:], n_[:], h[:], ALU.subtract).then_inc(st, 1)
                    dve.wait_ge(st, b + 1)
                    dve.wait_ge(x_done, b + 1)
                    nc.vector.scalar_tensor_tensor(out=y[:], in0=n_[:], scalar=has[:, ds(b, 1)], in1=h[:], op0=ALU.mult, op1=ALU.add).then_inc(y_done, 1)
                    dve.wait_ge(y_done, b + 1)
                    dve.sem_inc(h_free, 1)


def project_layer1(nc, c, dr, xs, node, scale, shift, a):
    with Stage(nc) as tmp:
        def sb(name, shape, dt=F32):
            return tmp.enter_context(nc.sbuf_tensor(name, shape, dt))

        def sem(name):
            return tmp.sem(name)
        w = sb("wlin", [P, 2, D + 2 * H])
        wT = sb("w1T", [P, 2, D])
        am = sb("attm", [P, 2, 2 * H])
        h = sb("ph", [P, D])
        hT = sb("phT", [P, 2, P])
        out = sb("pout", [P, D + 2 * H])
        psT = tmp.enter_context(nc.psum_tensor("ppsT", [P, 512], F32))
        psW = tmp.enter_context(nc.psum_tensor("ppsW", [P, 2, 512], F32))
        psO = tmp.enter_context(nc.psum_tensor("ppsO", [P, 512], F32))
        z, w_in, wt, wt_out, wa, wa_out, h_done, tr, hT_done, o_done, o_out, kept, x_done = map(sem, (
            "p_z", "p_w_in", "p_wt", "p_wto", "p_wa", "p_wao", "p_h", "p_tr", "p_hT", "p_o", "p_oo", "p_kept", "p_x"))
        e_done = sem("p_e")
        with nc.Block() as block:
            @block.sync
            def _(sp):
                sp.dma_start(w[:, :, 0:D], a['L1_gnn_W'].rearrange("(g p) d -> p g d", p=P)).then_inc(w_in, 16)
                sp.wait_ge(z, 1)
                for n, t in enumerate((a['L1_gnn_att_src'], a['L1_gnn_att_dst'])):
                    for hd in range(H):
                        u = hd % 2
                        sp.dma_start(am[u * DK:(u + 1) * DK, hd // 2, n * H + hd:n * H + hd + 1], t[hd].rearrange("(d o) -> d o", o=1)).then_inc(w_in, 16)
                sp.sem_inc(kept, 16)
                with sp.Fori(0, NB) as b:
                    sp.wait_ge(o_out, b + 2)
                    sp.dma_start(dr["x1t"][ts(b, P), :], out[:, 0:ROW1]).then_inc(kept, 16)
                sp.wait_ge(kept, 16 * (NB + 1))

            @block.gpsimd
            def _(pool):
                nc.gpsimd.memset(am[:], 0.0).then_inc(z, 1)
                with pool.Fori(0, NB) as b:
                    pool.wait_ge(h_done, b + 1)
                    nc.gpsimd.tensor_tensor(flat(xs[:, ds(b, 1)]), flat(xs[:, ds(b, 1)]), h[:], ALU.add).then_inc(x_done, 1)

            @block.scalar
            def _(act):
                with act.Fori(0, NB) as b:
                    act.wait_ge(tr, b + 1)
                    act.wait_ge(x_done, b)
                    nc.scalar.activation(h[:], flat(xs[:, ds(b, 1)]), ACT.Relu, bias=shift[:, ds(b, 1)], scale=scale[:, ds(b, 1)]).then_inc(h_done, 1)
                    act.wait_ge(tr, b + 2)
                    act.wait_ge(o_done, b + 1)
                    nc.scalar.copy(hT[:].rearrange("p n q -> p (n q)"), psT[:, 0:2 * P]).then_inc(hT_done, 1)

            @block.vector
            def _(dve):
                dve.sem_inc(o_out, 1)
                for g in range(2):
                    dve.wait_ge(wt, g + 1)
                    nc.vector.tensor_copy(wT[:, g], psW[:, g, 0:D]).then_inc(wt_out, 1)
                dve.wait_ge(wa, 1)
                nc.vector.tensor_copy(w[:, :, D:D + 2 * H], psT[:, 0:4 * H].rearrange("p (g n) -> p g n", g=2)).then_inc(wa_out, 1)
                with dve.Fori(0, NB) as b:
                    dve.wait_ge(o_done, b + 2)
                    dve.wait_ge(kept, 16 * (b + 1))
                    nc.vector.tensor_copy(node[:, ds(b, 1), 0:H].rearrange("p o h -> p (o h)"), psO[:, D + H:D + 2 * H]).then_inc(e_done, 1)
                    nc.vector.tensor_copy(node[:, ds(b, 1), H:2 * H].rearrange("p o h -> p (o h)"), psO[:, D:D + H]).then_inc(e_done, 1)
                    nc.vector.tensor_copy(out[:], psO[:, 0:D + 2 * H]).then_inc(o_out, 1)
                step = Chain(dve, sem("p_steps"))
                dve.wait_ge(e_done, 2 * NB)
                step(nc.vector.tensor_tensor(node[:, :, H:2 * H], node[:, :, 0:H], node[:, :, H:2 * H], ALU.add))
                step(nc.vector.scalar_tensor_tensor(out=node[:, :, H:2 * H], in0=node[:, :, H:2 * H], scalar=SLOPE, in1=node[:, :, H:2 * H],
                                                    op0=ALU.mult, op1=ALU.max))

            @block.tensor
            def _(pe):
                pe.wait_ge(w_in, 16 * 9)
                for g in range(2):
                    for u in range(2):
                        ins = nc.tensor.transpose(psW[:, g, u * P:(u + 1) * P], w[:, u, g * P:(g + 1) * P], c["ident"][:])
                    ins.then_inc(wt, 1)
                pe.wait_ge(wt_out, 2)
                for u in range(2):
                    for g in range(2):
                        ins = nc.tensor.matmul(psT[:, u * 2 * H:(u + 1) * 2 * H], wT[:, g, u * P:(u + 1) * P], am[:, g], start=(g == 0), stop=(g == 1))
                ins.then_inc(wa, 1)
                pe.sem_inc(tr, 1)
                pe.sem_inc(o_done, 1)
                pe.wait_ge(wa_out, 1)
                with pe.Fori(0, NB) as b:
                    pe.wait_ge(h_done, b + 1)
                    pe.wait_ge(hT_done, b)
                    for g in range(2):
                        ins = nc.tensor.transpose(psT[:, g * P:(g + 1) * P], h[:, g * P:(g + 1) * P], c["ident"][:])
                    ins.then_inc(tr, 1)
                    pe.wait_ge(hT_done, b + 1)
                    pe.wait_ge(o_out, b + 1)
                    for g in range(2):
                        ins = nc.tensor.matmul(psO[:, 0:D + 2 * H], hT[:, g], w[:, g], start=(g == 0), stop=(g == 1))
                    ins.then_inc(o_done, 1)


G7 = 7
NG7 = NB // G7


def finish(nc, c, dr, v, xs, acc, a, out):
    with Stage(nc) as tmp:
        def sb(name, shape, dt=F32):
            return tmp.enter_context(nc.sbuf_tensor(name, shape, dt))

        def sem(name):
            return tmp.sem(name)
        xw = sb("fxw", [P, G7, D])
        zero = sb("fzero", [P, NB, H])
        den = sb("fden", [P, NB, H])
        vec = sb("fvec", [P, 3, D])
        t1 = sb("ft1", [P, G7, D])
        mean = sb("fmean", [P, D])
        g_ = sb("fg", [P, D])
        sq = sb("fsq", [P, G7, D])
        pos = sb("fpos", [P, G7, D])
        neg = sb("fneg", [P, G7, D])
        psS = tmp.enter_context(nc.psum_tensor("psS", [P, 2, 512], F32))
        w_in, x_in, pre, f_done, s_done, m_done, d_done, q_done, v_done, y_done, e_done, o_done, st, st2, st3 = map(sem, (
            "f_w_in", "f_x_in", "f_pre", "f_done", "f_s", "f_m", "f_d", "f_q", "f_v", "f_y", "f_e", "f_o", "f_st", "f_st2", "f_st3"))
        saved = sem("f_saved")
        st4 = sem("f_st4")
        x_used = sem("f_x_used")
        with nc.Block() as block:
            @block.sync
            def _(sp):
                for n, t in enumerate((a['L1_gnn_bias'], a['L1_gnn_gamma'], a['L1_gnn_beta'])):
                    sp.dma_start(vec[:, n], t.rearrange("(o d) -> o d", o=1).to_broadcast([P, D])).then_inc(w_in, 16)
                with sp.Fori(0, NG7) as b:
                    sp.wait_ge(x_used, b + 1)
                    sp.dma_start(xw[:], dr["x1t"][ts(b, G7 * P), 0:D].rearrange("(k p) d -> p k d", p=P)).then_inc(x_in, 16)
                with sp.Fori(0, NG7 - 1) as b:
                    sp.wait_ge(o_done, b + 1)
                    sp.dma_start(out[ts(b, G7 * P), :].rearrange("(k p) d -> p k d", p=P), xs[:, ts(b, G7)]).then_inc(saved, 16)
                sp.wait_ge(o_done, NG7)
                sp.dma_start(out[(NB - G7) * P:(NB - 1) * P, :].rearrange("(k p) d -> p k d", p=P), xs[:, NB - G7:NB - 1]).then_inc(saved, 16)
                sp.dma_start(out[(NB - 1) * P:N, :], xs[0:NLAST, NB - 1]).then_inc(saved, 16)
                sp.wait_ge(saved, 16 * (NG7 + 1))

            @block.scalar
            def _(act):
                with act.Fori(0, NG7) as b:
                    act.wait_ge(d_done, b + 1)
                    act.wait_ge(v_done, b + 1)
                    nc.scalar.activation(sq[:], acc[:, ts(b, G7), 0:D], ACT.Square).then_inc(q_done, 1)
                act.wait_ge(st2, 1)
                nc.scalar.activation(g_[:], g_[:], ACT.Sqrt, bias=c["eps"][:, 0:1]).then_inc(st3, 1)
                with act.Fori(0, NG7) as b:
                    act.wait_ge(y_done, b + 1)
                    nc.scalar.activation(neg[:], neg[:], ACT.Exp).then_inc(e_done, 1)

            @block.tensor
            def _(pe):
                def column_sum(bank, source, ready, done, finished):
                    def group(b, first, last):
                        pe.wait_ge(ready, b + 1)
                        for k in range(G7):
                            end = last and k == G7 - 1
                            rows = NLAST if end else P
                            ins = nc.tensor.matmul(psS[:, bank, 0:D], c["ones"][0:rows], source(b, k, rows),
                                                   start=first and k == 0, stop=end, skip_group_check=True)
                        ins.then_inc(finished if last else done, 1)
                    group(0, True, False)
                    with pe.Fori(1, NG7 - 1) as b:
                        group(b, False, False)
                    group(NG7 - 1, False, True)
                pe.sem_inc(v_done, 1)
                column_sum(0, lambda b, k, n: acc[0:n, ds(b * G7 + k, 1), 0:D].rearrange("p o d -> p (o d)"), f_done, s_done, m_done)
                column_sum(1, lambda b, k, n: sq[0:n, k], q_done, v_done, m_done)

            @block.vector
            def _(dve):
                step = Chain(dve, st)
                tt, tsc, stt = nc.vector.tensor_tensor, nc.vector.tensor_scalar, nc.vector.scalar_tensor_tensor
                dve.sem_inc(x_used, 1)
                dve.wait_ge(w_in, 48)
                step(tt(den[:], acc[:, :, D:D + H], acc[:, :, D + H:MSG], ALU.add))
                step(tsc(zero[:], den[:], 0.5, None, ALU.is_lt))
                step(tt(acc[:, :, D + H:MSG], acc[:, :, D + H:MSG], zero[:], ALU.add))
                step(tt(den[:], den[:], zero[:], ALU.add))
                step(nc.vector.reciprocal(den[:], den[:]))
                step(tt(zero[:], acc[:, :, D + H:MSG], den[:], ALU.mult))

                def heads(ap):
                    return ap.rearrange("p k (h d) -> p k h d", h=H)

                def of_head(ap, b):
                    return ap[:, ts(b, G7)].unsqueeze(3).to_broadcast([P, G7, H, DK])

                def every(ap):
                    return ap.unsqueeze(1).to_broadcast([P, G7, D])
                with dve.Fori(0, NG7) as b:
                    def stp(ins, n):
                        ins.then_inc(pre, 1)
                        dve.wait_ge(pre, b * 3 + n)
                    rows = acc[:, ts(b, G7), 0:D]
                    dve.wait_ge(x_in, 16 * (b + 1))
                    stp(tt(heads(t1[:]), heads(xw[:]), of_head(zero, b), ALU.mult), 1)
                    dve.sem_inc(x_used, 1)
                    stp(tt(heads(rows), heads(rows), of_head(den, b), ALU.mult), 2)
                    stp(tt(rows, rows, t1[:], ALU.add), 3)
                    tt(rows, rows, every(vec[:, 0]), ALU.add).then_inc(f_done, 1)
                dve.wait_ge(m_done, 1)
                step(tsc(mean[:], psS[:, 0, 0:D], 1.0 / N, None, ALU.mult))
                dve.wait_ge(f_done, NG7)
                with dve.Fori(0, NG7) as b:
                    rows = acc[:, ts(b, G7), 0:D]
                    tt(rows, rows, every(mean[:]), ALU.subtract).then_inc(d_done, 1)
                dve.wait_ge(m_done, 2)
                tsc(g_[:], psS[:, 1, 0:D], 1.0 / N, None, ALU.mult).then_inc(st2, 1)
                dve.wait_ge(st3, 1)
                step(nc.vector.reciprocal(g_[:], g_[:]))
                step(tt(g_[:], g_[:], vec[:, 1], ALU.mult))
                dve.wait_ge(d_done, NG7)
                with dve.Fori(0, NG7) as b:
                    def stq(ins, n):
                        ins.then_inc(st4, 1)
                        dve.wait_ge(st4, b * 3 + n)
                    rows = acc[:, ts(b, G7), 0:D]
                    x_ = xs[:, ts(b, G7)]
                    stq(tt(rows, rows, every(g_[:]), ALU.mult), 1)
                    stq(tt(pos[:], rows, every(vec[:, 2]), ALU.add), 2)
                    tsc(neg[:], pos[:], 0.0, None, ALU.min).then_inc(y_done, 1)
                    stq(stt(out=pos[:], in0=pos[:], scalar=0.0, in1=x_, op0=ALU.max, op1=ALU.add), 3)
                    dve.wait_ge(e_done, b + 1)
                    stt(out=x_, in0=neg[:], scalar=-1.0, in1=pos[:], op0=ALU.add, op1=ALU.add).then_inc(o_done, 1)
                    dve.wait_ge(o_done, b + 1)


_INS = ['x', 'src', 'dst', 'edge_type_6', 'node_type_3', 'L0_gnn_Wk', 'L0_gnn_bk', 'L0_gnn_Wq', 'L0_gnn_bq',
        'L0_gnn_Wv', 'L0_gnn_bv', 'L0_gnn_Wa', 'L0_gnn_ba', 'L0_gnn_rel_pri', 'L0_gnn_rel_att', 'L0_gnn_rel_msg',
        'L0_gnn_skip', 'L0_gnn_ln_g', 'L0_gnn_ln_b', 'L1_gnn_W', 'L1_gnn_att_src', 'L1_gnn_att_dst', 'L1_gnn_bias',
        'L1_gnn_gamma', 'L1_gnn_beta']


def program(nc, out, a):
    with ExitStack() as ctx:
        def sb(name, shape, dt=F32):
            return ctx.enter_context(nc.sbuf_tensor(name, shape, dt))
        c = consts(nc, ctx)
        dr = scratch(nc)
        order_edges(nc, c, dr, a['src'], a['dst'], a['edge_type_6'])
        src, dst, etype = (dr[n].rearrange("e o -> (e o)") for n in ("src_o", "dst_o", "rel_o"))
        v = prepare_edges(nc, ctx, c, dr, src, dst, etype, a['node_type_3'])
        xs = sb("xs", [P, NB, D])
        mv = sb("mv", [P, NB, 2])
        scale = sb("scale", [P, NB])
        shift = sb("shift", [P, NB])
        clear = ctx.enter_context(nc.semaphore("clear"))
        with nc.Block() as block:
            @block.vector
            def _(dve):
                nc.vector.memset(xs[:, NB - 1], 0.0).then_inc(clear, 1)
                dve.wait_ge(clear, 1)
        node_stats(nc, c, "x", xs, mv, scale, shift, a['x'])
        with nc.sbuf_tensor("qs", [P, NB, D], F32) as qs:
            project(nc, c, dr, v, xs, qs, scale, shift, a)
            edge_scores(nc, c, dr, v, 0, dr["kv"], v["kvi"], qs, 2 * D)
        softmax_by_relation(nc, c, dr)
        scale2 = sb("scale2", [P, NB])
        shift2 = sb("shift2", [P, NB])
        with nc.sbuf_tensor("acc", [P, NB, MSG], F32) as acc:
            sum_messages(nc, c, dr, v, 0, dr["w0"], H, acc)
            update_nodes(nc, c, dr, v, xs, acc, mv, scale, shift, a)
            node_stats(nc, c, "out", acc, mv, scale2, shift2)
            normalise_nodes(nc, c, dr, v, xs, acc, scale, shift, scale2, shift2, a)
        node_stats(nc, c, "x1", xs, mv, scale, shift)
        node = sb("node", [P, NB, 2 * H])
        project_layer1(nc, c, dr, xs, node, scale, shift, a)
        edge_scores(nc, c, dr, v, 1, dr["x1t"], v["srci"], node, ROW1)
        softmax_weights(nc, c, dr)
        acc = sb("acc1", [P, NB, MSG])
        sum_messages(nc, c, dr, v, 1, dr["w1"], 2 * H, acc)
        finish(nc, c, dr, v, xs, acc, a, out)


def kernel(**inputs):
    import numpy as np
    import concourse.bacc as bacc
    from concourse.bass_utils import run_bass_kernel_spmd

    nc = bacc.Bacc("TRN2", target_bir_lowering=False, num_devices=1)
    arrays, args = {}, {}
    for name in _INS:
        a = np.ascontiguousarray(inputs[name])
        arrays[f"in_{name}"] = a
        args[name] = nc.dram_tensor(f"in_{name}", a.shape, mybir.dt.from_np(a.dtype), kind="ExternalInput").ap()
    out = nc.dram_tensor("out_0", (N, D), F32, kind="ExternalOutput").ap()
    program(nc, out, args)
    r = run_bass_kernel_spmd(nc, [arrays], core_ids=[0])
    return r.results[0]["out_0"]
```
